# Optimizing a Trainium2 kernel written in Bass

```python
import numpy as np
import jax
import jax.numpy as jnp

def _softmax(x, axis=-1):
    return jax.nn.softmax(x, axis=axis)

def _gelu(x):
    return jax.nn.gelu(x, approximate=True)

def _silu(x):
    return jax.nn.silu(x)

def _sigmoid(x):
    return jax.nn.sigmoid(x)

def _layernorm(x, axis=-1, eps=1e-05):
    m = jnp.mean(x, axis=axis, keepdims=True)
    v = jnp.var(x, axis=axis, keepdims=True)
    return (x - m) / jnp.sqrt(v + eps)

def _scatter_add(tgt, idx, src, axis=0):
    return tgt.at[idx].add(src)

def _segment_sum(src, seg, n):
    return jax.ops.segment_sum(src, seg, n)
kernel_name = 'mk_decoder_preln_d2_seqx_r4_70a530'

def setup_inputs(seed: int=0):
    np.random.seed(seed)
    _w = jnp.asarray

    def _rec_inputs():
        import jax
        import jax.numpy as jnp
        _rk = jax.random.key(seed)
        x = -0.0002928 + 1 * jax.random.normal(jax.random.fold_in(_rk, 1), (8, 256, 256), jnp.float32)
        _lenS = 256 - jax.random.randint(jax.random.fold_in(_rk, 7), (8,), 0, max(1, 256 // 4) + 1, jnp.int32)
        _lenS2 = 256 - jax.random.randint(jax.random.fold_in(_rk, 8), (8,), 0, max(1, 256 // 4) + 1, jnp.int32)
        _ctx_1024P = jax.random.normal(jax.random.fold_in(_rk, 11), (8, 16, 256), jnp.float32)
        _ctx_1024c = jax.random.dirichlet(jax.random.fold_in(_rk, 511), 0.3 * jnp.ones((16,), jnp.float32), (8, 256))
        _ctx_1024t = jnp.einsum('bsk,bkd->bsd', _ctx_1024c, _ctx_1024P)
        _ctx_1024t = _ctx_1024t * jax.lax.rsqrt(jnp.mean(jnp.square(_ctx_1024t)) + 1e-12) * 0.953939
        ctx_1024 = -1.39393e-06 + 0.999914 * (_ctx_1024t + 0.3 * jax.random.normal(jax.random.fold_in(_rk, 611), (8, 256, 256), jnp.float32))
        _validS = jnp.arange(256)[None, :] < _lenS[:, None]
        _validS2 = jnp.arange(256)[None, :] < _lenS2[:, None]
        _causal = jnp.tril(jnp.ones((256, 256), dtype=bool))
        mask_BxS2_ik0 = jnp.where(jnp.broadcast_to(_validS2[:, :], (8, 256)), 0, 1).astype(jnp.int32)
        return (x, ctx_1024, mask_BxS2_ik0)
    x, ctx_1024, mask_BxS2_ik0 = _rec_inputs()

    def _L0_attn_setup():
        import jax, jax.numpy as jnp
        import numpy as np
        HEADS = 16

        def _split_heads(t, h):
            b, y, hd = t.shape
            d = hd // h
            return t.reshape(b, y, h, d).transpose(0, 2, 1, 3).reshape(b * h, y, d)

        def _merge_heads(t, b, h):
            bh, y, d = t.shape
            return t.reshape(b, h, y, d).transpose(0, 2, 1, 3).reshape(b, y, h * d)
        key = jax.random.key(seed)
        ks = jax.random.split(key, 5)
        B, S, D = (8, 1024, 256)
        scale = 1.0 / np.sqrt(D)
        x = jax.random.normal(ks[0], (B, S, D), dtype=jnp.float32)
        Wq = jax.random.normal(ks[1], (D, D), dtype=jnp.float32) * scale
        Wk = jax.random.normal(ks[2], (D, D), dtype=jnp.float32) * scale
        Wv = jax.random.normal(ks[3], (D, D), dtype=jnp.float32) * scale
        Wo = jax.random.normal(ks[4], (D, D), dtype=jnp.float32) * scale
        return {'x': x, 'Wq': Wq, 'Wk': Wk, 'Wv': Wv, 'Wo': Wo}
    _L0_attn_all = _L0_attn_setup()
    _L0_attn_in = {k: v for k, v in _L0_attn_all.items() if k in ('Wq', 'Wk', 'Wv', 'Wo')}
    del _L0_attn_all

    def _L0_xattn_setup():
        import jax, jax.numpy as jnp
        import numpy as np
        import math
        EPS = 1e-08
        LN_EPS = 1e-05
        B, S, E, NH = (2, 512, 256, 4)
        DH = E // NH

        def _mlstm_cell(q, k, v, igate_w, igate_b, fgate_w, fgate_b, out_w):
            Bq, Sq, Eq = q.shape
            if_in = jnp.concatenate([q, k, v], axis=-1)
            ig = jnp.einsum('bsf,hf->bsh', if_in, igate_w) + igate_b
            fg = jnp.einsum('bsf,hf->bsh', if_in, fgate_w) + fgate_b
            ig = jnp.transpose(ig, (0, 2, 1))[..., None]
            fg = jnp.transpose(fg, (0, 2, 1))[..., None]
            qh = q.reshape(Bq, Sq, NH, DH).transpose(0, 2, 1, 3)
            kh = k.reshape(Bq, Sq, NH, DH).transpose(0, 2, 1, 3)
            vh = v.reshape(Bq, Sq, NH, DH).transpose(0, 2, 1, 3)
            log_fg = jax.nn.log_sigmoid(fg)
            cs = jnp.cumsum(log_fg, axis=2)
            cs_shift = jnp.concatenate([jnp.zeros_like(cs[:, :, :1]), cs[:, :, :-1]], axis=2)
            logfg_mat = cs - jnp.swapaxes(cs_shift, -2, -1)
            ltr = jnp.tril(jnp.ones((Sq, Sq), dtype=bool))
            logfg_mat = jnp.where(ltr, logfg_mat, -jnp.inf)
            log_D = logfg_mat + jnp.swapaxes(ig, -2, -1)
            max_log_D = jnp.max(log_D, axis=-1, keepdims=True)
            D = jnp.exp(log_D - max_log_D)
            qk = jnp.einsum('bhsd,bhtd->bhst', qh, kh / math.sqrt(DH))
            C = qk * D
            sum_C_abs = jnp.abs(jnp.sum(C, axis=-1, keepdims=True))
            normaliser = jnp.maximum(sum_C_abs, jnp.exp(-max_log_D))
            C_norm = C / (normaliser + EPS)
            h = jnp.einsum('bhst,bhtd->bhsd', C_norm, vh)
            mean = jnp.mean(h, axis=-1, keepdims=True)
            var = jnp.mean((h - mean) ** 2, axis=-1, keepdims=True)
            h_norm = (h - mean) / jnp.sqrt(var + LN_EPS)
            scale = (1.0 + out_w).reshape(1, NH, 1, DH)
            h_norm = h_norm * scale
            return h_norm.transpose(0, 2, 1, 3).reshape(Bq, Sq, Eq)
        key = jax.random.key(seed)
        ks = jax.random.split(key, 7)
        std_g = math.sqrt(2.0 / (5.0 * 3 * E))
        return {'q': jax.random.normal(ks[0], (B, S, E), dtype=jnp.float32), 'k': jax.random.normal(ks[1], (B, S, E), dtype=jnp.float32), 'v': jax.random.normal(ks[2], (B, S, E), dtype=jnp.float32), 'igate_w': jax.random.normal(ks[3], (NH, 3 * E), dtype=jnp.float32) * std_g, 'igate_b': jax.random.normal(ks[4], (NH,), dtype=jnp.float32) * 0.1, 'fgate_w': jax.random.normal(ks[5], (NH, 3 * E), dtype=jnp.float32) * std_g, 'fgate_b': jnp.linspace(3.4, 6.0, NH, dtype=jnp.float32), 'out_w': jnp.zeros((E,), dtype=jnp.float32)}
    _L0_xattn_all = _L0_xattn_setup()
    _L0_xattn_in = {k: v for k, v in _L0_xattn_all.items() if k in ('igate_w', 'igate_b', 'fgate_w', 'fgate_b', 'out_w')}
    del _L0_xattn_all

    def _L0_ffn_setup():
        import jax, jax.numpy as jnp
        import numpy as np
        HID = 256
        INTER = 1024
        RDIM = 128
        HEADS = 4
        NUM_EXPERTS = 4096
        NUM_KEYS = 128
        TOPK = 8
        B, T = (2, 512)
        key = jax.random.key(seed)
        ks = jax.random.split(key, 8)
        s = lambda fan_in: 1.0 / np.sqrt(fan_in)
        return {'hidden_states': jax.random.normal(ks[0], (B, T, HID), jnp.float32), 'Wq': jax.random.normal(ks[1], (HEADS * RDIM, HID), jnp.float32) * s(HID), 'keys': jax.random.normal(ks[2], (HEADS, NUM_KEYS, 2, RDIM // 2), jnp.float32) * s(RDIM // 2), 'down_embed': jax.random.normal(ks[3], (NUM_EXPERTS, HID), jnp.float32) * 0.02, 'up_embed': jax.random.normal(ks[4], (NUM_EXPERTS, HID), jnp.float32) * 0.02, 'Wg': jax.random.normal(ks[5], (INTER, HID), jnp.float32) * s(HID), 'Wu': jax.random.normal(ks[6], (INTER, HID), jnp.float32) * s(HID), 'Wd': jax.random.normal(ks[7], (HID, INTER), jnp.float32) * s(INTER)}
    _L0_ffn_all = _L0_ffn_setup()
    _L0_ffn_in = {k: v for k, v in _L0_ffn_all.items() if k in ('Wq', 'keys', 'down_embed', 'up_embed', 'Wg', 'Wu', 'Wd')}
    del _L0_ffn_all

    def _L1_attn_setup():
        import math
        import jax, jax.numpy as jnp
        import numpy as np
        B, T, C, H = (4, 512, 256, 256)
        key = jax.random.key(seed)
        kx, kk, kq, kv = jax.random.split(key, 4)
        s = 1.0 / math.sqrt(C)
        return {'x': jax.random.normal(kx, (B, T, C), dtype=jnp.float32), 'Wk': jax.random.uniform(kk, (C, H), dtype=jnp.float32, minval=-s, maxval=s), 'Wq': jax.random.uniform(kq, (C, H), dtype=jnp.float32, minval=-s, maxval=s), 'Wv': jax.random.uniform(kv, (C, H), dtype=jnp.float32, minval=-s, maxval=s)}
    _L1_attn_all = _L1_attn_setup()
    _L1_attn_in = {k: v for k, v in _L1_attn_all.items() if k in ('Wk', 'Wq', 'Wv')}
    del _L1_attn_all

    def _L1_xattn_setup():
        import jax, jax.numpy as jnp
        import numpy as np
        BLOCK = 16
        H = 16
        KV = 4
        HPG = H // KV
        DH = 64
        SCALE = 1.0 / np.sqrt(DH).astype(np.float32)
        key = jax.random.key(seed)
        ks = jax.random.split(key, 7)
        B, Ldec, Lenc, D = (2, 2048, 1024, 256)
        s = 1.0 / np.sqrt(D).astype(np.float32)
        return {'hidden_states': jax.random.normal(ks[0], (B, Ldec, D), jnp.float32), 'encoder_hidden_states': jax.random.normal(ks[1], (B, Lenc, D), jnp.float32), 'attention_mask': jax.random.randint(ks[2], (B, Lenc), 0, 2, jnp.int32), 'Wq': jax.random.normal(ks[3], (D, H * DH), jnp.float32) * s, 'Wk': jax.random.normal(ks[4], (D, KV * DH), jnp.float32) * s, 'Wv': jax.random.normal(ks[5], (D, KV * DH), jnp.float32) * s, 'Wo': jax.random.normal(ks[6], (H * DH, D), jnp.float32) * s}
    _L1_xattn_all = _L1_xattn_setup()
    _L1_xattn_in = {k: v for k, v in _L1_xattn_all.items() if k in ('Wq', 'Wk', 'Wv', 'Wo')}
    del _L1_xattn_all

    def _L1_ffn_setup():
        import jax, jax.numpy as jnp
        import numpy as np
        DIM = 256
        DEPTH = 6
        HEADS = 16
        DIM_HEAD = 64
        WINDOW = 64
        INNER = HEADS * DIM_HEAD
        DIM_INNER = int(DIM * 4 * 2 / 3)
        QK_SCALE = 8.0

        def shift_tokens(t):
            a, s = jnp.split(t, 2, -1)
            s = jnp.pad(s, ((0, 0), (1, 0), (0, 0)))[:, :-1]
            return jnp.concatenate([a, s], -1)

        def l2norm(t):
            return t / jnp.maximum(jnp.linalg.norm(t, axis=-1, keepdims=True), 1e-12)

        def rotate_half(x):
            x1, x2 = jnp.split(x, 2, -1)
            return jnp.concatenate([-x2, x1], -1)

        def rotary_tables(n):
            half = jnp.arange(0, DIM_HEAD, 2, dtype=jnp.float32)
            inv_freq = 1.0 / 10000.0 ** (half / DIM_HEAD)
            t = jnp.arange(n, dtype=jnp.float32)
            freqs = t[:, None] * inv_freq[None, :]
            freqs = jnp.concatenate([freqs, freqs], -1)
            base_scale = (half + 0.4 * DIM_HEAD) / (1.4 * DIM_HEAD)
            power = (t - n // 2) / (WINDOW // 2)
            scale = base_scale[None, :] ** power[:, None]
            scale = jnp.concatenate([scale, scale], -1)
            return (freqs, scale)

        def local_attention(q, k, v):
            b, h, n, d = q.shape
            w = WINDOW
            nw = n // w
            bq = q.reshape(b, h, nw, w, d)
            bk = k.reshape(b, h, nw, w, d)
            bv = v.reshape(b, h, nw, w, d)

            def look(t):
                p = jnp.pad(t, ((0, 0), (0, 0), (1, 0), (0, 0), (0, 0)))
                return jnp.concatenate([p[:, :, :nw], p[:, :, 1:]], axis=3)
            bk2, bv2 = (look(bk), look(bv))
            seq = jnp.arange(n).reshape(nw, w)
            seq_p = jnp.pad(seq, ((1, 0), (0, 0)), constant_values=-1)
            jt = jnp.concatenate([seq_p[:nw], seq_p[1:]], axis=1)
            it = seq[:, :, None]
            jb = jt[:, None, :]
            mask = (it < jb) | (it > jb + w) | (jb == -1)
            sim = jnp.einsum('bhwie,bhwje->bhwij', bq, bk2) * QK_SCALE
            sim = jnp.where(mask, -jnp.finfo(sim.dtype).max, sim)
            attn = jax.nn.softmax(sim, -1)
            out = jnp.einsum('bhwij,bhwje->bhwie', attn, bv2)
            return out.reshape(b, h, n, d)

        def attn_layer(x, Wqkv, qs, ksc, Wo):
            b, n, _ = x.shape
            qkv = x @ Wqkv
            q, k, v = jnp.split(qkv, 3, -1)
            sh = lambda t: t.reshape(b, n, HEADS, DIM_HEAD).transpose(0, 2, 1, 3)
            q, k, v = (sh(q), sh(k), sh(v))
            q = l2norm(q) * qs
            k = l2norm(k) * ksc
            freqs, scale = rotary_tables(n)
            cos, sin = (jnp.cos(freqs), jnp.sin(freqs))
            q = q * cos * scale + rotate_half(q) * sin * scale
            inv = 1.0 / scale
            k = k * cos * inv + rotate_half(k) * sin * inv
            out = local_attention(q, k, v)
            out = out.transpose(0, 2, 1, 3).reshape(b, n, INNER)
            return out @ Wo

        def ffn_layer(x, g, bln, W1, b1, W2, b2):
            mu = x.mean(-1, keepdims=True)
            var = ((x - mu) ** 2).mean(-1, keepdims=True)
            xn = (x - mu) / jnp.sqrt(var + 1e-05) * g + bln
            hg = xn @ W1 + b1
            a, gate = jnp.split(hg, 2, -1)
            return a * jax.nn.gelu(gate, approximate=False) @ W2 + b2
        key = jax.random.key(seed)
        ks = jax.random.split(key, 8)
        B, N = (2, 512)
        init = lambda k, shape: jax.random.normal(k, shape, jnp.float32) * 0.02
        return {'x': jax.random.normal(ks[0], (B, N, DIM), jnp.float32), 'Wqkv': init(ks[1], (DEPTH, DIM, 3 * INNER)), 'q_scale': jnp.ones((DEPTH, DIM_HEAD), jnp.float32), 'k_scale': jnp.ones((DEPTH, DIM_HEAD), jnp.float32), 'Wo': init(ks[2], (DEPTH, INNER, DIM)), 'ln_g': jnp.ones((DEPTH, DIM), jnp.float32), 'ln_b': jnp.zeros((DEPTH, DIM), jnp.float32), 'W1': init(ks[3], (DEPTH, DIM, 2 * DIM_INNER)), 'b1': jnp.zeros((DEPTH, 2 * DIM_INNER), jnp.float32), 'W2': init(ks[4], (DEPTH, DIM_INNER, DIM)), 'b2': jnp.zeros((DEPTH, DIM), jnp.float32)}
    _L1_ffn_all = _L1_ffn_setup()
    _L1_ffn_in = {k: v for k, v in _L1_ffn_all.items() if k in ('Wqkv', 'q_scale', 'k_scale', 'Wo', 'ln_g', 'ln_b', 'W1', 'b1', 'W2', 'b2')}
    del _L1_ffn_all
    return {'x': x, 'ctx_1024': ctx_1024, 'mask_BxS2_ik0': mask_BxS2_ik0, 'L0_attn_Wq': _L0_attn_in['Wq'], 'L0_attn_Wk': _L0_attn_in['Wk'], 'L0_attn_Wv': _L0_attn_in['Wv'], 'L0_attn_Wo': _L0_attn_in['Wo'], 'L0_xattn_igate_w': _L0_xattn_in['igate_w'], 'L0_xattn_igate_b': _L0_xattn_in['igate_b'], 'L0_xattn_fgate_w': _L0_xattn_in['fgate_w'], 'L0_xattn_fgate_b': _L0_xattn_in['fgate_b'], 'L0_xattn_out_w': _L0_xattn_in['out_w'], 'L0_ffn_Wq': _L0_ffn_in['Wq'], 'L0_ffn_keys': _L0_ffn_in['keys'], 'L0_ffn_down_embed': _L0_ffn_in['down_embed'], 'L0_ffn_up_embed': _L0_ffn_in['up_embed'], 'L0_ffn_Wg': _L0_ffn_in['Wg'], 'L0_ffn_Wu': _L0_ffn_in['Wu'], 'L0_ffn_Wd': _L0_ffn_in['Wd'], 'L1_attn_Wk': _L1_attn_in['Wk'], 'L1_attn_Wq': _L1_attn_in['Wq'], 'L1_attn_Wv': _L1_attn_in['Wv'], 'L1_xattn_Wq': _L1_xattn_in['Wq'], 'L1_xattn_Wk': _L1_xattn_in['Wk'], 'L1_xattn_Wv': _L1_xattn_in['Wv'], 'L1_xattn_Wo': _L1_xattn_in['Wo'], 'L1_ffn_Wqkv': _L1_ffn_in['Wqkv'], 'L1_ffn_q_scale': _L1_ffn_in['q_scale'], 'L1_ffn_k_scale': _L1_ffn_in['k_scale'], 'L1_ffn_Wo': _L1_ffn_in['Wo'], 'L1_ffn_ln_g': _L1_ffn_in['ln_g'], 'L1_ffn_ln_b': _L1_ffn_in['ln_b'], 'L1_ffn_W1': _L1_ffn_in['W1'], 'L1_ffn_b1': _L1_ffn_in['b1'], 'L1_ffn_W2': _L1_ffn_in['W2'], 'L1_ffn_b2': _L1_ffn_in['b2']}

def reference(x, ctx_1024, mask_BxS2_ik0, L0_attn_Wq, L0_attn_Wk, L0_attn_Wv, L0_attn_Wo, L0_xattn_igate_w, L0_xattn_igate_b, L0_xattn_fgate_w, L0_xattn_fgate_b, L0_xattn_out_w, L0_ffn_Wq, L0_ffn_keys, L0_ffn_down_embed, L0_ffn_up_embed, L0_ffn_Wg, L0_ffn_Wu, L0_ffn_Wd, L1_attn_Wk, L1_attn_Wq, L1_attn_Wv, L1_xattn_Wq, L1_xattn_Wk, L1_xattn_Wv, L1_xattn_Wo, L1_ffn_Wqkv, L1_ffn_q_scale, L1_ffn_k_scale, L1_ffn_Wo, L1_ffn_ln_g, L1_ffn_ln_b, L1_ffn_W1, L1_ffn_b1, L1_ffn_W2, L1_ffn_b2):
    import jax
    import jax.numpy as jnp

    def _L0_attn_ref(x, Wq, Wk, Wv, Wo):
        import jax, jax.numpy as jnp
        import numpy as np
        HEADS = 16

        def _split_heads(t, h):
            b, y, hd = t.shape
            d = hd // h
            return t.reshape(b, y, h, d).transpose(0, 2, 1, 3).reshape(b * h, y, d)

        def _merge_heads(t, b, h):
            bh, y, d = t.shape
            return t.reshape(b, h, y, d).transpose(0, 2, 1, 3).reshape(b, y, h * d)
        b = x.shape[0]
        h = HEADS
        q = _split_heads(x @ Wq.T, h)
        k = _split_heads(x @ Wk.T, h)
        v = _split_heads(x @ Wv.T, h)
        d = q.shape[-1]
        z = jnp.einsum('byq,byk->bkq', q, k) / jnp.sqrt(jnp.asarray(d, x.dtype))
        z = jax.nn.softmax(z, axis=-1)
        z = jnp.einsum('byz,bvy->bvz', z, v)
        z = _merge_heads(z, b, h)
        return z @ Wo.T

    def _L0_xattn_ref(q, k, v, igate_w, igate_b, fgate_w, fgate_b, out_w):
        import jax, jax.numpy as jnp
        import numpy as np
        import math
        EPS = 1e-08
        LN_EPS = 1e-05
        B, S, E, NH = (2, 512, 256, 4)
        DH = E // NH

        def _mlstm_cell(q, k, v, igate_w, igate_b, fgate_w, fgate_b, out_w):
            Bq, Sq, Eq = q.shape
            if_in = jnp.concatenate([q, k, v], axis=-1)
            ig = jnp.einsum('bsf,hf->bsh', if_in, igate_w) + igate_b
            fg = jnp.einsum('bsf,hf->bsh', if_in, fgate_w) + fgate_b
            ig = jnp.transpose(ig, (0, 2, 1))[..., None]
            fg = jnp.transpose(fg, (0, 2, 1))[..., None]
            qh = q.reshape(Bq, Sq, NH, DH).transpose(0, 2, 1, 3)
            kh = k.reshape(Bq, Sq, NH, DH).transpose(0, 2, 1, 3)
            vh = v.reshape(Bq, Sq, NH, DH).transpose(0, 2, 1, 3)
            log_fg = jax.nn.log_sigmoid(fg)
            cs = jnp.cumsum(log_fg, axis=2)
            cs_shift = jnp.concatenate([jnp.zeros_like(cs[:, :, :1]), cs[:, :, :-1]], axis=2)
            logfg_mat = cs - jnp.swapaxes(cs_shift, -2, -1)
            ltr = jnp.tril(jnp.ones((Sq, Sq), dtype=bool))
            logfg_mat = jnp.where(ltr, logfg_mat, -jnp.inf)
            log_D = logfg_mat + jnp.swapaxes(ig, -2, -1)
            max_log_D = jnp.max(log_D, axis=-1, keepdims=True)
            D = jnp.exp(log_D - max_log_D)
            qk = jnp.einsum('bhsd,bhtd->bhst', qh, kh / math.sqrt(DH))
            C = qk * D
            sum_C_abs = jnp.abs(jnp.sum(C, axis=-1, keepdims=True))
            normaliser = jnp.maximum(sum_C_abs, jnp.exp(-max_log_D))
            C_norm = C / (normaliser + EPS)
            h = jnp.einsum('bhst,bhtd->bhsd', C_norm, vh)
            mean = jnp.mean(h, axis=-1, keepdims=True)
            var = jnp.mean((h - mean) ** 2, axis=-1, keepdims=True)
            h_norm = (h - mean) / jnp.sqrt(var + LN_EPS)
            scale = (1.0 + out_w).reshape(1, NH, 1, DH)
            h_norm = h_norm * scale
            return h_norm.transpose(0, 2, 1, 3).reshape(Bq, Sq, Eq)
        return _mlstm_cell(q, k, v, igate_w, igate_b, fgate_w, fgate_b, out_w)

    def _L0_ffn_ref(hidden_states, Wq, keys, down_embed, up_embed, Wg, Wu, Wd):
        import jax, jax.numpy as jnp
        import numpy as np
        HID = 256
        INTER = 1024
        RDIM = 128
        HEADS = 4
        NUM_EXPERTS = 4096
        NUM_KEYS = 128
        TOPK = 8
        B, T = (2, 512)
        b, t, _ = hidden_states.shape
        q = hidden_states @ Wq.T
        q = q.reshape(b, t, 2, HEADS, RDIM // 2)
        q = jnp.transpose(q, (2, 0, 1, 3, 4))
        sim = jnp.einsum('pbthn,hkpn->pbthk', q, keys)
        sx, ix = jax.lax.top_k(sim[0], TOPK)
        sy, iy = jax.lax.top_k(sim[1], TOPK)
        all_scores = (sx[..., :, None] + sy[..., None, :]).reshape(b, t, HEADS, TOPK * TOPK)
        all_indices = (ix[..., :, None] * NUM_KEYS + iy[..., None, :]).reshape(b, t, HEADS, TOPK * TOPK)
        scores, pk = jax.lax.top_k(all_scores, TOPK)
        indices = jnp.take_along_axis(all_indices, pk, axis=-1)
        down = down_embed[indices]
        up = up_embed[indices]
        w = jnp.einsum('btd,bthkd->bthk', hidden_states, down)
        w = jax.nn.silu(w) * jax.nn.softmax(scores, axis=-1)
        experts_states = jnp.einsum('bthk,bthkd->btd', w, up)
        mlp = jax.nn.silu(hidden_states @ Wg.T) * (hidden_states @ Wu.T) @ Wd.T
        return mlp + experts_states

    def _L1_attn_ref(x, Wk, Wq, Wv):
        import math
        import jax, jax.numpy as jnp
        import numpy as np
        B, T, C, H = (4, 512, 256, 256)
        K = x @ Wk
        Q = x @ Wq
        V = x @ Wv
        scale = 1.0 / math.sqrt(K.shape[-1])
        wei = jnp.einsum('bth,bsh->bts', Q, K) * scale
        t = x.shape[1]
        causal = jnp.tril(jnp.ones((t, t), dtype=bool))
        wei = jnp.where(causal, wei, -jnp.inf)
        wei = jax.nn.softmax(wei, axis=-1)
        wei = jax.nn.relu(wei)
        return jnp.einsum('bts,bsh->bth', wei, V)

    def _L1_xattn_ref(hidden_states, encoder_hidden_states, attention_mask, Wq, Wk, Wv, Wo):
        import jax, jax.numpy as jnp
        import numpy as np
        BLOCK = 16
        H = 16
        KV = 4
        HPG = H // KV
        DH = 64
        SCALE = 1.0 / np.sqrt(DH).astype(np.float32)
        B, Ldec, D = hidden_states.shape
        Lenc = encoder_hidden_states.shape[1]
        pad = (BLOCK - Ldec % BLOCK) % BLOCK
        x = jnp.pad(hidden_states, ((0, 0), (0, pad), (0, 0))) if pad else hidden_states
        nb = (Ldec + pad) // BLOCK
        pooled = x.reshape(B, nb, BLOCK, D).mean(axis=2)
        q = (pooled @ Wq).reshape(B, nb, KV, HPG, DH)
        k = (encoder_hidden_states @ Wk).reshape(B, Lenc, KV, DH)
        v = (encoder_hidden_states @ Wv).reshape(B, Lenc, KV, DH)
        scores = jnp.einsum('bngqd,blgd->bgqnl', q, k) * SCALE
        mask = (attention_mask == 0)[:, None, None, None, :]
        scores = jnp.where(mask, jnp.float32(-1000000000.0), scores)
        attn = jax.nn.softmax(scores, axis=-1)
        out = jnp.einsum('bgqnl,blgd->bngqd', attn, v)
        out = out.reshape(B, nb, H * DH) @ Wo
        unpooled = jnp.broadcast_to(out[:, :, None, :], (B, nb, BLOCK, D)).reshape(B, nb * BLOCK, D)
        return unpooled[:, :Ldec, :]

    def _L1_ffn_ref(x, Wqkv, q_scale, k_scale, Wo, ln_g, ln_b, W1, b1, W2, b2):
        import jax, jax.numpy as jnp
        import numpy as np
        DIM = 256
        DEPTH = 6
        HEADS = 16
        DIM_HEAD = 64
        WINDOW = 64
        INNER = HEADS * DIM_HEAD
        DIM_INNER = int(DIM * 4 * 2 / 3)
        QK_SCALE = 8.0

        def shift_tokens(t):
            a, s = jnp.split(t, 2, -1)
            s = jnp.pad(s, ((0, 0), (1, 0), (0, 0)))[:, :-1]
            return jnp.concatenate([a, s], -1)

        def l2norm(t):
            return t / jnp.maximum(jnp.linalg.norm(t, axis=-1, keepdims=True), 1e-12)

        def rotate_half(x):
            x1, x2 = jnp.split(x, 2, -1)
            return jnp.concatenate([-x2, x1], -1)

        def rotary_tables(n):
            half = jnp.arange(0, DIM_HEAD, 2, dtype=jnp.float32)
            inv_freq = 1.0 / 10000.0 ** (half / DIM_HEAD)
            t = jnp.arange(n, dtype=jnp.float32)
            freqs = t[:, None] * inv_freq[None, :]
            freqs = jnp.concatenate([freqs, freqs], -1)
            base_scale = (half + 0.4 * DIM_HEAD) / (1.4 * DIM_HEAD)
            power = (t - n // 2) / (WINDOW // 2)
            scale = base_scale[None, :] ** power[:, None]
            scale = jnp.concatenate([scale, scale], -1)
            return (freqs, scale)

        def local_attention(q, k, v):
            b, h, n, d = q.shape
            w = WINDOW
            nw = n // w
            bq = q.reshape(b, h, nw, w, d)
            bk = k.reshape(b, h, nw, w, d)
            bv = v.reshape(b, h, nw, w, d)

            def look(t):
                p = jnp.pad(t, ((0, 0), (0, 0), (1, 0), (0, 0), (0, 0)))
                return jnp.concatenate([p[:, :, :nw], p[:, :, 1:]], axis=3)
            bk2, bv2 = (look(bk), look(bv))
            seq = jnp.arange(n).reshape(nw, w)
            seq_p = jnp.pad(seq, ((1, 0), (0, 0)), constant_values=-1)
            jt = jnp.concatenate([seq_p[:nw], seq_p[1:]], axis=1)
            it = seq[:, :, None]
            jb = jt[:, None, :]
            mask = (it < jb) | (it > jb + w) | (jb == -1)
            sim = jnp.einsum('bhwie,bhwje->bhwij', bq, bk2) * QK_SCALE
            sim = jnp.where(mask, -jnp.finfo(sim.dtype).max, sim)
            attn = jax.nn.softmax(sim, -1)
            out = jnp.einsum('bhwij,bhwje->bhwie', attn, bv2)
            return out.reshape(b, h, n, d)

        def attn_layer(x, Wqkv, qs, ksc, Wo):
            b, n, _ = x.shape
            qkv = x @ Wqkv
            q, k, v = jnp.split(qkv, 3, -1)
            sh = lambda t: t.reshape(b, n, HEADS, DIM_HEAD).transpose(0, 2, 1, 3)
            q, k, v = (sh(q), sh(k), sh(v))
            q = l2norm(q) * qs
            k = l2norm(k) * ksc
            freqs, scale = rotary_tables(n)
            cos, sin = (jnp.cos(freqs), jnp.sin(freqs))
            q = q * cos * scale + rotate_half(q) * sin * scale
            inv = 1.0 / scale
            k = k * cos * inv + rotate_half(k) * sin * inv
            out = local_attention(q, k, v)
            out = out.transpose(0, 2, 1, 3).reshape(b, n, INNER)
            return out @ Wo

        def ffn_layer(x, g, bln, W1, b1, W2, b2):
            mu = x.mean(-1, keepdims=True)
            var = ((x - mu) ** 2).mean(-1, keepdims=True)
            xn = (x - mu) / jnp.sqrt(var + 1e-05) * g + bln
            hg = xn @ W1 + b1
            a, gate = jnp.split(hg, 2, -1)
            return a * jax.nn.gelu(gate, approximate=False) @ W2 + b2
        for i in range(DEPTH):
            x = attn_layer(shift_tokens(x), Wqkv[i], q_scale[i], k_scale[i], Wo[i]) + x
            x = ffn_layer(shift_tokens(x), ln_g[i], ln_b[i], W1[i], b1[i], W2[i], b2[i]) + x
        return x
    x = x + _L0_attn_ref(_layernorm(x, axis=-1), L0_attn_Wq, L0_attn_Wk, L0_attn_Wv, L0_attn_Wo)
    x = x + _L0_xattn_ref(_layernorm(x, axis=-1), ctx_1024, ctx_1024, L0_xattn_igate_w, L0_xattn_igate_b, L0_xattn_fgate_w, L0_xattn_fgate_b, L0_xattn_out_w)
    x = x + _L0_ffn_ref(_layernorm(x, axis=-1), L0_ffn_Wq, L0_ffn_keys, L0_ffn_down_embed, L0_ffn_up_embed, L0_ffn_Wg, L0_ffn_Wu, L0_ffn_Wd)
    x = x + _L1_attn_ref(_layernorm(x, axis=-1), L1_attn_Wk, L1_attn_Wq, L1_attn_Wv)
    x = x + _L1_xattn_ref(_layernorm(x, axis=-1), ctx_1024, mask_BxS2_ik0, L1_xattn_Wq, L1_xattn_Wk, L1_xattn_Wv, L1_xattn_Wo)
    x = x + _L1_ffn_ref(_layernorm(x, axis=-1), L1_ffn_Wqkv, L1_ffn_q_scale, L1_ffn_k_scale, L1_ffn_Wo, L1_ffn_ln_g, L1_ffn_ln_b, L1_ffn_W1, L1_ffn_b1, L1_ffn_W2, L1_ffn_b2)
    return x

_drawn_inputs = setup_inputs


def setup_inputs(seed=0):
    import zlib

    import numpy as np

    out = dict(_drawn_inputs(seed))
    spreads = {'L0_xattn_out_w': (0.0, 0.1),
     'L1_ffn_q_scale': (1.0, 0.6),
     'L1_ffn_k_scale': (1.0, 0.6),
     'L1_ffn_ln_g': (1.0, 0.6),
     'L1_ffn_ln_b': (0.0, 0.8),
     'L1_ffn_b1': (0.0, 0.744),
     'L1_ffn_b2': (0.0, 0.1)}
    factors = {'L0_xattn_igate_b': 64.0,
     'L0_ffn_Wq': 8.0,
     'L0_ffn_keys': 8.0,
     'L0_ffn_down_embed': 8.0,
     'L0_ffn_up_embed': 8.0,
     'L1_attn_Wk': 3.741,
     'L1_attn_Wq': 3.787}
    for name, (base, spread) in spreads.items():
        noise = np.random.default_rng([zlib.crc32(name.encode()), seed]).standard_normal(out[name].shape)
        drawn = base * np.exp(spread * noise) if base else spread * noise
        out[name] = jnp.asarray(drawn.astype(out[name].dtype))
    for name, factor in factors.items():
        out[name] = (out[name] * factor).astype(out[name].dtype)
    return out
```

```python
import numpy as np
from contextlib import ExitStack
import concourse.bass as bass
from concourse import mybir

F32 = mybir.dt.float32
BF16 = mybir.dt.bfloat16
I32 = mybir.dt.int32
U32 = mybir.dt.uint32
ALU = mybir.AluOpType
ACT = mybir.ActivationFunctionType
AX = mybir.AxisListType.X

P = 128
BATCH, SEQ, D = 8, 256, 256
TILES = SEQ // P
KC = D // P
BIG = 1.0e30
DEPTH = 6


def wait(eng, sem, value):
    if isinstance(value, int) and value <= 0:
        return
    eng.wait_ge(sem, value)


def apart(eng, passed):
    eng.sem_inc(passed, 1)


def first_layers(nc, xall, ident, ident_bf, passed, dram):
    H4, DH = 4, 64
    NK, TOPK = 128, 8
    EXPERTS = dram["emb"].shape[0]
    GROUPS = TILES * H4
    RG = 2
    INTER = dram["c_wg"].shape[1]
    MC = INTER // P
    BLK, NB = 16, SEQ // 16
    SCALE = 1.0 / 8.0

    EVENTS_AB = ["a_hT", "a_q", "a_k", "a_v", "a_z", "a_o", "a_y", "b_cT", "b_hT", "b_g", "b_gt"] + [f"b_m{h}" for h in range(H4)] \
        + [f"b_qk{h}" for h in range(H4)] + ["b_h0", "b_h1"]
    EVENTS_C = ["c_hT", "c_q0", "c_q1"] + [f"c_s{i}" for i in range(4)] + [f"c_m{i}" for i in range(MC)] + ["c_y0", "c_y1"]
    EVENTS_DE = ["d_hT", "d_q", "d_k", "d_v", "d_s", "d_pT", "d_o"] + ["e_hT", "e_cT", "e_k", "e_v", "e_q", "e_s0", "e_s1", "e_pT", "e_o", "e_y", "e_u"]
    NAB, NC_, NDE = len(EVENTS_AB), len(EVENTS_C), len(EVENTS_DE)
    EV = NAB + NC_ + NDE
    BANKS = 8
    assert EV % BANKS == 0

    ctx = ExitStack()
    with ctx:
        def sb(name, shape, dt=F32):
            return ctx.enter_context(nc.sbuf_tensor("f_" + name, shape, dt))

        def sem(name):
            return ctx.enter_context(nc.semaphore("f_" + name))

        a_w = sb("a_w", [P, 4, KC, D])
        gate_w = sb("gate_w", [P, 3 * KC, 8])
        gate_b = sb("gate_b", [H4, 2])
        out_gain = sb("out_gain", [P, D])
        c_wq = sb("c_wq", [P, KC, 2 * H4 * DH])
        c_keys = sb("c_keys", [P, 2, 2, NK])
        c_wg, c_wu = sb("c_wg", [P, KC, INTER]), sb("c_wu", [P, KC, INTER])
        c_wd = sb("c_wd", [P, MC, D])
        d_w = sb("d_w", [P, 3, KC, D])
        e_wq = sb("e_wq", [P, KC, 16 * DH])
        e_wk, e_wv = sb("e_wk", [P, KC, D]), sb("e_wv", [P, KC, D])
        e_wo = sb("e_wo", [P, 8, D])
        block_mask = sb("block_mask", [P, KC, P])
        later = sb("later", [P, P], BF16)
        future = sb("future", [P, P], BF16)
        head_row = sb("head_row", [H4, H4, P])
        unpool = sb("unpool", [NB, SEQ])
        iota8 = sb("iota8", [P, TOPK])
        minus_half = sb("minus_half", [P, 8])
        zeros = sb("zeros", [H4, SEQ])
        h = sb("h", [P, TILES, D])
        hT = sb("hT", [P, KC, SEQ])
        bn, mv, var_eps, rstd = sb("bn", [P, TILES, 6]), sb("mv", [P, TILES, 2]), sb("var_eps", [P, TILES]), sb("rstd", [P, TILES])
        proj0, proj1, proj2 = (sb(f"proj{i}", [P, 2, 256]) for i in range(3))
        c_qT = sb("c_qT", [P, 2 * H4 * DH // P, SEQ])
        a_q, a_k, a_vT, a_oT = proj0, proj1, c_qT[:, 0:2, :], c_qT[:, 2:4, :]
        a_s, a_e, a_p = sb("a_s", [P, KC, P]), sb("a_e", [P, KC, P]), sb("a_p", [P, KC, P])
        a_top, a_neg, a_sum, a_inv = (sb(x, [P, KC]) for x in ("a_top", "a_neg", "a_sum", "a_inv"))
        ctx_tok = sb("ctx_tok", [P, TILES, D])
        ctx_one = sb("ctx_one", [P, TILES, H4, DH + 1])
        ctxT = sb("ctxT", [P, KC, SEQ])
        g_in, g_f, g_abs, g_exp, g_ln, g_log, g_cs, g_a, g_top, g_low, g_norm = (sb("g_" + x, [H4, SEQ]) for x in
            ("in", "f", "abs", "exp", "ln", "log", "cs", "a", "top", "low", "norm"))
        gT = sb("gT", [P, 2, TILES, H4])
        decay = sb("decay", [P, 2, 3 * P])
        mT = sb("mT", [P, MC, SEQ])
        b_c = mT[:, :, :].rearrange("p i q -> p (i q)")[:, 0:H4 * 3 * P].rearrange("p (h q) -> p h q", h=H4)
        b_norm, b_inv, b_mean, b_var, b_rstd = (sb(x, [P, TILES * H4]) for x in ("b_norm", "b_inv", "b_mean", "b_var", "b_rstd"))
        heads_buf = sb("heads_buf", [P, 2, TILES * H4, DH])
        b_u, b_sq = heads_buf[:, 0], heads_buf[:, 1]
        hc = sb("hc", [P, TILES, D])
        best = sb("best", [P, 2, GROUPS, TOPK])
        besti = sb("besti", [P, 2, GROUPS, TOPK], U32)
        bestf = sb("bestf", [P, 2, GROUPS, TOPK])
        pair_buf = sb("pair_buf", [P, 2, GROUPS * TOPK * TOPK])
        pair = pair_buf[:, 0, :].rearrange("p (g i j) -> p g i j", g=GROUPS, i=TOPK)
        pick = pair_buf[:, 1, :].rearrange("p (gk i) -> p gk i", i=TOPK)
        score = sb("score", [P, GROUPS, TOPK])
        pairi = sb("pairi", [P, GROUPS, TOPK], U32)
        pos = sb("pos", [P, 2, GROUPS * TOPK], U32)
        posf = sb("posf", [P, 2, GROUPS * TOPK])
        picked = sb("picked", [P, 2, GROUPS * TOPK])
        expertf = sb("expertf", [P, GROUPS * TOPK])
        expert = sb("expert", [P, GROUPS * TOPK], U32)
        sm_d, sm_e, weight = (sb(x, [P, GROUPS, TOPK]) for x in ("sm_d", "sm_e", "weight"))
        sm_sum, sm_inv = sb("sm_sum", [P, GROUPS]), sb("sm_inv", [P, GROUPS])
        rows = sb("rows", [P, RG, TOPK, 2 * D])
        dots, low, expd, sig, silu, coef = (sb(x, [P, 2, TOPK]) for x in ("dots", "low", "expd", "sig", "silu", "coef"))
        m_gate = sb("m_gate", [P, 2, SEQ])
        d_qT, d_kT, d_v = proj0, proj1, proj2
        d_p, d_pT = sb("d_p", [P, 3 * P]), sb("d_pT", [P, 3 * P])
        d_top, d_neg, d_sum, d_inv = (sb(x, [P, TILES]) for x in ("d_top", "d_neg", "d_sum", "d_inv"))
        ctx_e = sb("ctx_e", [P, TILES, D])
        ctxT_e = ctxT
        pooled = sb("pooled", [P, KC, NB])
        e_kT, e_v = proj0, proj1
        e_qT = sb("e_qT", [P, 2, 4 * NB])
        mask_i = sb("mask_i", [4 * NB, SEQ], I32)
        keep, shut = sb("keep", [4 * NB, SEQ]), sb("shut", [4 * NB, SEQ])
        e_s = pair_buf[0:4 * NB, :, :].rearrange("p a b -> p (a b)").rearrange("p (g n) -> p g n", g=H4)
        e_p = heads_buf[0:4 * NB, :, :, :].rearrange("p a h d -> p (a h d)").rearrange("p (g n) -> p g n", g=H4)
        e_top, e_neg, e_sum, e_inv = (sb(x, [4 * NB, H4]) for x in ("e_top", "e_neg", "e_sum", "e_inv"))
        e_pT = proj2[:, :, :].rearrange("p t (g n) -> p t g n", g=H4)
        e_o = sb("e_o", [P, 2 * 4 * NB])
        e_y = sb("e_y", [NB, D])

        bank = [ctx.enter_context(nc.psum_tensor(f"fp{i}", [P, 512], F32)) for i in range(BANKS)]

        loaded = {s: sem("loaded_" + s) for s in "abcde"}
        LOADS = {"a": 1, "b": 3, "c": 5, "d": 1, "e": 4}
        consts_set, set_step, gain_set = sem("consts_set"), sem("set_step"), sem("gain_set")
        ctx_loaded, ctx_e_loaded, mask_loaded = sem("ctx_loaded"), sem("ctx_e_loaded"), sem("mask_loaded")
        ps_full, ps_taken = sem("ps_full"), [sem(f"ps_taken{i}") for i in range(BANKS)]
        stats = {s: sem("stats_" + s) for s in "abcde"}
        rstds = {s: sem("rstds_" + s) for s in "abcde"}
        normed = {s: sem("normed_" + s) for s in "abcde"}
        a_masked, a_exped, a_probs = sem("a_masked"), sem("a_exped"), sem("a_probs")
        ctx_split = sem("ctx_split")
        gates_biased, gates_ln, gates_top, gates_norm = sem("gates_biased"), sem("gates_ln"), sem("gates_top"), sem("gates_norm")
        decayed, weighted = sem("decayed"), sem("weighted")
        b_centred, b_rooted, b_added = sem("b_centred"), sem("b_rooted"), sem("b_added")
        routed, sm_ready, sm_exped = sem("routed"), sem("sm_ready"), sem("sm_exped")
        gathered = [sem(f"gathered{i}") for i in range(RG)]
        rows_used = sem("rows_used")
        dotted, dots_exped = sem("dotted"), sem("dots_exped")
        m_silu = sem("m_silu")
        c_added = sem("c_added")
        d_topped, d_exped, d_added = sem("d_topped"), sem("d_exped"), sem("d_added")
        e_pooled, e_topped, e_exped, e_normed, e_added = sem("e_pooled"), sem("e_topped"), sem("e_exped"), sem("e_normed"), sem("e_added")
        act_b = sem("act_b")
        dve_ab, dve_c, dve_sum, dve_de = sem("dve_ab"), sem("dve_c"), sem("dve_sum"), sem("dve_de")

        class Slot:
            def __init__(self, name, n):
                if name in EVENTS_DE:
                    c = NAB + NC_ + EVENTS_DE.index(name)
                    if isinstance(n, int) and n == BATCH - 1:
                        c -= NAB + NC_
                    n = n + 1
                else:
                    c = (EVENTS_AB + EVENTS_C).index(name)
                    if isinstance(n, int) and n == 0:
                        c += NDE
                self.bank, self.taken = bank[c % BANKS], ps_taken[c % BANKS]
                self.before = n * (EV // BANKS) + c // BANKS
                self.after = self.before + 1
                self.full = n * EV + c + 1

        class Chain:
            def __init__(self, eng, semaphore, n, per):
                self.eng, self.sem, self.base, self.per, self.made = eng, semaphore, n * per, per, 0

            def link(self, instruction):
                instruction.then_inc(self.sem, 1)
                self.made += 1
                self.eng.wait_ge(self.sem, self.base + self.made)

            def close(self):
                assert self.made == self.per, (self.made, self.per)

        def flat(x):
            return x.rearrange("p a b -> p (a b)")

        POINTS = {"a0": [0], "a1": [1], "a2": [2], "a3": [3], "b0": [4], "b1": [5], "b2": [6], "b3": [7]}

        def program(ab, route, de, start, tail):
            def run(eng):
                start(eng)
                ab(eng, 0, None)
                route(eng, 0)
                with eng.Fori(1, BATCH) as n:
                    ab(eng, n, n - 1)
                    route(eng, n)
                    de(eng, n - 1)
                tail(eng, BATCH - 1)
                de(eng, BATCH - 1)
            return run

        block = ctx.enter_context(nc.Block())

        @block.sync
        def _(sp):
            def load(name, dst, src):
                sp.dma_start(dst, src).then_inc(loaded[name], 16)

            def load_ctx(n):
                wait(sp, ps_full, Slot("b_cT", n - 1).full if not isinstance(n, int) or n > 0 else 0)
                apart(sp, passed)
                wait(sp, ctx_split, n)
                sp.dma_start(ctx_tok[:, :, :], dram["ctx"][n].rearrange("(t p) d -> p t d", p=P)).then_inc(ctx_loaded, 16)

            def load_e(n):
                if not isinstance(n, int) or n > 0:
                    wait(sp, e_added, n)
                sp.dma_start(ctx_e[:, :, :], dram["ctx"][n].rearrange("(t p) d -> p t d", p=P)).then_inc(ctx_e_loaded, 16)
                sp.dma_start(mask_i[:, :], dram["mask"][n].rearrange("(a n) -> a n", a=1).broadcast_to([4 * NB, SEQ])).then_inc(mask_loaded, 16)

            load("a", a_w[:, :, :, :].rearrange("p w k n -> p (w k) n"), dram["a_w"].rearrange("w (k p) n -> p (w k) n", p=P))
            load_ctx(0)
            load("b", gate_w[:, :, :], dram["gate_w"].rearrange("(k p) n -> p k n", p=P))
            load("b", gate_b[:, :], dram["gate_b"])
            load("b", out_gain[:, :], dram["out_w"].rearrange("(a n) -> a n", a=1).broadcast_to([P, D]))
            load("c", c_wq[:, :, :], dram["c_wq"].rearrange("(k p) n -> p k n", p=P))
            load("c", c_keys[:, :, :, :].rearrange("p a b k -> p (a b k)"), dram["c_keys"])
            load("c", c_wg[:, :, :], dram["c_wg"].rearrange("(k p) n -> p k n", p=P))
            load("c", c_wu[:, :, :], dram["c_wu"].rearrange("(k p) n -> p k n", p=P))
            load("c", c_wd[:, :, :], dram["c_wd"].rearrange("(k p) n -> p k n", p=P))
            load("d", d_w[:, :, :, :].rearrange("p w k n -> p (w k) n"), dram["d_w"].rearrange("w (k p) n -> p (w k) n", p=P))
            load("e", e_wq[:, :, :], dram["e_wq"].rearrange("(k p) n -> p k n", p=P))
            load("e", e_wk[:, :, :], dram["e_wk"].rearrange("(k p) n -> p k n", p=P))
            load("e", e_wv[:, :, :], dram["e_wv"].rearrange("(k p) n -> p k n", p=P))
            load("e", e_wo[:, :, :], dram["e_wo"].rearrange("(c p) n -> p c n", p=P))
            load_e(0)
            load_ctx(1)
            with sp.Fori(1, BATCH - 1) as n:
                load_ctx(n + 1)
                load_e(n)
            load_e(BATCH - 1)

        @block.gpsimd
        def _(pool):
            made = [0]

            def select(view, pattern, base, mult, fill):
                pool.wait_ge(set_step, made[0])
                pool.affine_select(out=view, in_=view, pattern=pattern, base=base, channel_multiplier=mult,
                                   compare_op=ALU.is_ge, fill=fill).then_inc(set_step, 1)
                made[0] += 1

            def fill(view, value):
                pool.memset(view, value).then_inc(set_step, 1)
                made[0] += 1

            def start(pool):
                fill(block_mask[:, :, :], 0.0)
                blocks = block_mask[:, :, :].rearrange("p c (b j) -> p (c b) j", j=BLK).rearrange("p (c b) j -> p c b j", c=KC)
                select(blocks, [[0, KC], [-16, 8], [0, BLK]], 0, 1, -BIG)
                select(blocks, [[0, KC], [16, 8], [0, BLK]], 15, -1, -BIG)
                fill(later[:, :], 0.0)
                select(later[:, :], [[1, P]], 0, -1, BIG)
                fill(future[:, :], 0.0)
                select(future[:, :], [[-1, P]], 0, 1, -BIG)
                fill(head_row[:, :, :], 1.0)
                select(head_row[:, :, :], [[-1, H4], [0, P]], 0, 1, 0.0)
                select(head_row[:, :, :], [[1, H4], [0, P]], 0, -1, 0.0)
                fill(unpool[:, :], 1.0)
                select(unpool[:, :], [[1, SEQ]], 0, -BLK, 0.0)
                select(unpool[:, :], [[-1, SEQ]], BLK - 1, BLK, 0.0)
                pool.iota(iota8[:, :], pattern=[[1, TOPK]], base=0, channel_multiplier=0, allow_small_or_imprecise_dtypes=True).then_inc(set_step, 1)
                made[0] += 1
                fill(minus_half[:, :], -0.5)
                fill(zeros[:, :], 0.0)
                fill(ctx_one[:, :, :, :], 1.0)
                pool.wait_ge(set_step, made[0])
                pool.sem_inc(consts_set, 1)

            def rooted(pool, s, n):
                pool.wait_ge(stats[s], n + 1)
                pool.tensor_tensor(rstd[:, :], var_eps[:, :], minus_half[:, 0:TILES], ALU.pow).then_inc(rstds[s], 1)

            def gather(pool, n, g):
                if g >= RG:
                    pool.wait_ge(rows_used, GROUPS * n + g - RG + 1)
                else:
                    wait(pool, rows_used, GROUPS * n)
                apart(pool, passed)
                for k in range(TOPK):
                    pool.indirect_dma_start(rows[:, g % RG, k, :], None, dram["emb"],
                                            bass.IndirectOffsetOnAxis(ap=expert[:, g * TOPK + k:g * TOPK + k + 1], axis=0)).then_inc(gathered[g % RG], 16)

            def point(pool, where, m):
                if m is not None:
                    for g in POINTS[where]:
                        if g + RG < GROUPS:
                            gather(pool, m, g + RG)

            def ab(pool, n, m):
                rooted(pool, "a", n)
                for w in ("a0", "a1", "a2"):
                    point(pool, w, m)
                rooted(pool, "b", n)
                pool.wait_ge(ctx_loaded, 16 * (n + 1))
                wait(pool, b_centred, n)
                apart(pool, passed)
                pool.tensor_copy(ctx_one[:, :, :, 0:DH], ctx_tok[:, :, :].rearrange("p t (h d) -> p t h d", h=H4)).then_inc(ctx_split, 1)
                for w in ("a3", "b0", "b1", "b2", "b3"):
                    point(pool, w, m)
                pool.wait_ge(b_centred, n + 1)
                pool.tensor_tensor(b_rstd[:, :], b_var[:, :], minus_half[:, :], ALU.pow).then_inc(b_rooted, 1)

            def route(pool, n):
                rooted(pool, "c", n)
                pool.wait_ge(routed, n + 1)
                for g in range(RG):
                    gather(pool, n, g)

            def de(pool, n):
                rooted(pool, "d", n)
                rooted(pool, "e", n)

            def tail(pool, n):
                for w in POINTS:
                    point(pool, w, n)

            program(ab, route, de, start, tail)(pool)

        @block.tensor
        def _(pe):
            def turn(name, n, src):
                s = Slot(name, n)
                wait(pe, s.taken, s.before)
                for k in range(KC):
                    for t in range(TILES):
                        last = pe.transpose(s.bank[:, (k * TILES + t) * P:(k * TILES + t + 1) * P], src[:, t, k * P:(k + 1) * P], ident[:, :])
                last.then_inc(ps_full, 1)

            def by_token(name, n, xT, w, c=None):
                s = Slot(name, n)
                wait(pe, s.taken, s.before)
                for t in range(TILES):
                    for k in range(KC):
                        last = pe.matmul(s.bank[:, t * D:(t + 1) * D], xT[:, k, t * P:(t + 1) * P], w[:, k, 0:D], start=(k == 0), stop=(k == KC - 1))
                last.then_inc(ps_full, 1)

            def by_feature(name, n, xT, w, first=0):
                s = Slot(name, n)
                wait(pe, s.taken, s.before)
                for c in range(2):
                    for k in range(KC):
                        last = pe.matmul(s.bank[:, c * SEQ:(c + 1) * SEQ], w[:, k, (first + c) * P:(first + c + 1) * P], xT[:, k, :],
                                         start=(k == 0), stop=(k == KC - 1))
                last.then_inc(ps_full, 1)

            def copied(name, n):
                s = Slot(name, n)
                pe.wait_ge(s.taken, s.after)

            def ab(pe, n, m):
                pe.wait_ge(normed["a"], n + 1)
                turn("a_hT", n, h)
                copied("a_hT", n)
                pe.wait_ge(loaded["a"], 16 * LOADS["a"])
                by_token("a_q", n, hT, a_w[:, 0])
                by_token("a_k", n, hT, a_w[:, 1])
                by_feature("a_v", n, hT, a_w[:, 2])
                copied("a_q", n)
                copied("a_k", n)
                s = Slot("a_z", n)
                wait(pe, s.taken, s.before)
                for c in range(KC):
                    for t in range(TILES):
                        last = pe.matmul(s.bank[:, c * P:(c + 1) * P], a_k[:, t, c * P:(c + 1) * P], a_q[:, t, c * P:(c + 1) * P],
                                         start=(t == 0), stop=(t == TILES - 1))
                last.then_inc(ps_full, 1)
                copied("a_v", n)
                pe.wait_ge(a_probs, n + 1)
                s = Slot("a_o", n)
                wait(pe, s.taken, s.before)
                for c in range(KC):
                    last = pe.matmul(s.bank[:, c * SEQ:(c + 1) * SEQ], a_p[:, c, :], a_vT[:, c, :], start=True, stop=True)
                last.then_inc(ps_full, 1)
                copied("a_o", n)
                by_token("a_y", n, a_oT, a_w[:, 3])
                pe.wait_ge(ctx_loaded, 16 * (n + 1))
                turn("b_cT", n, ctx_tok)
                pe.wait_ge(normed["b"], n + 1)
                turn("b_hT", n, h)
                copied("b_cT", n)
                copied("b_hT", n)
                pe.wait_ge(loaded["b"], 16 * LOADS["b"])
                s = Slot("b_g", n)
                wait(pe, s.taken, s.before)
                for i in range(2):
                    for k in range(3 * KC):
                        src = hT if k < KC else ctxT
                        last = pe.matmul(s.bank[0:H4, i * SEQ:(i + 1) * SEQ], gate_w[:, k, i * H4:(i + 1) * H4], src[:, k % KC, :],
                                         start=(k == 0), stop=(k == 3 * KC - 1))
                last.then_inc(ps_full, 1)
                s = Slot("b_gt", n)
                wait(pe, s.taken, s.before)
                pe.wait_ge(gates_norm, n + 1)
                apart(pe, passed)
                for i, src in enumerate((g_a, g_norm)):
                    for t in range(TILES):
                        last = pe.transpose(s.bank[:, (i * TILES + t) * H4:(i * TILES + t + 1) * H4], src[:, t * P:(t + 1) * P], ident[0:H4, 0:H4])
                last.then_inc(ps_full, 1)
                for hd in range(H4):
                    s = Slot(f"b_m{hd}", n)
                    wait(pe, s.taken, s.before)
                    pe.matmul(s.bank[:, 0:SEQ], head_row[:, hd, :], g_top[:, :], start=True, stop=False)
                    pe.matmul(s.bank[:, SEQ:SEQ + P], head_row[:, hd, :], g_top[:, P:SEQ], start=False, stop=False)
                    pe.matmul(s.bank[:, 0:P], ident_bf[:, :], later[:, :], start=False, stop=False)
                    pe.matmul(s.bank[:, SEQ:SEQ + P], ident_bf[:, :], later[:, :], start=False, stop=True).then_inc(ps_full, 1)
                for hd in range(H4):
                    s = Slot(f"b_qk{hd}", n)
                    wait(pe, s.taken, s.before)
                    r = slice(DH * (hd % 2), DH * (hd % 2) + DH)
                    pe.matmul(s.bank[:, 0:SEQ], ctxT[r, hd // 2, 0:P], hT[r, hd // 2, :], start=True, stop=True)
                    pe.matmul(s.bank[:, SEQ:SEQ + P], ctxT[r, hd // 2, P:SEQ], hT[r, hd // 2, P:SEQ], start=True, stop=True).then_inc(ps_full, 1)
                pe.wait_ge(weighted, H4 * (n + 1))
                pe.wait_ge(ctx_split, n + 1)
                s = Slot("b_h0", n)
                wait(pe, s.taken, s.before)
                for hd in range(H4):
                    last = pe.matmul(s.bank[:, hd * (DH + 1):(hd + 1) * (DH + 1)], b_c[:, hd, 0:P], ctx_one[:, 0, hd, :], start=True, stop=True)
                last.then_inc(ps_full, 1)
                s = Slot("b_h1", n)
                wait(pe, s.taken, s.before)
                for hd in range(H4):
                    out = s.bank[:, hd * (DH + 1):(hd + 1) * (DH + 1)]
                    pe.matmul(out, b_c[:, hd, P:2 * P], ctx_one[:, 0, hd, :], start=True, stop=False)
                    last = pe.matmul(out, b_c[:, hd, 2 * P:3 * P], ctx_one[:, 1, hd, :], start=False, stop=True)
                last.then_inc(ps_full, 1)

            def route(pe, n):
                pe.wait_ge(normed["c"], n + 1)
                turn("c_hT", n, hc)
                copied("c_hT", n)
                pe.wait_ge(loaded["c"], 16 * LOADS["c"])
                by_feature("c_q0", n, hT, c_wq, 0)
                by_feature("c_q1", n, hT, c_wq, 2)
                copied("c_q0", n)
                copied("c_q1", n)
                for i in range(4):
                    t, par = i // 2, i % 2
                    s = Slot(f"c_s{i}", n)
                    wait(pe, s.taken, s.before)
                    r = slice(DH * par, DH * par + DH)
                    for j in range(4):
                        xy, pair_of = j // 2, j % 2
                        last = pe.matmul(s.bank[:, j * NK:(j + 1) * NK], c_qT[r, j, t * P:(t + 1) * P], c_keys[r, xy, pair_of, :], start=True, stop=True)
                    last.then_inc(ps_full, 1)
                for i in range(MC):
                    s = Slot(f"c_m{i}", n)
                    wait(pe, s.taken, s.before)
                    for j, w in enumerate((c_wg, c_wu)):
                        for k in range(KC):
                            last = pe.matmul(s.bank[:, j * SEQ:(j + 1) * SEQ], w[:, k, i * P:(i + 1) * P], hT[:, k, :], start=(k == 0), stop=(k == KC - 1))
                    last.then_inc(ps_full, 1)
                copied(f"c_m{MC - 2}", n)
                copied(f"c_m{MC - 1}", n)
                for t in range(TILES):
                    s = Slot(f"c_y{t}", n)
                    wait(pe, s.taken, s.before)
                    for i in range(MC):
                        last = pe.matmul(s.bank[:, 0:D], mT[:, i, t * P:(t + 1) * P], c_wd[:, i, :], start=(i == 0), stop=(i == MC - 1))
                    last.then_inc(ps_full, 1)

            def de(pe, n):
                pe.wait_ge(normed["d"], n + 1)
                turn("d_hT", n, h)
                copied("d_hT", n)
                pe.wait_ge(loaded["d"], 16 * LOADS["d"])
                by_feature("d_q", n, hT, d_w[:, 0])
                by_feature("d_k", n, hT, d_w[:, 1])
                by_token("d_v", n, hT, d_w[:, 2])
                copied("d_q", n)
                copied("d_k", n)
                s = Slot("d_s", n)
                wait(pe, s.taken, s.before)
                for k in range(KC):
                    pe.matmul(s.bank[:, 0:P], d_qT[:, k, 0:P], d_kT[:, k, 0:P], start=(k == 0), stop=False)
                for k in range(KC):
                    pe.matmul(s.bank[:, P:3 * P], d_qT[:, k, P:SEQ], d_kT[:, k, :], start=False, stop=False)
                pe.matmul(s.bank[:, 0:P], ident_bf[:, :], future[:, :], start=False, stop=False)
                pe.matmul(s.bank[:, 2 * P:3 * P], ident_bf[:, :], future[:, :], start=False, stop=True).then_inc(ps_full, 1)
                s = Slot("d_pT", n)
                wait(pe, s.taken, s.before)
                pe.wait_ge(d_exped, n + 1)
                for m in range(3):
                    last = pe.transpose(s.bank[:, m * P:(m + 1) * P], d_p[:, m * P:(m + 1) * P], ident[:, :])
                last.then_inc(ps_full, 1)
                copied("d_v", n)
                copied("d_pT", n)
                s = Slot("d_o", n)
                wait(pe, s.taken, s.before)
                pe.matmul(s.bank[:, 0:D], d_pT[:, 0:P], d_v[:, 0, :], start=True, stop=True)
                pe.matmul(s.bank[:, D:2 * D], d_pT[:, P:2 * P], d_v[:, 0, :], start=True, stop=False)
                pe.matmul(s.bank[:, D:2 * D], d_pT[:, 2 * P:3 * P], d_v[:, 1, :], start=False, stop=True).then_inc(ps_full, 1)
                pe.wait_ge(normed["e"], n + 1)
                turn("e_hT", n, h)
                pe.wait_ge(ctx_e_loaded, 16 * (n + 1))
                turn("e_cT", n, ctx_e)
                copied("e_cT", n)
                pe.wait_ge(loaded["e"], 16 * LOADS["e"])
                by_feature("e_k", n, ctxT_e, e_wk)
                by_token("e_v", n, ctxT_e, e_wv)
                pe.wait_ge(e_pooled, n + 1)
                s = Slot("e_q", n)
                wait(pe, s.taken, s.before)
                for c in range(8):
                    for k in range(KC):
                        last = pe.matmul(s.bank[:, c * NB:(c + 1) * NB], e_wq[:, k, c * P:(c + 1) * P], pooled[:, k, :], start=(k == 0), stop=(k == KC - 1))
                last.then_inc(ps_full, 1)
                copied("e_q", n)
                copied("e_k", n)
                for i in range(2):
                    s = Slot(f"e_s{i}", n)
                    wait(pe, s.taken, s.before)
                    apart(pe, passed)
                    r = slice(DH * i, DH * i + DH)
                    for half in range(2):
                        last = pe.matmul(s.bank[0:4 * NB, half * SEQ:(half + 1) * SEQ], e_qT[r, half, :], e_kT[r, half, :], start=True, stop=True)
                    last.then_inc(ps_full, 1)
                s = Slot("e_pT", n)
                wait(pe, s.taken, s.before)
                pe.wait_ge(e_normed, n + 1)
                apart(pe, passed)
                for t in range(TILES):
                    for g in range(H4):
                        last = pe.transpose(s.bank[:, (t * H4 + g) * 4 * NB:(t * H4 + g + 1) * 4 * NB], e_p[:, g, t * P:(t + 1) * P], ident[0:4 * NB, 0:4 * NB])
                last.then_inc(ps_full, 1)
                copied("e_v", n)
                copied("e_pT", n)
                s = Slot("e_o", n)
                wait(pe, s.taken, s.before)
                for j, g in enumerate((0, 2, 1, 3)):
                    for t in range(TILES):
                        last = pe.matmul(s.bank[DH * (g % 2):DH * (g % 2) + DH, (g // 2) * 4 * NB:(g // 2 + 1) * 4 * NB], e_v[:, t, g * DH:(g + 1) * DH], e_pT[:, t, j, :],
                                         start=(t == 0), stop=(t == TILES - 1))
                last.then_inc(ps_full, 1)
                copied("e_o", n)
                s = Slot("e_y", n)
                wait(pe, s.taken, s.before)
                for c in range(8):
                    last = pe.matmul(s.bank[0:NB, 0:D], e_o[:, c * NB:(c + 1) * NB], e_wo[:, c, :], start=(c == 0), stop=(c == 7))
                last.then_inc(ps_full, 1)
                copied("e_y", n)
                s = Slot("e_u", n)
                wait(pe, s.taken, s.before)
                for t in range(TILES):
                    last = pe.matmul(s.bank[:, t * D:(t + 1) * D], unpool[:, t * P:(t + 1) * P], e_y[:, :], start=True, stop=True)
                last.then_inc(ps_full, 1)

            def start(pe):
                for b in range(BANKS):
                    pe.sem_inc(ps_taken[b], len(range(b, NDE, BANKS)))
                pe.sem_inc(ps_full, NDE)
                pe.wait_ge(consts_set, 1)

            program(ab, route, de, start, lambda pe, n: None)(pe)

        @block.scalar
        def _(act):
            F = nc.scalar.activation

            def copy(name, n, dst, width=512, parts=P):
                s = Slot(name, n)
                act.wait_ge(ps_full, s.full)
                F(dst, s.bank[0:parts, 0:width], ACT.Copy).then_inc(s.taken, 1)

            def point(act, where, m):
                if m is not None:
                    for g in POINTS[where]:
                        act.wait_ge(dotted, GROUPS * m + g + 1)
                        F(expd[:, g % 2, :], low[:, g % 2, :], ACT.Exp, scale=-1.0).then_inc(dots_exped, 1)

            def ab(act, n, m):
                copy("a_hT", n, flat(hT[:, :, :]))
                copy("a_q", n, flat(a_q[:, :, :]))
                copy("a_v", n, flat(a_vT[:, :, :]))
                point(act, "a0", m)
                act.wait_ge(a_masked, n + 1)
                for c in range(KC):
                    last = F(a_e[:, c, :], a_s[:, c, :], ACT.Exp, bias=a_neg[:, c:c + 1], accum_out=a_sum[:, c:c + 1])
                last.then_inc(a_exped, 1)
                point(act, "a1", m)
                copy("a_o", n, flat(a_oT[:, :, :]))
                point(act, "a2", m)
                point(act, "a3", m)
                copy("b_cT", n, flat(ctxT[:, :, :]))
                copy("b_hT", n, flat(hT[:, :, :]))
                point(act, "b0", m)
                act.wait_ge(gates_biased, n + 1)
                chain = Chain(act, act_b, n, 2)
                chain.link(F(g_abs[:, :], g_f[:, :], ACT.Abs))
                chain.link(F(g_exp[:, :], g_abs[:, :], ACT.Exp, scale=-1.0))
                chain.close()
                F(g_ln[:, :], g_exp[:, :], ACT.Ln, bias=1.0).then_inc(gates_ln, 1)
                point(act, "b1", m)
                act.wait_ge(gates_top, n + 1)
                F(g_norm[:, :], g_low[:, :], ACT.Exp, scale=-1.0).then_inc(gates_norm, 1)
                point(act, "b2", m)
                for hd in range(H4):
                    s = Slot(f"b_m{hd}", n)
                    act.wait_ge(ps_full, s.full)
                    if hd == 0:
                        st = Slot("b_gt", n)
                        act.wait_ge(st.taken, st.after)
                    if hd >= 2:
                        act.wait_ge(weighted, H4 * n + hd - 1)
                    F(decay[:, hd % 2, 0:SEQ], s.bank[:, 0:SEQ], ACT.Exp, scale=-1.0, bias=gT[:, 0, 0, hd:hd + 1])
                    F(decay[:, hd % 2, SEQ:SEQ + P], s.bank[:, SEQ:SEQ + P], ACT.Exp, scale=-1.0, bias=gT[:, 0, 1, hd:hd + 1]).then_inc(s.taken, 1)
                point(act, "b3", m)

            def route(act, n):
                copy("c_hT", n, flat(hT[:, :, :]))
                copy("c_q0", n, flat(c_qT[:, 0:2, :]))
                copy("c_q1", n, flat(c_qT[:, 2:4, :]))
                for i in range(MC):
                    s = Slot(f"c_m{i}", n)
                    act.wait_ge(ps_full, s.full)
                    if i >= 2:
                        before = Slot(f"c_m{i - 2}", n)
                        act.wait_ge(before.taken, before.after)
                    F(m_gate[:, i % 2, :], s.bank[:, 0:SEQ], ACT.Silu).then_inc(m_silu, 1)
                act.wait_ge(sm_ready, n + 1)
                F(sm_e[:, :, :], sm_d[:, :, :], ACT.Exp).then_inc(sm_exped, 1)

            def de(act, n):
                copy("d_hT", n, flat(hT[:, :, :]))
                copy("d_q", n, flat(d_qT[:, :, :]))
                copy("d_v", n, flat(d_v[:, :, :]))
                act.wait_ge(d_topped, n + 1)
                s = Slot("d_s", n)
                F(d_p[:, 0:P], s.bank[:, 0:P], ACT.Exp, bias=d_neg[:, 0:1], scale=1.0 / 16.0, accum_out=d_sum[:, 0:1])
                F(d_p[:, P:3 * P], s.bank[:, P:3 * P], ACT.Exp, bias=d_neg[:, 1:2], scale=1.0 / 16.0, accum_out=d_sum[:, 1:2]).then_inc(d_exped, 1)
                act.wait_ge(d_exped, n + 1)
                act.sem_inc(s.taken, 1)
                copy("d_pT", n, d_pT[:, :], 3 * P)
                copy("e_cT", n, flat(ctxT_e[:, :, :]))
                copy("e_k", n, flat(e_kT[:, :, :]))
                copy("e_v", n, flat(e_v[:, :, :]))
                copy("e_q", n, flat(e_qT[:, :, :]), 8 * NB)
                act.wait_ge(e_topped, n + 1)
                for g in range(H4):
                    last = F(e_p[:, g, :], e_s[:, g, :], ACT.Exp, bias=e_neg[:, g:g + 1], accum_out=e_sum[:, g:g + 1])
                last.then_inc(e_exped, 1)
                copy("e_pT", n, flat(proj2[:, :, :]))
                copy("e_o", n, e_o[:, :], 2 * 4 * NB)
                copy("e_y", n, e_y[:, :], D, NB)

            def tail(act, n):
                for w in POINTS:
                    point(act, w, n)

            def start(act):
                act.wait_ge(consts_set, 1)

            program(ab, route, de, start, tail)(act)

        @block.vector
        def _(dve):
            V = nc.vector

            def copy(name, n, dst, width=512, parts=P):
                s = Slot(name, n)
                dve.wait_ge(ps_full, s.full)
                V.tensor_copy(dst, s.bank[0:parts, 0:width]).then_inc(s.taken, 1)

            def norm(dve, s, n, dst, chain):
                apart(dve, passed)
                for t in range(TILES):
                    last = V.bn_stats(bn[:, t, :], xall[:, n, t, :])
                chain.link(last)
                apart(dve, passed)
                for t in range(TILES):
                    last = V.bn_aggr(mv[:, t, :], bn[:, t, :])
                chain.link(last)
                V.tensor_scalar(var_eps[:, :], mv[:, :, 1], 1e-5, None, ALU.add).then_inc(stats[s], 1)
                dve.wait_ge(rstds[s], n + 1)
                for t in range(TILES):
                    last = V.tensor_scalar(dst[:, t, :], xall[:, n, t, :], mv[:, t, 0:1], rstd[:, t:t + 1], ALU.subtract, ALU.mult)
                last.then_inc(normed[s], 1)

            def dot(n, g):
                chain = Chain(dve, dve_sum, GROUPS * n + g, 4 + TOPK)
                dve.wait_ge(gathered[g % RG], TOPK * 16 * (GROUPS // RG * n + g // RG + 1))
                for k in range(TOPK):
                    last = V.tensor_tensor_reduce(rows[:, g % RG, k, 0:D], hc[:, g // H4, :], rows[:, g % RG, k, 0:D], 1.0, 0.0, ALU.mult, ALU.add, dots[:, g % 2, k:k + 1])
                chain.link(last)
                V.tensor_scalar(low[:, g % 2, :], dots[:, g % 2, :], -80.0, None, ALU.max).then_inc(dotted, 1)
                return chain

            def add_up(n, g, chain):
                dve.wait_ge(dots_exped, GROUPS * n + g + 1)
                b = g % 2
                chain.link(V.tensor_scalar(sig[:, b, :], expd[:, b, :], 1.0, None, ALU.add))
                chain.link(V.reciprocal(silu[:, b, :], sig[:, b, :]))
                chain.link(V.tensor_tensor(sig[:, b, :], silu[:, b, :], dots[:, b, :], ALU.mult))
                chain.link(V.tensor_tensor(coef[:, b, :], sig[:, b, :], weight[:, g, :], ALU.mult))
                x = xall[:, n, g // H4, :]
                for k in range(TOPK):
                    add = V.scalar_tensor_tensor(x, rows[:, g % RG, k, D:2 * D], coef[:, b, k:k + 1], x, ALU.mult, ALU.add)
                    if k < TOPK - 1:
                        chain.link(add)
                add.then_inc(rows_used, 1)
                dve.wait_ge(rows_used, GROUPS * n + g + 1)
                chain.close()

            def point(where, m):
                if m is not None:
                    for g in POINTS[where]:
                        add_up(m, g, dot(m, g))

            def ab(dve, n, m):
                chain = Chain(dve, dve_ab, n, DVE_AB)
                norm(dve, "a", n, h, chain)
                point("a0", m)
                copy("a_k", n, flat(a_k[:, :, :]))
                s = Slot("a_z", n)
                dve.wait_ge(ps_full, s.full)
                V.scalar_tensor_tensor(flat(a_s[:, :, :]), s.bank[:, 0:SEQ], 0.25, flat(block_mask[:, :, :]), ALU.mult, ALU.add).then_inc(s.taken, 1)
                dve.wait_ge(s.taken, s.after)
                chain.link(V.tensor_reduce(a_top[:, :], a_s[:, :, :], AX, ALU.max))
                V.tensor_scalar(a_neg[:, :], a_top[:, :], -1.0, None, ALU.mult).then_inc(a_masked, 1)
                point("a1", m)
                dve.wait_ge(a_exped, n + 1)
                chain.link(V.reciprocal(a_inv[:, :], a_sum[:, :]))
                V.tensor_tensor(a_p[:, :, :], a_e[:, :, :], a_inv[:, :].rearrange("p (c a) -> p c a", a=1).broadcast_to([P, KC, P]), ALU.mult).then_inc(a_probs, 1)
                point("a2", m)
                s = Slot("a_y", n)
                dve.wait_ge(ps_full, s.full)
                x = xall[:, n, :, :]
                V.tensor_tensor(x, s.bank[:, :].rearrange("p (t d) -> p t d", t=TILES), x, ALU.add).then_inc(s.taken, 1)
                dve.wait_ge(s.taken, s.after)
                norm(dve, "b", n, h, chain)
                point("a3", m)
                s = Slot("b_g", n)
                dve.wait_ge(ps_full, s.full)
                V.tensor_scalar(g_in[:, :], s.bank[0:H4, 0:SEQ], gate_b[:, 0:1], None, ALU.add)
                V.tensor_scalar(g_f[:, :], s.bank[0:H4, SEQ:2 * SEQ], gate_b[:, 1:2], None, ALU.add).then_inc(gates_biased, 1)
                dve.wait_ge(gates_biased, n + 1)
                dve.sem_inc(s.taken, 1)
                point("b0", m)
                dve.wait_ge(gates_ln, n + 1)
                chain.link(V.scalar_tensor_tensor(g_log[:, :], g_f[:, :], 0.0, g_ln[:, :], ALU.min, ALU.subtract))
                chain.link(V.tensor_tensor_scan(g_cs[:, :], g_log[:, :], zeros[:, :], 0.0, ALU.add, ALU.add))
                V.tensor_copy(g_a[:, 0:1], g_in[:, 0:1])
                chain.link(V.tensor_tensor(g_a[:, 1:SEQ], g_in[:, 1:SEQ], g_cs[:, 0:SEQ - 1], ALU.subtract))
                chain.link(V.tensor_tensor_scan(g_top[:, :], g_a[:, :], zeros[:, :], -BIG, ALU.max, ALU.add))
                V.tensor_tensor(g_low[:, :], g_cs[:, :], g_top[:, :], ALU.add).then_inc(gates_top, 1)
                point("b1", m)
                copy("b_gt", n, gT[:, :, :, :].rearrange("p i t h -> p (i t h)"), 16)
                point("b2", m)
                for hd in range(H4):
                    s = Slot(f"b_qk{hd}", n)
                    dve.wait_ge(ps_full, s.full)
                    st = Slot(f"b_m{hd}", n)
                    dve.wait_ge(st.taken, st.after)
                    V.scalar_tensor_tensor(b_c[:, hd, :], s.bank[:, 0:3 * P], SCALE, decay[:, hd % 2, :], ALU.mult, ALU.mult).then_inc(weighted, 1)
                    dve.wait_ge(weighted, H4 * n + hd + 1)
                    dve.sem_inc(s.taken, 1)
                point("b3", m)
                inv, mean, var, rs = b_inv, b_mean, b_var, b_rstd
                for t in range(TILES):
                    s = Slot(f"b_h{t}", n)
                    dve.wait_ge(ps_full, s.full)
                    heads = s.bank[:, 0:H4 * (DH + 1)].rearrange("p (h d) -> p h d", h=H4)
                    th = slice(t * H4, (t + 1) * H4)
                    chain.link(V.tensor_scalar(b_norm[:, th], heads[:, :, DH], -1.0, None, ALU.mult))
                    chain.link(V.tensor_tensor(inv[:, th], b_norm[:, th], heads[:, :, DH], ALU.max))
                    chain.link(V.tensor_tensor(b_norm[:, th], inv[:, th], gT[:, 1, t, :], ALU.max))
                    chain.link(V.tensor_scalar(inv[:, th], b_norm[:, th], 1e-8, None, ALU.add))
                    chain.link(V.reciprocal(inv[:, th], inv[:, th]))
                    V.tensor_tensor(b_u[:, th, :], heads[:, :, 0:DH], inv[:, th].rearrange("p (h a) -> p h a", a=1).broadcast_to([P, H4, DH]), ALU.mult).then_inc(s.taken, 1)
                    dve.wait_ge(s.taken, s.after)

                def per_head(x):
                    return x[:, :].rearrange("p (h a) -> p h a", a=1).broadcast_to([P, TILES * H4, DH])

                chain.link(V.tensor_reduce(var[:, :], b_u[:, :, :], AX, ALU.add))
                chain.link(V.tensor_scalar(mean[:, :], var[:, :], 1.0 / DH, None, ALU.mult))
                chain.link(V.tensor_tensor(b_u[:, :, :], b_u[:, :, :], per_head(mean), ALU.subtract))
                chain.link(V.tensor_tensor(b_sq[:, :, :], b_u[:, :, :], b_u[:, :, :], ALU.mult))
                chain.link(V.tensor_reduce(mean[:, :], b_sq[:, :, :], AX, ALU.add))
                V.tensor_scalar(var[:, :], mean[:, :], 1.0 / DH, 1e-5, ALU.mult, ALU.add).then_inc(b_centred, 1)
                dve.wait_ge(b_rooted, n + 1)
                chain.link(V.tensor_tensor(b_u[:, :, :], b_u[:, :, :], per_head(rs), ALU.mult))
                chain.link(V.tensor_tensor(b_sq[:, :, :].rearrange("p (t h) d -> p t (h d)", t=TILES), b_u[:, :, :].rearrange("p (t h) d -> p t (h d)", t=TILES),
                                           out_gain[:, :].rearrange("p (a d) -> p a d", a=1).broadcast_to([P, TILES, D]), ALU.mult))
                chain.link(V.tensor_tensor(x, b_sq[:, :, :].rearrange("p (t h) d -> p t (h d)", t=TILES), x, ALU.add))
                chain.close()

            def route(dve, n):
                chain = Chain(dve, dve_c, n, DVE_C)
                norm(dve, "c", n, hc, chain)
                for i in range(4):
                    t, par = i // 2, i % 2
                    s = Slot(f"c_s{i}", n)
                    dve.wait_ge(ps_full, s.full)
                    apart(dve, passed)
                    for j in range(4):
                        last = V.max(best[:, j // 2, t * H4 + 2 * (j % 2) + par, :], s.bank[:, j * NK:(j + 1) * NK])
                    chain.link(last)
                    apart(dve, passed)
                    for j in range(4):
                        at = t * H4 + 2 * (j % 2) + par
                        last = V.max_index(besti[:, j // 2, at, :], best[:, j // 2, at, :], s.bank[:, j * NK:(j + 1) * NK])
                    last.then_inc(s.taken, 1)
                dve.wait_ge(s.taken, s.after)
                V.tensor_copy(bestf[:, :, :, :], besti[:, :, :, :])
                chain.link(V.tensor_tensor(pair[:, :, :, :], best[:, 0].rearrange("p g (i a) -> p g i a", a=1).broadcast_to([P, GROUPS, TOPK, TOPK]),
                                           best[:, 1].rearrange("p g (a j) -> p g a j", a=1).broadcast_to([P, GROUPS, TOPK, TOPK]), ALU.add))
                apart(dve, passed)
                for g in range(GROUPS):
                    last = V.max(score[:, g, :], pair[:, g, :, :].rearrange("p i j -> p (i j)"))
                chain.link(last)
                apart(dve, passed)
                for g in range(GROUPS):
                    last = V.max_index(pairi[:, g, :], score[:, g, :], pair[:, g, :, :].rearrange("p i j -> p (i j)"))
                chain.link(last)
                V.tensor_scalar(pos[:, 0, :], pairi[:, :, :].rearrange("p g k -> p (g k)"), 3, None, ALU.logical_shift_right)
                chain.link(V.tensor_scalar(pos[:, 1, :], pairi[:, :, :].rearrange("p g k -> p (g k)"), 7, None, ALU.bitwise_and))
                chain.link(V.tensor_copy(posf[:, :, :], pos[:, :, :]))
                for xy in range(2):
                    at = posf[:, xy, :].rearrange("p (k a) -> p k a", a=1).broadcast_to([P, GROUPS * TOPK, TOPK])
                    place = iota8[:, :].rearrange("p (a i) -> p a i", a=1).broadcast_to([P, GROUPS * TOPK, TOPK])
                    chain.link(V.tensor_tensor(pick[:, :, :], at, place, ALU.is_equal))
                    by_group = pick[:, :, :].rearrange("p (g k) i -> p g k i", g=GROUPS)
                    chain.link(V.tensor_tensor(by_group, by_group, bestf[:, xy].rearrange("p g (a i) -> p g a i", a=1).broadcast_to([P, GROUPS, TOPK, TOPK]), ALU.mult))
                    chain.link(V.tensor_reduce(picked[:, xy, :], pick[:, :, :], AX, ALU.add))
                chain.link(V.scalar_tensor_tensor(expertf[:, :], picked[:, 0, :], float(NK), picked[:, 1, :], ALU.mult, ALU.add))
                chain.link(V.tensor_scalar(expertf[:, :], expertf[:, :], float(EXPERTS - 1), None, ALU.min))
                V.tensor_copy(expert[:, :], expertf[:, :]).then_inc(routed, 1)
                V.tensor_tensor(sm_d[:, :, :], score[:, :, :], score[:, :, 0:1].broadcast_to([P, GROUPS, TOPK]), ALU.subtract).then_inc(sm_ready, 1)
                for i in range(MC):
                    s = Slot(f"c_m{i}", n)
                    dve.wait_ge(m_silu, MC * n + i + 1)
                    V.tensor_tensor(mT[:, i, :], s.bank[:, SEQ:2 * SEQ], m_gate[:, i % 2, :], ALU.mult).then_inc(s.taken, 1)
                dve.wait_ge(sm_exped, n + 1)
                chain.link(V.tensor_reduce(sm_sum[:, :], sm_e[:, :, :], AX, ALU.add))
                chain.link(V.reciprocal(sm_inv[:, :], sm_sum[:, :]))
                chain.link(V.tensor_tensor(weight[:, :, :], sm_e[:, :, :], sm_inv[:, :].rearrange("p (g a) -> p g a", a=1).broadcast_to([P, GROUPS, TOPK]), ALU.mult))
                for t in range(TILES):
                    s = Slot(f"c_y{t}", n)
                    dve.wait_ge(ps_full, s.full)
                    x = xall[:, n, t, :]
                    V.tensor_tensor(x, s.bank[:, 0:D], x, ALU.add).then_inc(s.taken, 1)
                    dve.wait_ge(s.taken, s.after)
                chain.close()

            def de(dve, n):
                chain = Chain(dve, dve_de, n, DVE_DE)
                norm(dve, "d", n, h, chain)
                copy("d_k", n, flat(d_kT[:, :, :]))
                s = Slot("d_s", n)
                dve.wait_ge(ps_full, s.full)
                V.tensor_reduce(d_top[:, 0:1], s.bank[:, 0:P], AX, ALU.max)
                chain.link(V.tensor_reduce(d_top[:, 1:2], s.bank[:, P:3 * P], AX, ALU.max))
                V.tensor_scalar(d_neg[:, :], d_top[:, :], -1.0 / 16.0, None, ALU.mult).then_inc(d_topped, 1)
                dve.wait_ge(d_exped, n + 1)
                chain.link(V.reciprocal(d_inv[:, :], d_sum[:, :]))
                s = Slot("d_o", n)
                dve.wait_ge(ps_full, s.full)
                for t in range(TILES):
                    x = xall[:, n, t, :]
                    last = V.scalar_tensor_tensor(x, s.bank[:, t * D:(t + 1) * D], d_inv[:, t:t + 1], x, ALU.mult, ALU.add)
                last.then_inc(s.taken, 1)
                dve.wait_ge(s.taken, s.after)
                norm(dve, "e", n, h, chain)
                s = Slot("e_hT", n)
                dve.wait_ge(ps_full, s.full)
                V.tensor_reduce(flat(pooled[:, :, :]), s.bank[:, :].rearrange("p (kb j) -> p kb j", j=BLK), AX, ALU.add).then_inc(e_pooled, 1)
                dve.wait_ge(e_pooled, n + 1)
                dve.sem_inc(s.taken, 1)
                dve.wait_ge(mask_loaded, 16 * (n + 1))
                chain.link(V.tensor_scalar(keep[:, :], mask_i[:, :], 0.0, None, ALU.not_equal))
                chain.link(V.tensor_scalar(shut[:, :], keep[:, :], 1.0, 1.0e9, ALU.subtract, ALU.mult))
                chain.link(V.tensor_scalar(keep[:, :], keep[:, :], SCALE / BLK, None, ALU.mult))

                def each(x, k):
                    return x[:, :].rearrange("p (a n) -> p a n", a=1).broadcast_to([4 * NB, k, SEQ])

                for i in range(2):
                    s = Slot(f"e_s{i}", n)
                    dve.wait_ge(ps_full, s.full)
                    V.tensor_tensor(e_s[:, 2 * i:2 * i + 2, :], s.bank[0:4 * NB, :].rearrange("p (g n) -> p g n", g=2), each(keep, 2), ALU.mult).then_inc(s.taken, 1)
                    dve.wait_ge(s.taken, s.after)
                chain.link(V.tensor_tensor(e_s[:, :, :], e_s[:, :, :], each(shut, H4), ALU.add))
                chain.link(V.tensor_reduce(e_top[:, :], e_s[:, :, :], AX, ALU.max))
                V.tensor_scalar(e_neg[:, :], e_top[:, :], -1.0, None, ALU.mult).then_inc(e_topped, 1)
                dve.wait_ge(e_exped, n + 1)
                chain.link(V.reciprocal(e_inv[:, :], e_sum[:, :]))
                V.tensor_tensor(e_p[:, :, :], e_p[:, :, :], e_inv[:, :].rearrange("p (g a) -> p g a", a=1).broadcast_to([4 * NB, H4, SEQ]), ALU.mult).then_inc(e_normed, 1)
                s = Slot("e_u", n)
                dve.wait_ge(ps_full, s.full)
                x = xall[:, n, :, :]
                V.tensor_tensor(x, s.bank[:, :].rearrange("p (t d) -> p t d", t=TILES), x, ALU.add).then_inc(e_added, 1)
                dve.wait_ge(e_added, n + 1)
                dve.sem_inc(s.taken, 1)
                chain.close()

            def start(dve):
                dve.wait_ge(consts_set, 1)
                dve.wait_ge(loaded["b"], 16 * LOADS["b"])
                V.tensor_scalar(out_gain[:, :], out_gain[:, :], 1.0, None, ALU.add).then_inc(gain_set, 1)
                dve.wait_ge(gain_set, 1)

            def tail(dve, n):
                for w in POINTS:
                    point(w, n)

            DVE_AB, DVE_C, DVE_DE = 28, 22, 12
            program(ab, route, de, start, tail)(dve)


def local_layers(nc, xall, ident, ident_bf, passed, dram, L, out_dram):
    H, DH = 16, 64
    INNER = H * DH
    HP = H // 2
    FF = dram["L1_ffn_W2"].shape[1]
    FC = (FF + P - 1) // P
    FR = FF - (FC - 1) * P
    STEPS = L * BATCH
    KW = 192

    TP_FRONT, TP_ATTN = 9, 20
    TP = TP_FRONT + TP_ATTN + 1
    PJ_FRONT, PJ_FFN = 12, FC
    PJ = PJ_FRONT + PJ_FFN
    assert TP % 2 == 0 and PJ % 2 == 0 and PJ_FFN % 2 == 0

    ctx = ExitStack()
    with ctx:
        def sb(name, shape, dt=F32):
            return ctx.enter_context(nc.sbuf_tensor("l_" + name, shape, dt))

        def sem(name):
            return ctx.enter_context(nc.semaphore("l_" + name))

        w_qkv = sb("w_qkv", [P, KC, 3 * INNER])
        w_o = sb("w_o", [P, INNER // P, D])
        w_1 = sb("w_1", [P, KC, 2 * FF])
        w_2 = sb("w_2", [P, FC, D])
        ff_cols = sb("ff_cols", [P, 2 * FC + 2 * KC])
        b1 = ff_cols[:, 0:2 * FC].rearrange("p (s c) -> p s c", s=2)
        ln_g, ln_b = ff_cols[:, 2 * FC:2 * FC + KC], ff_cols[:, 2 * FC + KC:]
        b2 = sb("b_2", [1, D])
        qk_gain = sb("qk_gain", [P, 2, 2, DH])
        rope_base = sb("rope_0", [P, 2, 2, TILES, DH])
        rope = sb("rope", [P, 2, 2, TILES, DH])
        band = sb("band", [P, 2 * KW], BF16)
        ones = sb("ones_row", [1, P])
        stream = sb("stream", [P, BATCH, TILES, D])
        ALLT = BATCH * TILES
        all_bn = sb("all_bn", [P, ALLT, 6])
        all_mv = sb("all_mv", [P, ALLT, 2])
        all_var = sb("all_var", [P, ALLT])
        all_half = sb("all_half", [P, ALLT])
        all_rstd = sb("all_rstd", [P, ALLT])
        xs = sb("xs", [P, TILES, D])
        xT = sb("xT", [P, KC, SEQ])
        qk_raw = sb("qk_raw", [P, 2, 512])
        qk_sq = sb("qk_sq", [P, 2, 512])
        qk_cos = sb("qk_cos", [P, 2, 512])
        qk_sin = sb("qk_sin", [P, 2, 512])
        qk_rot = sb("qk_rot", [P, 2, 512])
        ss = sb("ss", [P, 2, 8])
        ssm = sb("ssm", [P, 2, 8])
        r_q = sb("r_q", [P, TILES, H])
        r_k = sb("r_k", [P, 2, 8])
        minus_half = sb("minus_half", [P, 8])
        qT = sb("qT", [P, HP, SEQ])
        kT = sb("kT", [P, HP, SEQ])
        v = sb("v", [P, TILES, INNER])
        top = sb("top", [P, 2, TILES])
        neg_top = sb("neg_top", [P, 2, TILES])
        p_sum = sb("p_sum", [P, H, TILES])
        p_inv = sb("p_inv", [P, 4, TILES])
        probs = sb("probs", [P, 3, 3 * P])
        pT = sb("pT", [P, 2, 3, P])
        o_tok = sb("o_tok", [P, TILES, INNER])
        oT = sb("oT", [P, INNER // P, SEQ])
        xf = sb("xf", [P, TILES, D])
        xn = sb("xn", [P, TILES, D])
        xnT = sb("xnT", [P, KC, SEQ])
        bn = sb("bn", [P, TILES, 6])
        mv = sb("mv", [P, TILES, 2])
        var_eps = sb("var_eps", [P, TILES])
        rstd = sb("rstd", [P, TILES])
        gate = sb("gate", [P, 2, SEQ])
        hT = sb("hT", [P, FC, SEQ])

        tp = [ctx.enter_context(nc.psum_tensor(f"tp{i}", [P, 512], F32)) for i in range(2)]
        pj = [ctx.enter_context(nc.psum_tensor(f"pj{i}", [P, 512], F32)) for i in range(2)]
        sc = [ctx.enter_context(nc.psum_tensor(f"sc{i}", [P, 512], F32)) for i in range(2)]
        o_ps = ctx.enter_context(nc.psum_tensor("o_ps", [P, 512], F32))
        y_ps = ctx.enter_context(nc.psum_tensor("y_ps", [P, TILES, D], F32))

        const_loaded, consts_set = sem("const_loaded"), sem("consts_set")
        wqkv_loaded, wo_loaded, wf_loaded = sem("wqkv_loaded"), sem("wo_loaded"), sem("wf_loaded")
        xs_staged, xf_staged = sem("xs_staged"), sem("xf_staged")
        rope_ready = sem("rope_ready")
        tp_full, tp_taken = sem("tp_full"), [sem("tp_taken0"), sem("tp_taken1")]
        pj_full, pj_taken = sem("pj_full"), [sem("pj_taken0"), sem("pj_taken1")]
        qk_read = sem("qk_read")
        rotated = sem("rotated")
        sc_full, top_ready, exped = sem("sc_full"), sem("top_ready"), sem("exped")
        pT_used = sem("pT_used")
        o_taken = sem("o_taken")
        wo_done, w2_done = sem("wo_done"), sem("w2_done")
        res_a, res_f = sem("res_a"), sem("res_f")
        stats_ready, rstd_ready, xn_ready = sem("stats_ready"), sem("rstd_ready"), sem("xn_ready")
        gated = sem("gated")
        dve_attn, dve_ln, pool_front, pool_init = sem("dve_attn"), sem("dve_ln"), sem("pool_front"), sem("pool_init")
        entry_stats, entry_rstd, entry_done, dve_entry = sem("entry_stats"), sem("entry_rstd"), sem("entry_done"), sem("dve_entry")
        summed = sem("summed")
        stored = sem("stored")

        def tp_slot(kind, n, c=0):
            c += {"front": 0, "attn": TP_FRONT + 1, "ffn": TP_FRONT + TP}[kind]
            if isinstance(n, int):
                c += (kind == "front" and n == 0) - TP_FRONT * (kind == "ffn" and n == STEPS - 1)
            return c % 2, n * (TP // 2) + c // 2, n * TP + c + 1

        def pj_slot(kind, n, c):
            c += {"front": 0, "ffn": PJ_FRONT + PJ}[kind]
            if isinstance(n, int):
                c += PJ_FFN * (kind == "front" and n == 0) - PJ_FRONT * (kind == "ffn" and n == STEPS - 1)
            return c % 2, n * (PJ // 2) + c // 2, n * PJ + c + 1

        PROJ = [(t, s, c) for t in range(TILES) for s in range(3) for c in range(2)]
        QK = [x for x in PROJ if x[1] < 2]
        LAG = 3
        ORDER = []
        for j in range(len(PROJ) + LAG):
            if j < len(PROJ):
                ORDER.append(("project", j))
            if j >= LAG and PROJ[j - LAG] in QK:
                ORDER.append(("turn", QK.index(PROJ[j - LAG])))
        BY_ACT = lambda i: i % 2 == 1

        block = ctx.enter_context(nc.Block())

        @block.sync
        def _(sp):
            def load_qkv(l):
                for k in range(KC):
                    sp.dma_start(w_qkv[:, k, :], dram["L1_ffn_Wqkv"][l, k * P:(k + 1) * P, :]).then_inc(wqkv_loaded, 16)
                sp.dma_start(qk_gain[:, :, :, :].rearrange("p a b d -> p (a b d)"),
                             dram["gains"][l, :].rearrange("(a n) -> a n", a=1).broadcast_to([P, 4 * DH])).then_inc(wqkv_loaded, 16)

            def load_o(l):
                sp.dma_start(w_o[:, :, :], dram["L1_ffn_Wo"][l].rearrange("(c p) n -> p c n", p=P)).then_inc(wo_loaded, 16)

            def load_ff(l):
                sp.dma_start(w_1[:, :, :], dram["L1_ffn_W1"][l].rearrange("(c p) n -> p c n", p=P)).then_inc(wf_loaded, 16)
                sp.dma_start(w_2[:, 0:FC - 1, :], dram["L1_ffn_W2"][l, 0:(FC - 1) * P, :].rearrange("(c p) n -> p c n", p=P)).then_inc(wf_loaded, 16)
                sp.dma_start(w_2[0:FR, FC - 1, :], dram["L1_ffn_W2"][l, (FC - 1) * P:FF, :]).then_inc(wf_loaded, 16)
                sp.dma_start(ff_cols[:, :], dram["ff_cols"][l]).then_inc(wf_loaded, 16)
                sp.dma_start(b2[:, :], dram["L1_ffn_b2"][l, :].rearrange("(a n) -> a n", a=1)).then_inc(wf_loaded, 16)

            def stage(dst, row, staged):
                half = D // 2
                sp.dma_start(dst[:, :, 0:half], stream[:, row, :, 0:half]).then_inc(staged, 16)
                sp.dma_start(dst[1:P, :, half:D], stream[0:P - 1, row, :, half:D]).then_inc(staged, 16)
                sp.dma_start(dst[0:1, 1, half:D], stream[P - 1:P, row, 0, half:D]).then_inc(staged, 16)

            def stage_attn(n, row, first):
                if not first:
                    sp.wait_ge(res_f, n - BATCH + 1)
                wait(sp, tp_full, tp_slot("front", n - 1)[2])
                stage(xs, row, xs_staged)

            def stage_ffn(n, row):
                sp.wait_ge(res_a, n + 1)
                apart(sp, passed)
                wait(sp, xn_ready, n)
                stage(xf, row, xf_staged)

            def layer(l, first=False, last=False):
                def step(r):
                    stage_ffn(l * BATCH + r, r)
                    stage_attn(l * BATCH + r + 2, r + 2, first)

                step(0)
                with sp.Fori(1, BATCH - 2) as r:
                    step(r)
                n = l * BATCH + BATCH - 2
                stage_ffn(n, BATCH - 2)
                if not last:
                    stage_attn(n + 2, 0, False)
                    sp.wait_ge(pj_full, pj_slot("front", n + 1, PJ_FRONT - 1)[2])
                    apart(sp, passed)
                    sp.wait_ge(rope_ready, n + 2)
                    load_qkv(l + 1)
                stage_ffn(n + 1, BATCH - 1)
                if not last:
                    sp.wait_ge(wo_done, n + 2)
                    load_o(l + 1)
                    stage_attn(n + 3, 1, False)
                    sp.wait_ge(w2_done, n + 2)
                    load_ff(l + 1)

            def store(row):
                sp.dma_start(out_dram[row].rearrange("(t p) d -> p t d", p=P), xall[:, row, :, :]).then_inc(stored, 16)

            sp.dma_start(rope_base[:, :, :, :, :].rearrange("p a b t d -> p (a b t d)"), dram["rope_base"]).then_inc(const_loaded, 16)
            load_qkv(0)
            sp.wait_ge(consts_set, 2)
            sp.wait_ge(entry_done, 1)
            stage_attn(0, 0, True)
            load_o(0)
            load_ff(0)
            stage_attn(1, 1, True)
            layer(0, first=True, last=(L == 1))
            if L > 2:
                with sp.Fori(1, L - 1) as l:
                    layer(l)
            if L > 1:
                layer(L - 1, last=True)
            for r in range(BATCH):
                sp.wait_ge(summed, r + 1)
                store(r)
            sp.wait_ge(stored, 16 * BATCH)

        def program(front, attn, ffn, start=None):
            def run(eng):
                if start:
                    start(eng)
                front(eng, 0, None)
                attn(eng, 0)
                front(eng, 1, 0)
                ffn(eng, 0)
                with eng.Fori(1, STEPS - 1) as n:
                    attn(eng, n)
                    front(eng, n + 1, n)
                    ffn(eng, n)
                attn(eng, STEPS - 1)
                front(eng, None, STEPS - 1)
                ffn(eng, STEPS - 1)
            return run

        @block.gpsimd
        def _(pool):
            def start(pool):
                pool.memset(xs[:, :, :], 0.0).then_inc(consts_set, 1)
                pool.memset(xf[:, :, :], 0.0).then_inc(consts_set, 1)
                pool.memset(minus_half[:, :], -0.5).then_inc(consts_set, 1)
                pool.memset(probs[:, :, :], 0.0).then_inc(consts_set, 1)
                pool.memset(ones[:, :], 1.0).then_inc(consts_set, 1)
                pool.memset(all_half[:, :], -0.5).then_inc(pool_init, 1)
                pool.memset(band[:, :], 0.0).then_inc(pool_init, 1)
                pool.wait_ge(pool_init, 1)
                pool.wait_ge(entry_stats, 1)
                pool.tensor_tensor(all_rstd[:, :], all_var[:, :], all_half[:, :], ALU.pow).then_inc(entry_rstd, 1)
                tiles = band[:, :].rearrange("p (t k) -> p t k", t=2)
                for i, (steps, base, per_query) in enumerate((([[0, 2], [-1, KW]], 64, 1), ([[0, 2], [1, KW]], 0, -1),
                                                              ([[1000, 2], [1, KW]], -64, 0))):
                    pool.wait_ge(pool_init, i + 2)
                    pool.affine_select(out=tiles, in_=tiles, pattern=steps, base=base, channel_multiplier=per_query,
                                       compare_op=ALU.is_ge, fill=-BIG).then_inc(pool_init, 1)
                pool.wait_ge(pool_init, 5)
                pool.wait_ge(const_loaded, 16)
                pool.wait_ge(consts_set, 5)

            def ln_rstd(n):
                pool.wait_ge(stats_ready, n + 1)
                pool.tensor_tensor(rstd[:, :], var_eps[:, :], minus_half[:, 0:TILES], ALU.pow).then_inc(rstd_ready, 1)

            def front(pool, n, ln):
                if n is not None:
                    pool.wait_ge(wqkv_loaded, 48 * (n // BATCH + 1))
                    wait(pool, qk_read, 8 * n)
                    for s in range(2):
                        last = pool.tensor_tensor(rope[:, s, :, :, :], rope_base[:, s, :, :, :],
                                                  qk_gain[:, s, :, :].rearrange("p b (a d) -> p b a d", a=1).broadcast_to([P, 2, TILES, DH]), ALU.mult)
                    last.then_inc(rope_ready, 1)
                    made = n * 20
                for i, (t, s, c) in enumerate(QK):
                    if ln is not None and i == 5:
                        ln_rstd(ln)
                    if n is None:
                        continue
                    b = i % 2
                    pool.wait_ge(qk_read, 8 * n + i + 1)
                    apart(pool, passed)
                    pool.tensor_scalar(ssm[:, b, :], ss[:, b, :], 1e-24, None, ALU.max).then_inc(pool_front, 1)
                    made += 1
                    pool.wait_ge(pool_front, made)
                    if i == 0:
                        wait(pool, exped, 16 * n)
                    r = r_q[:, t, 8 * c:8 * c + 8] if s == 0 else r_k[:, b, :]
                    pool.tensor_tensor(r, ssm[:, b, :], minus_half[:, :], ALU.pow).then_inc(pool_front, 1)
                    made += 1
                    wait(pool, tp_full, tp_slot("front", n, i - 1)[2] if i >= 2 else tp_slot("front", n - 1, i + 7)[2])
                    add = pool.tensor_tensor(qk_rot[:, b, :], qk_cos[:, b, :], qk_sin[:, b, :], ALU.add)
                    if s == 0:
                        add.then_inc(rotated, 1)
                        continue
                    add.then_inc(pool_front, 1)
                    made += 1
                    pool.wait_ge(pool_front, made)
                    heads = qk_rot[:, b, :].rearrange("p (h d) -> p h d", h=8)
                    pool.tensor_tensor(heads, heads, r_k[:, b, :].rearrange("p (h a) -> p h a", a=1).broadcast_to([P, 8, DH]),
                                       ALU.mult).then_inc(rotated, 1)

            program(front, lambda eng, n: None, lambda eng, n: None, start)(pool)

        @block.tensor
        def _(pe):
            def turn_in(slot):
                wait(pe, tp_taken[slot[0]], slot[1])
                return tp[slot[0]]

            def x_blocks(src, slot):
                bank = turn_in(slot)
                for k in range(KC):
                    for t in range(TILES):
                        last = pe.transpose(bank[:, (k * TILES + t) * P:(k * TILES + t + 1) * P], src[:, t, k * P:(k + 1) * P], ident[:, :])
                last.then_inc(tp_full, 1)
                pe.wait_ge(tp_taken[slot[0]], slot[1] + 1)

            def front(pe, n, ln):
                if n is None:
                    return
                pe.wait_ge(xs_staged, 48 * (n + 1))
                x_blocks(xs, tp_slot("front", n))
                for what, j in ORDER:
                    if what == "project":
                        t, s, c = PROJ[j]
                        b, before, _ = pj_slot("front", n, j)
                        if j == 0:
                            pe.wait_ge(wqkv_loaded, 48 * (n // BATCH + 1))
                        wait(pe, pj_taken[b], before)
                        for k in range(KC):
                            last = pe.matmul(pj[b][:, :], xT[:, k, t * P:(t + 1) * P], w_qkv[:, k, s * INNER + c * 512:s * INNER + (c + 1) * 512],
                                             start=(k == 0), stop=(k == KC - 1))
                        last.then_inc(pj_full, 1)
                    else:
                        pe.wait_ge(rotated, 8 * n + j + 1)
                        bank = turn_in(tp_slot("front", n, j + 1))
                        for m in range(4):
                            last = pe.transpose(bank[:, m * P:(m + 1) * P], qk_rot[:, j % 2, m * P:(m + 1) * P], ident[:, :])
                        last.then_inc(tp_full, 1)

            def attn(pe, n):
                def rows(h):
                    return slice(64 * (h % 2), 64 * (h % 2) + 64)

                def scores(h):
                    if h == 0:
                        for c in (TP_FRONT - 2, TP_FRONT - 1):
                            b, before, _ = tp_slot("front", n, c)
                            pe.wait_ge(tp_taken[b], before + 1)
                    wait(pe, exped, 16 * n + h - 1)
                    bank = sc[h % 2]
                    pe.matmul(bank[:, 0:2 * KW], ident_bf[:, :], band[:, :], start=True, stop=False)
                    pe.matmul(bank[:, 64:KW], qT[rows(h), h // 2, 0:P], kT[rows(h), h // 2, 0:P], start=False, stop=False)
                    pe.matmul(bank[:, KW:2 * KW], qT[rows(h), h // 2, P:2 * P], kT[rows(h), h // 2, 64:2 * P],
                              start=False, stop=True).then_inc(sc_full, 1)

                def turn(h):
                    pe.wait_ge(exped, 16 * n + h + 1)
                    bank = turn_in(tp_slot("attn", n, h))
                    for m in range(3):
                        last = pe.transpose(bank[:, m * P:(m + 1) * P], probs[:, h % 3, m * P:(m + 1) * P], ident[:, :])
                    last.then_inc(tp_full, 1)

                def values(h):
                    b, before, _ = tp_slot("attn", n, h)
                    pe.wait_ge(tp_taken[b], before + 1)
                    if h == 0:
                        for j in (PJ_FRONT - 2, PJ_FRONT - 1):
                            b, before, _ = pj_slot("front", n, j)
                            pe.wait_ge(pj_taken[b], before + 1)
                    if h % 4 == 0:
                        wait(pe, o_taken, 4 * n + h // 4)
                    at = (h % 4) * 2 * DH
                    hd = slice(h * DH, (h + 1) * DH)
                    pe.matmul(o_ps[:, at:at + DH], pT[:, h % 2, 0, :], v[:, 0, hd], start=True, stop=True)
                    pe.matmul(o_ps[:, at + DH:at + 2 * DH], pT[:, h % 2, 1, :], v[:, 0, hd], start=True, stop=False)
                    last = pe.matmul(o_ps[:, at + DH:at + 2 * DH], pT[:, h % 2, 2, :], v[:, 1, hd], start=False, stop=True)
                    last.then_inc(pT_used, 1)

                def o_turn(g):
                    pe.wait_ge(o_taken, 4 * n + g + 1)
                    bank = turn_in(tp_slot("attn", n, 16 + g))
                    for k in range(2):
                        for t in range(TILES):
                            last = pe.transpose(bank[:, (k * TILES + t) * P:(k * TILES + t + 1) * P], o_tok[:, t, (2 * g + k) * P:(2 * g + k + 1) * P], ident[:, :])
                    last.then_inc(tp_full, 1)

                for i in range(H + 3):
                    if i < H:
                        scores(i)
                    if 2 <= i < H + 2:
                        turn(i - 2)
                    if i >= 3:
                        values(i - 3)
                for g in range(4):
                    o_turn(g)
                for g in (2, 3):
                    b, before, _ = tp_slot("attn", n, 16 + g)
                    pe.wait_ge(tp_taken[b], before + 1)
                pe.wait_ge(wo_loaded, 16 * (n // BATCH + 1))
                wait(pe, res_f, n)
                for t in range(TILES):
                    for k in range(INNER // P):
                        last = pe.matmul(y_ps[:, t, :], oT[:, k, t * P:(t + 1) * P], w_o[:, k, :], start=(k == 0), stop=(k == INNER // P - 1))
                last.then_inc(wo_done, 1)

            def ffn(pe, n):
                pe.wait_ge(xn_ready, n + 1)
                x_blocks(xn, tp_slot("ffn", n))
                pe.wait_ge(wf_loaded, 80 * (n // BATCH + 1))
                for f in range(FC):
                    m = P if f < FC - 1 else FR
                    b, before, _ = pj_slot("ffn", n, f)
                    wait(pe, pj_taken[b], before)
                    for s in range(2):
                        for k in range(KC):
                            last = pe.matmul(pj[b][0:m, s * SEQ:(s + 1) * SEQ], w_1[:, k, s * FF + f * P:s * FF + f * P + m], xnT[:, k, :],
                                             start=(k == 0), stop=(k == KC - 1))
                    last.then_inc(pj_full, 1)
                pe.wait_ge(res_a, n + 1)
                for f in (FC - 2, FC - 1):
                    b, before, _ = pj_slot("ffn", n, f)
                    pe.wait_ge(pj_taken[b], before + 1)
                for t in range(TILES):
                    for f in range(FC):
                        m = P if f < FC - 1 else FR
                        pe.matmul(y_ps[:, t, :], hT[0:m, f, t * P:(t + 1) * P], w_2[0:m, f, :], start=(f == 0), stop=False)
                    last = pe.matmul(y_ps[:, t, :], ones[0:1, :], b2[0:1, :], start=False, stop=True)
                last.then_inc(w2_done, 1)

            def start(pe):
                for b in range(2):
                    pe.sem_inc(pj_taken[b], PJ_FFN // 2)
                pe.sem_inc(pj_full, PJ_FFN)
                pe.sem_inc(tp_taken[0], 1)
                pe.sem_inc(tp_full, 1)
                pe.wait_ge(consts_set, 5)

            program(front, attn, ffn, start)(pe)

        def copy_turned(eng, copy, n, i):
            t, s, c = QK[i]
            b, _, full = tp_slot("front", n, i + 1)
            eng.wait_ge(tp_full, full)
            copy((kT if s else qT)[:, 4 * c:4 * c + 4, t * P:(t + 1) * P], tp[b][:, :].rearrange("p (m q) -> p m q", m=4)).then_inc(tp_taken[b], 1)

        def copy_probs(eng, copy, n, h):
            b, _, full = tp_slot("attn", n, h)
            eng.wait_ge(tp_full, full)
            wait(eng, pT_used, 16 * n + h - 1)
            copy(pT[:, h % 2, :, :].rearrange("p m q -> p (m q)"), tp[b][:, 0:3 * P]).then_inc(tp_taken[b], 1)

        def copy_out(eng, copy, n, g):
            b, _, full = tp_slot("attn", n, 16 + g)
            eng.wait_ge(tp_full, full)
            copy(oT[:, 2 * g:2 * g + 2, :].rearrange("p k q -> p (k q)"), tp[b][:, :]).then_inc(tp_taken[b], 1)

        @block.scalar
        def _(act):
            def copy(dst, src):
                return nc.scalar.activation(dst, src, ACT.Copy)

            def front(act, n, ln):
                if n is None:
                    return
                b, _, full = tp_slot("front", n)
                act.wait_ge(tp_full, full)
                copy(xT[:, :, :].rearrange("p k q -> p (k q)"), tp[b][:, :]).then_inc(tp_taken[b], 1)
                for what, j in ORDER:
                    if what == "project":
                        t, s, c = PROJ[j]
                        b, _, full = pj_slot("front", n, j)
                        act.wait_ge(pj_full, full)
                        if s == 2:
                            copy(v[:, t, c * 512:(c + 1) * 512], pj[b][:, :]).then_inc(pj_taken[b], 1)
                            continue
                        i = QK.index(PROJ[j])
                        wait(act, qk_read, 8 * n + i - 1)
                        copy(qk_raw[:, i % 2, :], pj[b][:, :])
                        nc.scalar.activation(qk_sq[:, i % 2, :], pj[b][:, :], ACT.Square).then_inc(pj_taken[b], 1)
                    elif BY_ACT(j):
                        copy_turned(act, copy, n, j)

            def attn(act, n):
                def exps(h):
                    act.wait_ge(top_ready, 16 * n + h + 1)
                    wait(act, tp_full, tp_slot("attn", n, h - 3)[2] if h >= 3 else tp_slot("attn", n - 1, H + h - 3)[2])
                    for t in range(TILES):
                        src = sc[h % 2][:, 64:KW] if t == 0 else sc[h % 2][:, KW:2 * KW]
                        dst = probs[:, h % 3, 0:P] if t == 0 else probs[:, h % 3, P + 64:3 * P]
                        last = nc.scalar.activation(dst, src, ACT.Exp, bias=neg_top[:, h % 2, t:t + 1], scale=r_q[:, t, h:h + 1],
                                                    accum_out=p_sum[:, h, t:t + 1])
                    last.then_inc(exped, 1)

                for i in range(H + 2):
                    if i < H:
                        exps(i)
                    if i >= 2 and BY_ACT(i - 2):
                        copy_probs(act, copy, n, i - 2)
                for g in range(4):
                    if BY_ACT(g):
                        copy_out(act, copy, n, g)

            def ffn(act, n):
                b, _, full = tp_slot("ffn", n)
                act.wait_ge(tp_full, full)
                act.wait_ge(wf_loaded, 80 * (n // BATCH + 1))
                for k in range(KC):
                    last = nc.scalar.activation(xnT[:, k, :], tp[b][:, k * SEQ:(k + 1) * SEQ], ACT.Identity, bias=ln_b[:, k:k + 1], scale=ln_g[:, k:k + 1])
                last.then_inc(tp_taken[b], 1)
                for f in range(FC):
                    m = P if f < FC - 1 else FR
                    b, _, full = pj_slot("ffn", n, f)
                    act.wait_ge(pj_full, full)
                    nc.scalar.activation(gate[0:m, f % 2, :], pj[b][0:m, SEQ:2 * SEQ], ACT.Gelu, bias=b1[0:m, 1, f:f + 1]).then_inc(gated, 1)

            program(front, attn, ffn, lambda act: act.wait_ge(consts_set, 5))(act)

        @block.vector
        def _(dve):
            def copy(dst, src):
                return nc.vector.tensor_copy(dst, src)

            def start(dve):
                tiles_in = xall[:, :, :, :].rearrange("p b t d -> p (b t) d")
                tiles_out = stream[:, :, :, :].rearrange("p b t d -> p (b t) d")
                for i in range(ALLT):
                    last = nc.vector.bn_stats(all_bn[:, i, :], tiles_in[:, i, :])
                last.then_inc(dve_entry, 1)
                dve.wait_ge(dve_entry, 1)
                for i in range(ALLT):
                    last = nc.vector.bn_aggr(all_mv[:, i, :], all_bn[:, i, :])
                last.then_inc(dve_entry, 1)
                dve.wait_ge(dve_entry, 2)
                nc.vector.tensor_scalar(all_var[:, :], all_mv[:, :, 1], 1e-5, None, ALU.add).then_inc(entry_stats, 1)
                dve.wait_ge(entry_rstd, 1)
                for i in range(ALLT):
                    last = nc.vector.tensor_scalar(tiles_out[:, i, :], tiles_in[:, i, :], all_mv[:, i, 0:1], all_rstd[:, i:i + 1],
                                                   ALU.subtract, ALU.mult)
                last.then_inc(entry_done, 1)
                dve.wait_ge(entry_done, 1)
                dve.wait_ge(consts_set, 5)

            def ln_stats(n):
                dve.wait_ge(xf_staged, 48 * (n + 1))
                for t in range(TILES):
                    last = nc.vector.bn_stats(bn[:, t, :], xf[:, t, :])
                last.then_inc(dve_ln, 1)
                dve.wait_ge(dve_ln, 2 * n + 1)
                apart(dve, passed)
                for t in range(TILES):
                    last = nc.vector.bn_aggr(mv[:, t, :], bn[:, t, :])
                last.then_inc(dve_ln, 1)
                dve.wait_ge(dve_ln, 2 * n + 2)
                nc.vector.tensor_scalar(var_eps[:, :], mv[:, :, 1], 1e-5, None, ALU.add).then_inc(stats_ready, 1)

            def ln_apply(n):
                dve.wait_ge(rstd_ready, n + 1)
                wait(dve, tp_full, tp_slot("ffn", n - 1)[2])
                for t in range(TILES):
                    last = nc.vector.tensor_scalar(xn[:, t, :], xf[:, t, :], mv[:, t, 0:1], rstd[:, t:t + 1], ALU.subtract, ALU.mult)
                last.then_inc(xn_ready, 1)

            def front(dve, n, ln):
                if n is not None:
                    dve.wait_ge(rope_ready, n + 1)
                for what, j in ORDER:
                    if what == "project" and ln is not None and j == 4:
                        ln_stats(ln)
                    if what == "project" and ln is not None and j == 8:
                        ln_apply(ln)
                    if n is None:
                        continue
                    if what == "turn":
                        if not BY_ACT(j):
                            copy_turned(dve, copy, n, j)
                        continue
                    t, s, c = PROJ[j]
                    if s == 2:
                        continue
                    i = QK.index(PROJ[j])
                    b, before, _ = pj_slot("front", n, j)
                    dve.wait_ge(pj_taken[b], before + 1)
                    wait(dve, rotated, 8 * n + i - 1)
                    wait(dve, pool_front, n * 20 + sum(2 + QK[x][1] for x in range(i - 1)))
                    raw, cos, sin = (x[:, i % 2, :].rearrange("p (h d) -> p h d", h=8) for x in (qk_raw, qk_cos, qk_sin))
                    nc.vector.tensor_reduce(ss[:, i % 2, :], qk_sq[:, i % 2, :].rearrange("p (h d) -> p h d", h=8), AX, ALU.add)

                    def table(r, lo, hi):
                        return rope[:, s, r, t, lo:hi].rearrange("p (a d) -> p a d", a=1).broadcast_to([P, 8, hi - lo])

                    nc.vector.tensor_tensor(cos, raw, table(0, 0, DH), ALU.mult)
                    hd = DH // 2
                    nc.vector.tensor_tensor(sin[:, :, 0:hd], raw[:, :, hd:DH], table(1, 0, hd), ALU.mult)
                    nc.vector.tensor_tensor(sin[:, :, hd:DH], raw[:, :, 0:hd], table(1, hd, DH), ALU.mult).then_inc(qk_read, 1)

            def attn(dve, n):
                def tops(h):
                    dve.wait_ge(sc_full, 16 * n + h + 1)
                    if h == 0:
                        dve.wait_ge(rotated, 8 * n + 8)
                    nc.vector.tensor_reduce(top[:, h % 2, :], sc[h % 2][:, 0:2 * KW].rearrange("p (t k) -> p t k", t=2), AX, ALU.max).then_inc(dve_attn, 1)
                    dve.wait_ge(dve_attn, 20 * n + marks[h])
                    nc.vector.scalar_tensor_tensor(neg_top[:, h % 2, :], top[:, h % 2, :], -1.0, r_q[:, :, h], ALU.mult, ALU.mult).then_inc(top_ready, 1)

                def out_group(g):
                    dve.wait_ge(pT_used, 16 * n + 4 * g + 4)
                    nc.vector.reciprocal(p_inv[:, :, :], p_sum[:, 4 * g:4 * g + 4, :]).then_inc(dve_attn, 1)
                    dve.wait_ge(dve_attn, 20 * n + marks[H + g])
                    for t in range(TILES):
                        last = nc.vector.tensor_tensor(
                            o_tok[:, t, g * 4 * DH:(g + 1) * 4 * DH].rearrange("p (h d) -> p h d", h=4),
                            o_ps[:, :].rearrange("p (h t d) -> p h t d", h=4, t=TILES)[:, :, t, :],
                            p_inv[:, :, t:t + 1].broadcast_to([P, 4, DH]), ALU.mult)
                    last.then_inc(o_taken, 1)

                order = []
                for i in range(H + 5):
                    if i < H:
                        order.append(("tops", i))
                    if 2 <= i < H + 2 and not BY_ACT(i - 2):
                        order.append(("copy", i - 2))
                    if i >= 7 and (i - 7) % 4 == 0 and (i - 7) // 4 < 4:
                        order.append(("group", (i - 7) // 4))
                marks, made = {}, 0
                for what, k in order:
                    if what != "copy":
                        made += 1
                        marks[k if what == "tops" else H + k] = made
                assert made == 20
                for what, k in order:
                    if what == "tops":
                        tops(k)
                    elif what == "copy":
                        copy_probs(dve, copy, n, k)
                    else:
                        out_group(k)
                for g in range(4):
                    if not BY_ACT(g):
                        copy_out(dve, copy, n, g)
                dve.wait_ge(wo_done, n + 1)
                row = n % BATCH
                nc.vector.tensor_tensor(stream[:, row, :, :], y_ps[:, :, :], stream[:, row, :, :], ALU.add).then_inc(res_a, 1)

            def ffn(dve, n):
                for f in range(FC):
                    m = P if f < FC - 1 else FR
                    b, _, _ = pj_slot("ffn", n, f)
                    dve.wait_ge(gated, FC * n + f + 1)
                    nc.vector.scalar_tensor_tensor(hT[0:m, f, :], pj[b][0:m, 0:SEQ], b1[0:m, 0, f:f + 1], gate[0:m, f % 2, :],
                                                   ALU.add, ALU.mult).then_inc(pj_taken[b], 1)
                dve.wait_ge(w2_done, n + 1)
                row = n % BATCH
                nc.vector.tensor_tensor(stream[:, row, :, :], y_ps[:, :, :], stream[:, row, :, :], ALU.add).then_inc(res_f, 1)

            program(front, attn, ffn, start)(dve)
            for row in range(BATCH):
                dve.wait_ge(res_f, (L - 1) * BATCH + row + 1)
                nc.vector.tensor_tensor(xall[:, row, :, :], xall[:, row, :, :], stream[:, row, :, :], ALU.add).then_inc(summed, 1)


def build(nc, dram, out_dram):
    with ExitStack() as ctx:
        xall = ctx.enter_context(nc.sbuf_tensor("x_all", [P, BATCH, TILES, D], F32))
        ident = ctx.enter_context(nc.sbuf_tensor("identity", [P, P], F32))
        ident_bf = ctx.enter_context(nc.sbuf_tensor("identity_bf", [P, P], BF16))
        x_loaded = ctx.enter_context(nc.semaphore("x_loaded"))
        passed = ctx.enter_context(nc.semaphore("passed"))
        identity_step = ctx.enter_context(nc.semaphore("identity_step"))
        with nc.Block() as block:
            @block.sync
            def _(sp):
                sp.dma_start(xall[:, :, :, :].rearrange("p b t d -> p (b t) d"), dram["x"].rearrange("b (t p) d -> p (b t) d", p=P)).then_inc(x_loaded, 16)
                sp.wait_ge(x_loaded, 16)

            @block.gpsimd
            def _(pool):
                pool.memset(ident[:, :], 0.0).then_inc(identity_step, 1)
                pool.wait_ge(identity_step, 1)
                pool.affine_select(out=ident[:, :], in_=ident[:, :], compare_op=ALU.not_equal, fill=1.0, base=0,
                                   pattern=[[-1, P]], channel_multiplier=1).then_inc(identity_step, 1)
                pool.wait_ge(identity_step, 2)
                pool.tensor_copy(ident_bf[:, :], ident[:, :]).then_inc(identity_step, 1)
                pool.wait_ge(identity_step, 3)
        first_layers(nc, xall, ident, ident_bf, passed, dram)
        local_layers(nc, xall, ident, ident_bf, passed, dram, DEPTH, out_dram)


def rotary_base():
    dim, window, qk_scale = 64, 64, 8.0
    half = np.arange(0, dim, 2, dtype=np.float32)
    inv_freq = (1.0 / 10000.0 ** (half / dim)).astype(np.float32)
    t = np.arange(SEQ, dtype=np.float32)
    freqs = np.concatenate([t[:, None] * inv_freq[None, :]] * 2, -1)
    base = (half + 0.4 * dim) / (1.4 * dim)
    power = (t - SEQ // 2) / (window // 2)
    scale = np.concatenate([(base[None, :] ** power[:, None]).astype(np.float32)] * 2, -1)
    sign = np.where(np.arange(dim) < dim // 2, -1.0, 1.0)
    q = np.stack([np.cos(freqs) * scale, np.sin(freqs) * scale * sign])
    k = np.stack([np.cos(freqs) / scale * qk_scale, np.sin(freqs) / scale * qk_scale * sign])
    both = np.stack([q, k]).reshape(2, 2, TILES, P, dim)
    return np.ascontiguousarray(both.transpose(3, 0, 1, 2, 4).reshape(P, -1), dtype=np.float32)


def lay_out(inp):
    a = {k: np.asarray(v) for k, v in inp.items()}
    c = lambda x: np.ascontiguousarray(x)
    o = {"x": c(a["x"]), "ctx": c(a["ctx_1024"]), "mask": c(a["mask_BxS2_ik0"])}
    o["a_w"] = c(np.stack([a[f"L0_attn_W{w}"].T for w in "qkvo"]))
    o["gate_w"] = c(np.concatenate([a["L0_xattn_igate_w"], a["L0_xattn_fgate_w"]]).T)
    o["gate_b"] = c(np.stack([a["L0_xattn_igate_b"], a["L0_xattn_fgate_b"]], 1))
    o["out_w"] = c(a["L0_xattn_out_w"])
    o["c_wq"] = c(a["L0_ffn_Wq"].T)
    keys = a["L0_ffn_keys"]
    nk, dh = keys.shape[1], keys.shape[3]
    o["c_keys"] = c(keys.reshape(2, 2, nk, 2, dh).transpose(1, 4, 3, 0, 2).reshape(2 * dh, 4 * nk))
    o["c_wg"], o["c_wu"], o["c_wd"] = c(a["L0_ffn_Wg"].T), c(a["L0_ffn_Wu"].T), c(a["L0_ffn_Wd"].T)
    o["emb"] = c(np.concatenate([a["L0_ffn_down_embed"], a["L0_ffn_up_embed"]], 1))
    o["d_w"] = c(np.stack([a[f"L1_attn_W{w}"] for w in "qkv"]))
    o["e_wq"] = c(a["L1_xattn_Wq"].reshape(D, 2, 2, 4, 64).transpose(0, 1, 3, 2, 4).reshape(D, -1))
    o["e_wk"], o["e_wv"] = c(a["L1_xattn_Wk"]), c(a["L1_xattn_Wv"])
    o["e_wo"] = c(a["L1_xattn_Wo"].reshape(2, 2, 4, 64, D).transpose(0, 2, 1, 3, 4).reshape(-1, D))
    f = "L1_ffn_"
    for w in ("Wqkv", "Wo", "W1", "W2", "b2"):
        o[f + w] = c(a[f + w])
    rolled = lambda g: np.concatenate([g, g[:, 32:], g[:, :32]], 1)
    o["gains"] = c(np.concatenate([rolled(a[f + "q_scale"]), rolled(a[f + "k_scale"])], 1))
    depth, two_ff = a[f + "b1"].shape
    ff = two_ff // 2
    chunks = (ff + P - 1) // P
    b1 = np.pad(a[f + "b1"].reshape(depth, 2, ff), ((0, 0), (0, 0), (0, chunks * P - ff)))
    cols = [b1.reshape(depth, 2, chunks, P).transpose(0, 3, 1, 2).reshape(depth, P, -1)]
    cols += [a[f + g].reshape(depth, KC, P).transpose(0, 2, 1) for g in ("ln_g", "ln_b")]
    o["ff_cols"] = c(np.concatenate(cols, 2))
    o["rope_base"] = rotary_base()
    return o


def kernel(**inputs):
    import concourse.bacc as bacc
    from concourse.bass_utils import run_bass_kernel_spmd

    nc = bacc.Bacc("TRN2", target_bir_lowering=False, num_devices=1)
    arrays = lay_out(inputs)
    dram = {k: nc.dram_tensor(f"in_{k}", v.shape, mybir.dt.from_np(v.dtype), kind="ExternalInput").ap() for k, v in arrays.items()}
    out = nc.dram_tensor("out", (BATCH, SEQ, D), F32, kind="ExternalOutput").ap()
    build(nc, dram, out)
    r = run_bass_kernel_spmd(nc, [{f"in_{k}": v for k, v in arrays.items()}], core_ids=[0])
    return r.results[0]["out"]
```

```python
import numpy as np
from contextlib import ExitStack
import concourse.bass as bass
from concourse import mybir

F32 = mybir.dt.float32
BF16 = mybir.dt.bfloat16
I32 = mybir.dt.int32
U32 = mybir.dt.uint32
ALU = mybir.AluOpType
ACT = mybir.ActivationFunctionType
AX = mybir.AxisListType.X

P = 128
BATCH, SEQ, D = 8, 256, 256
TILES = SEQ // P
KC = D // P
BIG = 1.0e30
DEPTH = 6


def wait(eng, sem, value):
    if isinstance(value, int) and value <= 0:
        return
    eng.wait_ge(sem, value)


def apart(eng, passed):
    eng.sem_inc(passed, 1)


def first_layers(nc, xall, ident, ident_bf, passed, dram):
    H4, DH = 4, 64
    NK, TOPK = 128, 8
    EXPERTS = dram["emb"].shape[0]
    GROUPS = TILES * H4
    RG = 2
    INTER = dram["c_wg"].shape[1]
    MC = INTER // P
    BLK, NB = 16, SEQ // 16
    SCALE = 1.0 / 8.0

    EVENTS_AB = ["a_hT", "a_q", "a_k", "a_v", "a_z", "a_o", "a_y", "b_cT", "b_hT", "b_g", "b_gt"] + [f"b_m{h}" for h in range(H4)] \
        + [f"b_qk{h}" for h in range(H4)] + ["b_h0", "b_h1"]
    EVENTS_C = ["c_hT", "c_q0", "c_q1"] + [f"c_s{i}" for i in range(4)] + [f"c_m{i}" for i in range(MC)] + ["c_y0", "c_y1"]
    EVENTS_DE = ["d_hT", "d_q", "d_k", "d_v", "d_s", "d_pT", "d_o"] + ["e_hT", "e_cT", "e_k", "e_v", "e_q", "e_s0", "e_s1", "e_pT", "e_o", "e_y", "e_u"]
    C_PIECES = [["c_hT"], ["c_q0", "c_q1"], [f"c_s{i}" for i in range(4)], [], [f"c_m{i}" for i in range(MC // 2)],
                [f"c_m{i}" for i in range(MC // 2, MC)], ["c_y0", "c_y1"]]
    DE_PIECES = [["d_hT"], ["d_q", "d_k", "d_v"], ["d_s"], ["d_pT", "d_o"], ["e_hT", "e_cT"], ["e_k", "e_v", "e_q"], ["e_s0", "e_s1"],
                 ["e_pT", "e_o"], ["e_y", "e_u"]]
    TURNS = "c c d c d d d d c c d c d c d d".split()
    assert sum(C_PIECES, []) == EVENTS_C and sum(DE_PIECES, []) == EVENTS_DE
    assert TURNS.count("c") == len(C_PIECES) and TURNS.count("d") == len(DE_PIECES)
    EVENTS_CDE, left = [], {"c": list(C_PIECES), "d": list(DE_PIECES)}
    for turn in TURNS:
        EVENTS_CDE += left[turn].pop(0)
    NAB, NC_, NDE = len(EVENTS_AB), len(EVENTS_C), len(EVENTS_DE)
    EV = NAB + NC_ + NDE
    BANKS = 8
    assert EV % BANKS == 0

    ctx = ExitStack()
    with ctx:
        def sb(name, shape, dt=F32):
            return ctx.enter_context(nc.sbuf_tensor("f_" + name, shape, dt))

        def sem(name):
            return ctx.enter_context(nc.semaphore("f_" + name))

        a_w = sb("a_w", [P, 4, KC, D])
        gate_w = sb("gate_w", [P, 3 * KC, 8])
        gate_b = sb("gate_b", [H4, 2])
        out_gain = sb("out_gain", [P, D])
        c_wq = sb("c_wq", [P, KC, 2 * H4 * DH])
        c_keys = sb("c_keys", [P, 2, 2, NK])
        c_wg, c_wu = sb("c_wg", [P, KC, INTER]), sb("c_wu", [P, KC, INTER])
        c_wd = sb("c_wd", [P, MC, D])
        d_w = sb("d_w", [P, 3, KC, D])
        e_wq = sb("e_wq", [P, KC, 16 * DH])
        e_wk, e_wv = sb("e_wk", [P, KC, D]), sb("e_wv", [P, KC, D])
        e_wo = sb("e_wo", [P, 8, D])
        block_mask = sb("block_mask", [P, KC, P])
        later = sb("later", [P, P], BF16)
        future = sb("future", [P, P], BF16)
        head_row = sb("head_row", [H4, H4, P])
        unpool = sb("unpool", [NB, SEQ])
        iota8 = sb("iota8", [P, TOPK])
        minus_half = sb("minus_half", [P, 8])
        zeros = sb("zeros", [H4, SEQ])
        h = sb("h", [P, TILES, D])
        hT = sb("hT", [P, KC, SEQ])
        norm_bufs = [(sb(f"bn{i}", [P, TILES, 6]), sb(f"mv{i}", [P, TILES, 2]), sb(f"var_eps{i}", [P, TILES]), sb(f"rstd{i}", [P, TILES])) for i in range(2)]
        hT_de = sb("hT_de", [P, KC, SEQ])
        proj0, proj1, proj2 = (sb(f"proj{i}", [P, 2, 256]) for i in range(3))
        c_qT = sb("c_qT", [P, 2 * H4 * DH // P, SEQ])
        a_q, a_k, a_vT, a_oT = proj0, proj1, c_qT[:, 0:2, :], c_qT[:, 2:4, :]
        a_s, a_e, a_p = sb("a_s", [P, KC, P]), sb("a_e", [P, KC, P]), sb("a_p", [P, KC, P])
        a_top, a_neg, a_sum, a_inv = (sb(x, [P, KC]) for x in ("a_top", "a_neg", "a_sum", "a_inv"))
        ctx_tok = sb("ctx_tok", [P, TILES, D])
        ctx_one = sb("ctx_one", [P, TILES, H4, DH + 1])
        ctxT = sb("ctxT", [P, KC, SEQ])
        g_in, g_f, g_abs, g_exp, g_ln, g_log, g_cs, g_a, g_top, g_low, g_norm = (sb("g_" + x, [H4, SEQ]) for x in
            ("in", "f", "abs", "exp", "ln", "log", "cs", "a", "top", "low", "norm"))
        gT = sb("gT", [P, 2, TILES, H4])
        decay = sb("decay", [P, 2, 3 * P])
        mT = sb("mT", [P, MC, SEQ])
        b_c = mT[:, :, :].rearrange("p i q -> p (i q)")[:, 0:H4 * 3 * P].rearrange("p (h q) -> p h q", h=H4)
        b_norm, b_inv, b_mean, b_var, b_rstd = (sb(x, [P, TILES * H4]) for x in ("b_norm", "b_inv", "b_mean", "b_var", "b_rstd"))
        heads_buf = sb("heads_buf", [P, 2, TILES * H4, DH])
        b_u, b_sq = heads_buf[:, 0], heads_buf[:, 1]
        hc = sb("hc", [P, TILES, D])
        best = sb("best", [P, 2, GROUPS, TOPK])
        besti = sb("besti", [P, 2, GROUPS, TOPK], U32)
        bestf = sb("bestf", [P, 2, GROUPS, TOPK])
        pair_buf = sb("pair_buf", [P, 2, GROUPS * TOPK * TOPK])
        pair = pair_buf[:, 0, :].rearrange("p (g i j) -> p g i j", g=GROUPS, i=TOPK)
        pick = pair_buf[:, 1, :].rearrange("p (gk i) -> p gk i", i=TOPK)
        score = sb("score", [P, GROUPS, TOPK])
        pairi = sb("pairi", [P, GROUPS, TOPK], U32)
        pos = sb("pos", [P, 2, GROUPS * TOPK], U32)
        posf = sb("posf", [P, 2, GROUPS * TOPK])
        picked = sb("picked", [P, 2, GROUPS * TOPK])
        expertf = sb("expertf", [P, GROUPS * TOPK])
        expert = sb("expert", [P, GROUPS * TOPK], U32)
        sm_d, sm_e, weight = (sb(x, [P, GROUPS, TOPK]) for x in ("sm_d", "sm_e", "weight"))
        sm_sum, sm_inv = sb("sm_sum", [P, GROUPS]), sb("sm_inv", [P, GROUPS])
        rows = sb("rows", [P, RG, TOPK, 2 * D])
        dots, low, expd, sig, silu, coef = (sb(x, [P, 2, TOPK]) for x in ("dots", "low", "expd", "sig", "silu", "coef"))
        m_gate = sb("m_gate", [P, 2, SEQ])
        d_qT, d_kT, d_v = proj0, proj1, proj2
        d_p, d_pT = sb("d_p", [P, 3 * P]), sb("d_pT", [P, 3 * P])
        d_top, d_neg, d_sum, d_inv = (sb(x, [P, TILES]) for x in ("d_top", "d_neg", "d_sum", "d_inv"))
        ctx_e = sb("ctx_e", [P, TILES, D])
        ctxT_e = ctxT
        pooled = sb("pooled", [P, KC, NB])
        e_kT, e_v = proj0, proj1
        e_qT = sb("e_qT", [P, 2, 4 * NB])
        mask_i = sb("mask_i", [4 * NB, SEQ], I32)
        keep, shut = sb("keep", [4 * NB, SEQ]), sb("shut", [4 * NB, SEQ])
        e_s = sb("e_s", [4 * NB, H4, SEQ])
        e_p = heads_buf[0:4 * NB, :, :, :].rearrange("p a h d -> p (a h d)").rearrange("p (g n) -> p g n", g=H4)
        e_top, e_neg, e_sum, e_inv = (sb(x, [4 * NB, H4]) for x in ("e_top", "e_neg", "e_sum", "e_inv"))
        e_pT = proj2[:, :, :].rearrange("p t (g n) -> p t g n", g=H4)
        e_o = sb("e_o", [P, 2 * 4 * NB])
        e_y = sb("e_y", [NB, D])

        bank = [ctx.enter_context(nc.psum_tensor(f"fp{i}", [P, 512], F32)) for i in range(BANKS)]

        loaded = {s: sem("loaded_" + s) for s in "abcde"}
        LOADS = {"a": 1, "b": 3, "c": 5, "d": 1, "e": 4}
        consts_set, set_step, gain_set = sem("consts_set"), sem("set_step"), sem("gain_set")
        ctx_loaded, ctx_e_loaded, mask_loaded = sem("ctx_loaded"), sem("ctx_e_loaded"), sem("mask_loaded")
        ps_full, ps_taken = sem("ps_full"), [sem(f"ps_taken{i}") for i in range(BANKS)]
        stats = {s: sem("stats_" + s) for s in "abcde"}
        rstds = {s: sem("rstds_" + s) for s in "abcde"}
        normed = {s: sem("normed_" + s) for s in "abcde"}
        a_masked, a_exped, a_probs = sem("a_masked"), sem("a_exped"), sem("a_probs")
        ctx_split = sem("ctx_split")
        gates_biased, gates_ln, gates_top, gates_norm = sem("gates_biased"), sem("gates_ln"), sem("gates_top"), sem("gates_norm")
        decayed, weighted = sem("decayed"), sem("weighted")
        b_centred, b_rooted, b_added = sem("b_centred"), sem("b_rooted"), sem("b_added")
        routed, sm_ready, sm_exped = sem("routed"), sem("sm_ready"), sem("sm_exped")
        gathered = [sem(f"gathered{i}") for i in range(RG)]
        rows_used = sem("rows_used")
        dotted, dots_exped = sem("dotted"), sem("dots_exped")
        m_silu = sem("m_silu")
        c_added = sem("c_added")
        d_topped, d_exped, d_added = sem("d_topped"), sem("d_exped"), sem("d_added")
        e_pooled, e_topped, e_exped, e_normed, e_added = sem("e_pooled"), sem("e_topped"), sem("e_exped"), sem("e_normed"), sem("e_added")
        act_b = sem("act_b")
        dve_ab, dve_c, dve_sum, dve_de = sem("dve_ab"), sem("dve_c"), sem("dve_sum"), sem("dve_de")

        class Slot:
            def __init__(self, name, n):
                step = n + (name in EVENTS_DE)
                if isinstance(n, int) and step == 0:
                    c = NDE + (EVENTS_AB + EVENTS_C).index(name)
                elif isinstance(n, int) and step == BATCH:
                    c = EVENTS_DE.index(name)
                else:
                    c = (EVENTS_AB + EVENTS_CDE).index(name)
                n = step
                self.bank, self.taken = bank[c % BANKS], ps_taken[c % BANKS]
                self.before = n * (EV // BANKS) + c // BANKS
                self.after = self.before + 1
                self.full = n * EV + c + 1

        class Chain:
            def __init__(self, eng, semaphore, n, per):
                self.eng, self.sem, self.base, self.per, self.made = eng, semaphore, n * per, per, 0

            def link(self, instruction):
                instruction.then_inc(self.sem, 1)
                self.made += 1
                self.eng.wait_ge(self.sem, self.base + self.made)

            def close(self):
                assert self.made == self.per, (self.made, self.per)

        def flat(x):
            return x.rearrange("p a b -> p (a b)")

        POINTS = {"a0": [0], "a1": [1], "a2": [2], "a3": [3], "b0": [4], "b1": [5], "b2": [6], "b3": [7]}

        def take_turns(**parts):
            for turn in TURNS:
                if turn in parts:
                    next(parts[turn], None)

        def program(ab, route, de, start, tail):
            def run(eng):
                start(eng)
                ab(eng, 0, None)
                take_turns(c=route(eng, 0))
                with eng.Fori(1, BATCH) as n:
                    ab(eng, n, n - 1)
                    take_turns(c=route(eng, n), d=de(eng, n - 1))
                tail(eng, BATCH - 1)
                take_turns(d=de(eng, BATCH - 1))
            return run

        block = ctx.enter_context(nc.Block())

        @block.sync
        def _(sp):
            def load(name, dst, src):
                sp.dma_start(dst, src).then_inc(loaded[name], 16)

            def load_ctx(n):
                wait(sp, ps_full, Slot("b_cT", n - 1).full if not isinstance(n, int) or n > 0 else 0)
                apart(sp, passed)
                wait(sp, ctx_split, n)
                sp.dma_start(ctx_tok[:, :, :], dram["ctx"][n].rearrange("(t p) d -> p t d", p=P)).then_inc(ctx_loaded, 16)

            def load_e(n):
                if not isinstance(n, int) or n > 0:
                    wait(sp, e_added, n)
                sp.dma_start(ctx_e[:, :, :], dram["ctx"][n].rearrange("(t p) d -> p t d", p=P)).then_inc(ctx_e_loaded, 16)
                sp.dma_start(mask_i[:, :], dram["mask"][n].rearrange("(a n) -> a n", a=1).broadcast_to([4 * NB, SEQ])).then_inc(mask_loaded, 16)

            load("a", a_w[:, :, :, :].rearrange("p w k n -> p (w k) n"), dram["a_w"].rearrange("w (k p) n -> p (w k) n", p=P))
            load_ctx(0)
            load("b", gate_w[:, :, :], dram["gate_w"].rearrange("(k p) n -> p k n", p=P))
            load("b", gate_b[:, :], dram["gate_b"])
            load("b", out_gain[:, :], dram["out_w"].rearrange("(a n) -> a n", a=1).broadcast_to([P, D]))
            load("c", c_wq[:, :, :], dram["c_wq"].rearrange("(k p) n -> p k n", p=P))
            load("c", c_keys[:, :, :, :].rearrange("p a b k -> p (a b k)"), dram["c_keys"])
            load("c", c_wg[:, :, :], dram["c_wg"].rearrange("(k p) n -> p k n", p=P))
            load("c", c_wu[:, :, :], dram["c_wu"].rearrange("(k p) n -> p k n", p=P))
            load("c", c_wd[:, :, :], dram["c_wd"].rearrange("(k p) n -> p k n", p=P))
            load("d", d_w[:, :, :, :].rearrange("p w k n -> p (w k) n"), dram["d_w"].rearrange("w (k p) n -> p (w k) n", p=P))
            load("e", e_wq[:, :, :], dram["e_wq"].rearrange("(k p) n -> p k n", p=P))
            load("e", e_wk[:, :, :], dram["e_wk"].rearrange("(k p) n -> p k n", p=P))
            load("e", e_wv[:, :, :], dram["e_wv"].rearrange("(k p) n -> p k n", p=P))
            load("e", e_wo[:, :, :], dram["e_wo"].rearrange("(c p) n -> p c n", p=P))
            load_e(0)
            load_ctx(1)
            with sp.Fori(1, BATCH - 1) as n:
                load_ctx(n + 1)
                load_e(n)
            load_e(BATCH - 1)

        @block.gpsimd
        def _(pool):
            made = [0]

            def select(view, pattern, base, mult, fill):
                pool.wait_ge(set_step, made[0])
                pool.affine_select(out=view, in_=view, pattern=pattern, base=base, channel_multiplier=mult,
                                   compare_op=ALU.is_ge, fill=fill).then_inc(set_step, 1)
                made[0] += 1

            def fill(view, value):
                pool.memset(view, value).then_inc(set_step, 1)
                made[0] += 1

            def start(pool):
                fill(block_mask[:, :, :], 0.0)
                blocks = block_mask[:, :, :].rearrange("p c (b j) -> p (c b) j", j=BLK).rearrange("p (c b) j -> p c b j", c=KC)
                select(blocks, [[0, KC], [-16, 8], [0, BLK]], 0, 1, -BIG)
                select(blocks, [[0, KC], [16, 8], [0, BLK]], 15, -1, -BIG)
                fill(later[:, :], 0.0)
                select(later[:, :], [[1, P]], 0, -1, BIG)
                fill(future[:, :], 0.0)
                select(future[:, :], [[-1, P]], 0, 1, -BIG)
                fill(head_row[:, :, :], 1.0)
                select(head_row[:, :, :], [[-1, H4], [0, P]], 0, 1, 0.0)
                select(head_row[:, :, :], [[1, H4], [0, P]], 0, -1, 0.0)
                fill(unpool[:, :], 1.0)
                select(unpool[:, :], [[1, SEQ]], 0, -BLK, 0.0)
                select(unpool[:, :], [[-1, SEQ]], BLK - 1, BLK, 0.0)
                pool.iota(iota8[:, :], pattern=[[1, TOPK]], base=0, channel_multiplier=0, allow_small_or_imprecise_dtypes=True).then_inc(set_step, 1)
                made[0] += 1
                fill(minus_half[:, :], -0.5)
                fill(zeros[:, :], 0.0)
                fill(ctx_one[:, :, :, :], 1.0)
                pool.wait_ge(set_step, made[0])
                pool.sem_inc(consts_set, 1)

            def rooted(pool, s, n):
                _, _, var_eps, rstd = norm_bufs[s in "de"]
                pool.wait_ge(stats[s], n + 1)
                pool.tensor_tensor(rstd[:, :], var_eps[:, :], minus_half[:, 0:TILES], ALU.pow).then_inc(rstds[s], 1)

            def gather(pool, n, g):
                if g >= RG:
                    pool.wait_ge(rows_used, GROUPS * n + g - RG + 1)
                else:
                    wait(pool, rows_used, GROUPS * n)
                apart(pool, passed)
                for k in range(TOPK):
                    pool.indirect_dma_start(rows[:, g % RG, k, :], None, dram["emb"],
                                            bass.IndirectOffsetOnAxis(ap=expert[:, g * TOPK + k:g * TOPK + k + 1], axis=0)).then_inc(gathered[g % RG], 16)

            def point(pool, where, m):
                if m is not None:
                    for g in POINTS[where]:
                        if g + RG < GROUPS:
                            gather(pool, m, g + RG)

            def ab(pool, n, m):
                rooted(pool, "a", n)
                point(pool, "a0", m)
                point(pool, "a1", m)
                rooted(pool, "b", n)
                point(pool, "a2", m)
                pool.wait_ge(ctx_loaded, 16 * (n + 1))
                wait(pool, b_centred, n)
                apart(pool, passed)
                pool.tensor_copy(ctx_one[:, :, :, 0:DH], ctx_tok[:, :, :].rearrange("p t (h d) -> p t h d", h=H4)).then_inc(ctx_split, 1)
                for w in ("a3", "b0", "b1", "b2", "b3"):
                    point(pool, w, m)
                pool.wait_ge(b_centred, n + 1)
                pool.tensor_tensor(b_rstd[:, :], b_var[:, :], minus_half[:, :], ALU.pow).then_inc(b_rooted, 1)

            def route(pool, n):
                rooted(pool, "c", n)
                yield
                yield
                yield
                yield
                pool.wait_ge(routed, n + 1)
                gather(pool, n, 0)
                yield
                yield
                gather(pool, n, 1)

            def de(pool, n):
                rooted(pool, "d", n)
                yield
                yield
                yield
                yield
                rooted(pool, "e", n)
                yield
                yield
                yield
                yield

            def tail(pool, n):
                for w in POINTS:
                    point(pool, w, n)

            program(ab, route, de, start, tail)(pool)

        @block.tensor
        def _(pe):
            def turn(name, n, src):
                s = Slot(name, n)
                wait(pe, s.taken, s.before)
                for k in range(KC):
                    for t in range(TILES):
                        last = pe.transpose(s.bank[:, (k * TILES + t) * P:(k * TILES + t + 1) * P], src[:, t, k * P:(k + 1) * P], ident[:, :])
                last.then_inc(ps_full, 1)

            def by_token(name, n, xT, w):
                s = Slot(name, n)
                wait(pe, s.taken, s.before)
                for t in range(TILES):
                    for k in range(KC):
                        last = pe.matmul(s.bank[:, t * D:(t + 1) * D], xT[:, k, t * P:(t + 1) * P], w[:, k, 0:D], start=(k == 0), stop=(k == KC - 1))
                last.then_inc(ps_full, 1)

            def by_feature(name, n, xT, w, first=0):
                s = Slot(name, n)
                wait(pe, s.taken, s.before)
                for c in range(2):
                    for k in range(KC):
                        last = pe.matmul(s.bank[:, c * SEQ:(c + 1) * SEQ], w[:, k, (first + c) * P:(first + c + 1) * P], xT[:, k, :],
                                         start=(k == 0), stop=(k == KC - 1))
                last.then_inc(ps_full, 1)

            def copied(name, n):
                s = Slot(name, n)
                pe.wait_ge(s.taken, s.after)

            def ab(pe, n, m):
                pe.wait_ge(normed["a"], n + 1)
                turn("a_hT", n, h)
                copied("a_hT", n)
                pe.wait_ge(loaded["a"], 16 * LOADS["a"])
                by_token("a_q", n, hT, a_w[:, 0])
                by_token("a_k", n, hT, a_w[:, 1])
                by_feature("a_v", n, hT, a_w[:, 2])
                copied("a_q", n)
                copied("a_k", n)
                s = Slot("a_z", n)
                wait(pe, s.taken, s.before)
                for c in range(KC):
                    for t in range(TILES):
                        last = pe.matmul(s.bank[:, c * P:(c + 1) * P], a_k[:, t, c * P:(c + 1) * P], a_q[:, t, c * P:(c + 1) * P],
                                         start=(t == 0), stop=(t == TILES - 1))
                last.then_inc(ps_full, 1)
                copied("a_v", n)
                pe.wait_ge(a_probs, n + 1)
                s = Slot("a_o", n)
                wait(pe, s.taken, s.before)
                for c in range(KC):
                    last = pe.matmul(s.bank[:, c * SEQ:(c + 1) * SEQ], a_p[:, c, :], a_vT[:, c, :], start=True, stop=True)
                last.then_inc(ps_full, 1)
                copied("a_o", n)
                by_token("a_y", n, a_oT, a_w[:, 3])
                pe.wait_ge(ctx_loaded, 16 * (n + 1))
                turn("b_cT", n, ctx_tok)
                pe.wait_ge(normed["b"], n + 1)
                turn("b_hT", n, h)
                copied("b_cT", n)
                copied("b_hT", n)
                pe.wait_ge(loaded["b"], 16 * LOADS["b"])
                s = Slot("b_g", n)
                wait(pe, s.taken, s.before)
                for i in range(2):
                    for k in range(3 * KC):
                        src = hT if k < KC else ctxT
                        last = pe.matmul(s.bank[0:H4, i * SEQ:(i + 1) * SEQ], gate_w[:, k, i * H4:(i + 1) * H4], src[:, k % KC, :],
                                         start=(k == 0), stop=(k == 3 * KC - 1))
                last.then_inc(ps_full, 1)
                s = Slot("b_gt", n)
                wait(pe, s.taken, s.before)
                pe.wait_ge(gates_norm, n + 1)
                apart(pe, passed)
                for i, src in enumerate((g_a, g_norm)):
                    for t in range(TILES):
                        last = pe.transpose(s.bank[:, (i * TILES + t) * H4:(i * TILES + t + 1) * H4], src[:, t * P:(t + 1) * P], ident[0:H4, 0:H4])
                last.then_inc(ps_full, 1)
                for hd in range(H4):
                    s = Slot(f"b_m{hd}", n)
                    wait(pe, s.taken, s.before)
                    pe.matmul(s.bank[:, 0:SEQ], head_row[:, hd, :], g_top[:, :], start=True, stop=False)
                    pe.matmul(s.bank[:, SEQ:SEQ + P], head_row[:, hd, :], g_top[:, P:SEQ], start=False, stop=False)
                    pe.matmul(s.bank[:, 0:P], ident_bf[:, :], later[:, :], start=False, stop=False)
                    pe.matmul(s.bank[:, SEQ:SEQ + P], ident_bf[:, :], later[:, :], start=False, stop=True).then_inc(ps_full, 1)
                for hd in range(H4):
                    s = Slot(f"b_qk{hd}", n)
                    wait(pe, s.taken, s.before)
                    r = slice(DH * (hd % 2), DH * (hd % 2) + DH)
                    pe.matmul(s.bank[:, 0:SEQ], ctxT[r, hd // 2, 0:P], hT[r, hd // 2, :], start=True, stop=True)
                    pe.matmul(s.bank[:, SEQ:SEQ + P], ctxT[r, hd // 2, P:SEQ], hT[r, hd // 2, P:SEQ], start=True, stop=True).then_inc(ps_full, 1)
                pe.wait_ge(weighted, H4 * (n + 1))
                pe.wait_ge(ctx_split, n + 1)
                s = Slot("b_h0", n)
                wait(pe, s.taken, s.before)
                for hd in range(H4):
                    last = pe.matmul(s.bank[:, hd * (DH + 1):(hd + 1) * (DH + 1)], b_c[:, hd, 0:P], ctx_one[:, 0, hd, :], start=True, stop=True)
                last.then_inc(ps_full, 1)
                s = Slot("b_h1", n)
                wait(pe, s.taken, s.before)
                for hd in range(H4):
                    out = s.bank[:, hd * (DH + 1):(hd + 1) * (DH + 1)]
                    pe.matmul(out, b_c[:, hd, P:2 * P], ctx_one[:, 0, hd, :], start=True, stop=False)
                    last = pe.matmul(out, b_c[:, hd, 2 * P:3 * P], ctx_one[:, 1, hd, :], start=False, stop=True)
                last.then_inc(ps_full, 1)

            def route(pe, n):
                pe.wait_ge(normed["c"], n + 1)
                turn("c_hT", n, hc)
                copied("c_hT", n)
                pe.wait_ge(loaded["c"], 16 * LOADS["c"])
                yield
                by_feature("c_q0", n, hT, c_wq, 0)
                by_feature("c_q1", n, hT, c_wq, 2)
                copied("c_q0", n)
                copied("c_q1", n)
                yield
                for i in range(4):
                    t, par = i // 2, i % 2
                    s = Slot(f"c_s{i}", n)
                    wait(pe, s.taken, s.before)
                    r = slice(DH * par, DH * par + DH)
                    for j in range(4):
                        xy, pair_of = j // 2, j % 2
                        last = pe.matmul(s.bank[:, j * NK:(j + 1) * NK], c_qT[r, j, t * P:(t + 1) * P], c_keys[r, xy, pair_of, :], start=True, stop=True)
                    last.then_inc(ps_full, 1)
                yield
                yield
                for i in range(MC):
                    if i == MC // 2:
                        yield
                    s = Slot(f"c_m{i}", n)
                    wait(pe, s.taken, s.before)
                    for j, w in enumerate((c_wg, c_wu)):
                        for k in range(KC):
                            last = pe.matmul(s.bank[:, j * SEQ:(j + 1) * SEQ], w[:, k, i * P:(i + 1) * P], hT[:, k, :], start=(k == 0), stop=(k == KC - 1))
                    last.then_inc(ps_full, 1)
                yield
                copied(f"c_m{MC - 2}", n)
                copied(f"c_m{MC - 1}", n)
                for t in range(TILES):
                    s = Slot(f"c_y{t}", n)
                    wait(pe, s.taken, s.before)
                    for i in range(MC):
                        last = pe.matmul(s.bank[:, 0:D], mT[:, i, t * P:(t + 1) * P], c_wd[:, i, :], start=(i == 0), stop=(i == MC - 1))
                    last.then_inc(ps_full, 1)

            def de(pe, n):
                pe.wait_ge(normed["d"], n + 1)
                turn("d_hT", n, h)
                yield
                copied("d_hT", n)
                pe.wait_ge(loaded["d"], 16 * LOADS["d"])
                by_feature("d_q", n, hT_de, d_w[:, 0])
                by_feature("d_k", n, hT_de, d_w[:, 1])
                by_token("d_v", n, hT_de, d_w[:, 2])
                yield
                copied("d_q", n)
                copied("d_k", n)
                s = Slot("d_s", n)
                wait(pe, s.taken, s.before)
                for k in range(KC):
                    pe.matmul(s.bank[:, 0:P], d_qT[:, k, 0:P], d_kT[:, k, 0:P], start=(k == 0), stop=False)
                for k in range(KC):
                    pe.matmul(s.bank[:, P:3 * P], d_qT[:, k, P:SEQ], d_kT[:, k, :], start=False, stop=False)
                pe.matmul(s.bank[:, 0:P], ident_bf[:, :], future[:, :], start=False, stop=False)
                pe.matmul(s.bank[:, 2 * P:3 * P], ident_bf[:, :], future[:, :], start=False, stop=True).then_inc(ps_full, 1)
                yield
                s = Slot("d_pT", n)
                wait(pe, s.taken, s.before)
                pe.wait_ge(d_exped, n + 1)
                for m in range(3):
                    last = pe.transpose(s.bank[:, m * P:(m + 1) * P], d_p[:, m * P:(m + 1) * P], ident[:, :])
                last.then_inc(ps_full, 1)
                copied("d_v", n)
                copied("d_pT", n)
                s = Slot("d_o", n)
                wait(pe, s.taken, s.before)
                pe.matmul(s.bank[:, 0:D], d_pT[:, 0:P], d_v[:, 0, :], start=True, stop=True)
                pe.matmul(s.bank[:, D:2 * D], d_pT[:, P:2 * P], d_v[:, 0, :], start=True, stop=False)
                pe.matmul(s.bank[:, D:2 * D], d_pT[:, 2 * P:3 * P], d_v[:, 1, :], start=False, stop=True).then_inc(ps_full, 1)
                yield
                pe.wait_ge(normed["e"], n + 1)
                turn("e_hT", n, h)
                pe.wait_ge(ctx_e_loaded, 16 * (n + 1))
                turn("e_cT", n, ctx_e)
                yield
                copied("e_cT", n)
                pe.wait_ge(loaded["e"], 16 * LOADS["e"])
                by_feature("e_k", n, ctxT_e, e_wk)
                by_token("e_v", n, ctxT_e, e_wv)
                pe.wait_ge(e_pooled, n + 1)
                s = Slot("e_q", n)
                wait(pe, s.taken, s.before)
                for c in range(8):
                    for k in range(KC):
                        last = pe.matmul(s.bank[:, c * NB:(c + 1) * NB], e_wq[:, k, c * P:(c + 1) * P], pooled[:, k, :], start=(k == 0), stop=(k == KC - 1))
                last.then_inc(ps_full, 1)
                yield
                copied("e_q", n)
                copied("e_k", n)
                for i in range(2):
                    s = Slot(f"e_s{i}", n)
                    wait(pe, s.taken, s.before)
                    apart(pe, passed)
                    r = slice(DH * i, DH * i + DH)
                    for half in range(2):
                        last = pe.matmul(s.bank[0:4 * NB, half * SEQ:(half + 1) * SEQ], e_qT[r, half, :], e_kT[r, half, :], start=True, stop=True)
                    last.then_inc(ps_full, 1)
                yield
                s = Slot("e_pT", n)
                wait(pe, s.taken, s.before)
                pe.wait_ge(e_normed, n + 1)
                apart(pe, passed)
                for t in range(TILES):
                    for g in range(H4):
                        last = pe.transpose(s.bank[:, (t * H4 + g) * 4 * NB:(t * H4 + g + 1) * 4 * NB], e_p[:, g, t * P:(t + 1) * P], ident[0:4 * NB, 0:4 * NB])
                last.then_inc(ps_full, 1)
                copied("e_v", n)
                copied("e_pT", n)
                s = Slot("e_o", n)
                wait(pe, s.taken, s.before)
                for j, g in enumerate((0, 2, 1, 3)):
                    for t in range(TILES):
                        last = pe.matmul(s.bank[DH * (g % 2):DH * (g % 2) + DH, (g // 2) * 4 * NB:(g // 2 + 1) * 4 * NB], e_v[:, t, g * DH:(g + 1) * DH], e_pT[:, t, j, :],
                                         start=(t == 0), stop=(t == TILES - 1))
                last.then_inc(ps_full, 1)
                yield
                copied("e_o", n)
                s = Slot("e_y", n)
                wait(pe, s.taken, s.before)
                for c in range(8):
                    last = pe.matmul(s.bank[0:NB, 0:D], e_o[:, c * NB:(c + 1) * NB], e_wo[:, c, :], start=(c == 0), stop=(c == 7))
                last.then_inc(ps_full, 1)
                copied("e_y", n)
                s = Slot("e_u", n)
                wait(pe, s.taken, s.before)
                for t in range(TILES):
                    last = pe.matmul(s.bank[:, t * D:(t + 1) * D], unpool[:, t * P:(t + 1) * P], e_y[:, :], start=True, stop=True)
                last.then_inc(ps_full, 1)

            def start(pe):
                for b in range(BANKS):
                    pe.sem_inc(ps_taken[b], len(range(b, NDE, BANKS)))
                pe.sem_inc(ps_full, NDE)
                pe.wait_ge(consts_set, 1)

            program(ab, route, de, start, lambda pe, n: None)(pe)

        @block.scalar
        def _(act):
            F = nc.scalar.activation

            def copy(name, n, dst, width=512, parts=P):
                s = Slot(name, n)
                act.wait_ge(ps_full, s.full)
                F(dst, s.bank[0:parts, 0:width], ACT.Copy).then_inc(s.taken, 1)

            def point(act, where, m):
                if m is not None:
                    for g in POINTS[where]:
                        act.wait_ge(dotted, GROUPS * m + g + 1)
                        F(expd[:, g % 2, :], low[:, g % 2, :], ACT.Exp, scale=-1.0).then_inc(dots_exped, 1)

            def ab(act, n, m):
                copy("a_hT", n, flat(hT[:, :, :]))
                point(act, "a0", m)
                copy("a_q", n, flat(a_q[:, :, :]))
                copy("a_v", n, flat(a_vT[:, :, :]))
                act.wait_ge(a_masked, n + 1)
                for c in range(KC):
                    last = F(a_e[:, c, :], a_s[:, c, :], ACT.Exp, bias=a_neg[:, c:c + 1], accum_out=a_sum[:, c:c + 1])
                last.then_inc(a_exped, 1)
                point(act, "a1", m)
                copy("a_o", n, flat(a_oT[:, :, :]))
                point(act, "a2", m)
                point(act, "a3", m)
                copy("b_cT", n, flat(ctxT[:, :, :]))
                copy("b_hT", n, flat(hT[:, :, :]))
                point(act, "b0", m)
                act.wait_ge(gates_biased, n + 1)
                chain = Chain(act, act_b, n, 2)
                chain.link(F(g_abs[:, :], g_f[:, :], ACT.Abs))
                chain.link(F(g_exp[:, :], g_abs[:, :], ACT.Exp, scale=-1.0))
                chain.close()
                F(g_ln[:, :], g_exp[:, :], ACT.Ln, bias=1.0).then_inc(gates_ln, 1)
                point(act, "b1", m)
                act.wait_ge(gates_top, n + 1)
                F(g_norm[:, :], g_low[:, :], ACT.Exp, scale=-1.0).then_inc(gates_norm, 1)
                point(act, "b2", m)
                for hd in range(H4):
                    s = Slot(f"b_m{hd}", n)
                    act.wait_ge(ps_full, s.full)
                    if hd == 0:
                        st = Slot("b_gt", n)
                        act.wait_ge(st.taken, st.after)
                    if hd >= 2:
                        act.wait_ge(weighted, H4 * n + hd - 1)
                    F(decay[:, hd % 2, 0:SEQ], s.bank[:, 0:SEQ], ACT.Exp, scale=-1.0, bias=gT[:, 0, 0, hd:hd + 1])
                    F(decay[:, hd % 2, SEQ:SEQ + P], s.bank[:, SEQ:SEQ + P], ACT.Exp, scale=-1.0, bias=gT[:, 0, 1, hd:hd + 1]).then_inc(s.taken, 1)
                point(act, "b3", m)

            def route(act, n):
                copy("c_hT", n, flat(hT[:, :, :]))
                yield
                copy("c_q0", n, flat(c_qT[:, 0:2, :]))
                copy("c_q1", n, flat(c_qT[:, 2:4, :]))
                yield
                yield
                act.wait_ge(sm_ready, n + 1)
                F(sm_e[:, :, :], sm_d[:, :, :], ACT.Exp).then_inc(sm_exped, 1)
                yield
                for i in range(MC):
                    if i == MC // 2:
                        yield
                    s = Slot(f"c_m{i}", n)
                    act.wait_ge(ps_full, s.full)
                    if i >= 2:
                        before = Slot(f"c_m{i - 2}", n)
                        act.wait_ge(before.taken, before.after)
                    F(m_gate[:, i % 2, :], s.bank[:, 0:SEQ], ACT.Silu).then_inc(m_silu, 1)
                yield

            def de(act, n):
                copy("d_hT", n, flat(hT_de[:, :, :]))
                yield
                copy("d_q", n, flat(d_qT[:, :, :]))
                copy("d_v", n, flat(d_v[:, :, :]))
                yield
                act.wait_ge(d_topped, n + 1)
                s = Slot("d_s", n)
                F(d_p[:, 0:P], s.bank[:, 0:P], ACT.Exp, bias=d_neg[:, 0:1], scale=1.0 / 16.0, accum_out=d_sum[:, 0:1])
                F(d_p[:, P:3 * P], s.bank[:, P:3 * P], ACT.Exp, bias=d_neg[:, 1:2], scale=1.0 / 16.0, accum_out=d_sum[:, 1:2]).then_inc(d_exped, 1)
                act.wait_ge(d_exped, n + 1)
                act.sem_inc(s.taken, 1)
                yield
                copy("d_pT", n, d_pT[:, :], 3 * P)
                yield
                copy("e_cT", n, flat(ctxT_e[:, :, :]))
                yield
                copy("e_k", n, flat(e_kT[:, :, :]))
                copy("e_v", n, flat(e_v[:, :, :]))
                copy("e_q", n, flat(e_qT[:, :, :]), 8 * NB)
                yield
                act.wait_ge(e_topped, n + 1)
                for g in range(H4):
                    last = F(e_p[:, g, :], e_s[:, g, :], ACT.Exp, bias=e_neg[:, g:g + 1], accum_out=e_sum[:, g:g + 1])
                last.then_inc(e_exped, 1)
                yield
                copy("e_pT", n, flat(proj2[:, :, :]))
                copy("e_o", n, e_o[:, :], 2 * 4 * NB)
                yield
                copy("e_y", n, e_y[:, :], D, NB)

            def tail(act, n):
                for w in POINTS:
                    point(act, w, n)

            def start(act):
                act.wait_ge(consts_set, 1)

            program(ab, route, de, start, tail)(act)

        @block.vector
        def _(dve):
            V = nc.vector

            def copy(name, n, dst, width=512, parts=P):
                s = Slot(name, n)
                dve.wait_ge(ps_full, s.full)
                V.tensor_copy(dst, s.bank[0:parts, 0:width]).then_inc(s.taken, 1)

            def norm(dve, s, n, dst, chain):
                bn, mv, var_eps, rstd = norm_bufs[s in "de"]
                apart(dve, passed)
                for t in range(TILES):
                    last = V.bn_stats(bn[:, t, :], xall[:, n, t, :])
                chain.link(last)
                apart(dve, passed)
                for t in range(TILES):
                    last = V.bn_aggr(mv[:, t, :], bn[:, t, :])
                chain.link(last)
                V.tensor_scalar(var_eps[:, :], mv[:, :, 1], 1e-5, None, ALU.add).then_inc(stats[s], 1)
                dve.wait_ge(rstds[s], n + 1)
                for t in range(TILES):
                    last = V.tensor_scalar(dst[:, t, :], xall[:, n, t, :], mv[:, t, 0:1], rstd[:, t:t + 1], ALU.subtract, ALU.mult)
                last.then_inc(normed[s], 1)

            def dot(n, g):
                chain = Chain(dve, dve_sum, SUM_STEPS * n + (4 + TOPK) * g, 1)
                dve.wait_ge(gathered[g % RG], TOPK * 16 * (GROUPS // RG * n + g // RG + 1))
                for k in range(TOPK):
                    last = V.tensor_tensor_reduce(rows[:, g % RG, k, 0:D], hc[:, g // H4, :], rows[:, g % RG, k, 0:D], 1.0, 0.0, ALU.mult, ALU.add, dots[:, g % 2, k:k + 1])
                chain.link(last)
                V.tensor_scalar(low[:, g % 2, :], dots[:, g % 2, :], -80.0, None, ALU.max).then_inc(dotted, 1)

            def add_up(n, g):
                chain = Chain(dve, dve_sum, SUM_STEPS * n + (4 + TOPK) * g + 1, 1)
                dve.wait_ge(dots_exped, GROUPS * n + g + 1)
                b = g % 2
                chain.link(V.tensor_scalar(sig[:, b, :], expd[:, b, :], 1.0, None, ALU.add))
                chain.link(V.reciprocal(silu[:, b, :], sig[:, b, :]))
                chain.link(V.tensor_tensor(sig[:, b, :], silu[:, b, :], dots[:, b, :], ALU.mult))
                chain.link(V.tensor_tensor(coef[:, b, :], sig[:, b, :], weight[:, g, :], ALU.mult))
                x = xall[:, n, g // H4, :]
                for k in range(TOPK):
                    add = V.scalar_tensor_tensor(x, rows[:, g % RG, k, D:2 * D], coef[:, b, k:k + 1], x, ALU.mult, ALU.add)
                    if k < TOPK - 1:
                        chain.link(add)
                add.then_inc(rows_used, 1)
                dve.wait_ge(rows_used, GROUPS * n + g + 1)

            def point(where, m):
                if m is not None:
                    for g in POINTS[where]:
                        dot(m, g)
                        add_up(m, g)

            def ab(dve, n, m):
                chain = Chain(dve, dve_ab, n, DVE_AB)
                norm(dve, "a", n, h, chain)
                point("a0", m)
                copy("a_k", n, flat(a_k[:, :, :]))
                s = Slot("a_z", n)
                dve.wait_ge(ps_full, s.full)
                V.scalar_tensor_tensor(flat(a_s[:, :, :]), s.bank[:, 0:SEQ], 0.25, flat(block_mask[:, :, :]), ALU.mult, ALU.add).then_inc(s.taken, 1)
                dve.wait_ge(s.taken, s.after)
                chain.link(V.tensor_reduce(a_top[:, :], a_s[:, :, :], AX, ALU.max))
                V.tensor_scalar(a_neg[:, :], a_top[:, :], -1.0, None, ALU.mult).then_inc(a_masked, 1)
                point("a1", m)
                dve.wait_ge(a_exped, n + 1)
                chain.link(V.reciprocal(a_inv[:, :], a_sum[:, :]))
                V.tensor_tensor(a_p[:, :, :], a_e[:, :, :], a_inv[:, :].rearrange("p (c a) -> p c a", a=1).broadcast_to([P, KC, P]), ALU.mult).then_inc(a_probs, 1)
                point("a2", m)
                s = Slot("a_y", n)
                dve.wait_ge(ps_full, s.full)
                x = xall[:, n, :, :]
                V.tensor_tensor(x, s.bank[:, :].rearrange("p (t d) -> p t d", t=TILES), x, ALU.add).then_inc(s.taken, 1)
                dve.wait_ge(s.taken, s.after)
                norm(dve, "b", n, h, chain)
                point("a3", m)
                s = Slot("b_g", n)
                dve.wait_ge(ps_full, s.full)
                V.tensor_scalar(g_in[:, :], s.bank[0:H4, 0:SEQ], gate_b[:, 0:1], None, ALU.add)
                V.tensor_scalar(g_f[:, :], s.bank[0:H4, SEQ:2 * SEQ], gate_b[:, 1:2], None, ALU.add).then_inc(gates_biased, 1)
                dve.wait_ge(gates_biased, n + 1)
                dve.sem_inc(s.taken, 1)
                point("b0", m)
                dve.wait_ge(gates_ln, n + 1)
                chain.link(V.scalar_tensor_tensor(g_log[:, :], g_f[:, :], 0.0, g_ln[:, :], ALU.min, ALU.subtract))
                chain.link(V.tensor_tensor_scan(g_cs[:, :], g_log[:, :], zeros[:, :], 0.0, ALU.add, ALU.add))
                V.tensor_copy(g_a[:, 0:1], g_in[:, 0:1])
                chain.link(V.tensor_tensor(g_a[:, 1:SEQ], g_in[:, 1:SEQ], g_cs[:, 0:SEQ - 1], ALU.subtract))
                chain.link(V.tensor_tensor_scan(g_top[:, :], g_a[:, :], zeros[:, :], -BIG, ALU.max, ALU.add))
                V.tensor_tensor(g_low[:, :], g_cs[:, :], g_top[:, :], ALU.add).then_inc(gates_top, 1)
                point("b1", m)
                copy("b_gt", n, gT[:, :, :, :].rearrange("p i t h -> p (i t h)"), 16)
                point("b2", m)
                for hd in range(H4):
                    s = Slot(f"b_qk{hd}", n)
                    dve.wait_ge(ps_full, s.full)
                    st = Slot(f"b_m{hd}", n)
                    dve.wait_ge(st.taken, st.after)
                    V.scalar_tensor_tensor(b_c[:, hd, :], s.bank[:, 0:3 * P], SCALE, decay[:, hd % 2, :], ALU.mult, ALU.mult).then_inc(weighted, 1)
                    dve.wait_ge(weighted, H4 * n + hd + 1)
                    dve.sem_inc(s.taken, 1)
                point("b3", m)
                inv, mean, var, rs = b_inv, b_mean, b_var, b_rstd
                for t in range(TILES):
                    s = Slot(f"b_h{t}", n)
                    dve.wait_ge(ps_full, s.full)
                    heads = s.bank[:, 0:H4 * (DH + 1)].rearrange("p (h d) -> p h d", h=H4)
                    th = slice(t * H4, (t + 1) * H4)
                    chain.link(V.tensor_scalar(b_norm[:, th], heads[:, :, DH], -1.0, None, ALU.mult))
                    chain.link(V.tensor_tensor(inv[:, th], b_norm[:, th], heads[:, :, DH], ALU.max))
                    chain.link(V.tensor_tensor(b_norm[:, th], inv[:, th], gT[:, 1, t, :], ALU.max))
                    chain.link(V.tensor_scalar(inv[:, th], b_norm[:, th], 1e-8, None, ALU.add))
                    chain.link(V.reciprocal(inv[:, th], inv[:, th]))
                    V.tensor_tensor(b_u[:, th, :], heads[:, :, 0:DH], inv[:, th].rearrange("p (h a) -> p h a", a=1).broadcast_to([P, H4, DH]), ALU.mult).then_inc(s.taken, 1)
                    dve.wait_ge(s.taken, s.after)

                def per_head(x):
                    return x[:, :].rearrange("p (h a) -> p h a", a=1).broadcast_to([P, TILES * H4, DH])

                chain.link(V.tensor_reduce(var[:, :], b_u[:, :, :], AX, ALU.add))
                chain.link(V.tensor_scalar(mean[:, :], var[:, :], 1.0 / DH, None, ALU.mult))
                chain.link(V.tensor_tensor(b_u[:, :, :], b_u[:, :, :], per_head(mean), ALU.subtract))
                chain.link(V.tensor_tensor(b_sq[:, :, :], b_u[:, :, :], b_u[:, :, :], ALU.mult))
                chain.link(V.tensor_reduce(mean[:, :], b_sq[:, :, :], AX, ALU.add))
                V.tensor_scalar(var[:, :], mean[:, :], 1.0 / DH, 1e-5, ALU.mult, ALU.add).then_inc(b_centred, 1)
                dve.wait_ge(b_rooted, n + 1)
                chain.link(V.tensor_tensor(b_u[:, :, :], b_u[:, :, :], per_head(rs), ALU.mult))
                chain.link(V.tensor_tensor(b_sq[:, :, :].rearrange("p (t h) d -> p t (h d)", t=TILES), b_u[:, :, :].rearrange("p (t h) d -> p t (h d)", t=TILES),
                                           out_gain[:, :].rearrange("p (a d) -> p a d", a=1).broadcast_to([P, TILES, D]), ALU.mult))
                chain.link(V.tensor_tensor(x, b_sq[:, :, :].rearrange("p (t h) d -> p t (h d)", t=TILES), x, ALU.add))
                chain.close()

            def route(dve, n):
                chain = Chain(dve, dve_c, n, DVE_C)
                norm(dve, "c", n, hc, chain)
                yield
                yield
                for i in range(4):
                    t, par = i // 2, i % 2
                    s = Slot(f"c_s{i}", n)
                    dve.wait_ge(ps_full, s.full)
                    apart(dve, passed)
                    for j in range(4):
                        last = V.max(best[:, j // 2, t * H4 + 2 * (j % 2) + par, :], s.bank[:, j * NK:(j + 1) * NK])
                    chain.link(last)
                    apart(dve, passed)
                    for j in range(4):
                        at = t * H4 + 2 * (j % 2) + par
                        last = V.max_index(besti[:, j // 2, at, :], best[:, j // 2, at, :], s.bank[:, j * NK:(j + 1) * NK])
                    last.then_inc(s.taken, 1)
                yield
                dve.wait_ge(s.taken, s.after)
                V.tensor_copy(bestf[:, :, :, :], besti[:, :, :, :])
                chain.link(V.tensor_tensor(pair[:, :, :, :], best[:, 0].rearrange("p g (i a) -> p g i a", a=1).broadcast_to([P, GROUPS, TOPK, TOPK]),
                                           best[:, 1].rearrange("p g (a j) -> p g a j", a=1).broadcast_to([P, GROUPS, TOPK, TOPK]), ALU.add))
                apart(dve, passed)
                for g in range(GROUPS):
                    last = V.max(score[:, g, :], pair[:, g, :, :].rearrange("p i j -> p (i j)"))
                chain.link(last)
                apart(dve, passed)
                for g in range(GROUPS):
                    last = V.max_index(pairi[:, g, :], score[:, g, :], pair[:, g, :, :].rearrange("p i j -> p (i j)"))
                chain.link(last)
                V.tensor_scalar(pos[:, 0, :], pairi[:, :, :].rearrange("p g k -> p (g k)"), 3, None, ALU.logical_shift_right)
                chain.link(V.tensor_scalar(pos[:, 1, :], pairi[:, :, :].rearrange("p g k -> p (g k)"), 7, None, ALU.bitwise_and))
                chain.link(V.tensor_copy(posf[:, :, :], pos[:, :, :]))
                for xy in range(2):
                    at = posf[:, xy, :].rearrange("p (k a) -> p k a", a=1).broadcast_to([P, GROUPS * TOPK, TOPK])
                    place = iota8[:, :].rearrange("p (a i) -> p a i", a=1).broadcast_to([P, GROUPS * TOPK, TOPK])
                    chain.link(V.tensor_tensor(pick[:, :, :], at, place, ALU.is_equal))
                    by_group = pick[:, :, :].rearrange("p (g k) i -> p g k i", g=GROUPS)
                    chain.link(V.tensor_tensor(by_group, by_group, bestf[:, xy].rearrange("p g (a i) -> p g a i", a=1).broadcast_to([P, GROUPS, TOPK, TOPK]), ALU.mult))
                    chain.link(V.tensor_reduce(picked[:, xy, :], pick[:, :, :], AX, ALU.add))
                chain.link(V.scalar_tensor_tensor(expertf[:, :], picked[:, 0, :], float(NK), picked[:, 1, :], ALU.mult, ALU.add))
                chain.link(V.tensor_scalar(expertf[:, :], expertf[:, :], float(EXPERTS - 1), None, ALU.min))
                V.tensor_copy(expert[:, :], expertf[:, :]).then_inc(routed, 1)
                V.tensor_tensor(sm_d[:, :, :], score[:, :, :], score[:, :, 0:1].broadcast_to([P, GROUPS, TOPK]), ALU.subtract).then_inc(sm_ready, 1)
                yield
                for i in range(MC):
                    if i == MC // 2:
                        yield
                    s = Slot(f"c_m{i}", n)
                    dve.wait_ge(m_silu, MC * n + i + 1)
                    V.tensor_tensor(mT[:, i, :], s.bank[:, SEQ:2 * SEQ], m_gate[:, i % 2, :], ALU.mult).then_inc(s.taken, 1)
                yield
                dve.wait_ge(sm_exped, n + 1)
                chain.link(V.tensor_reduce(sm_sum[:, :], sm_e[:, :, :], AX, ALU.add))
                chain.link(V.reciprocal(sm_inv[:, :], sm_sum[:, :]))
                chain.link(V.tensor_tensor(weight[:, :, :], sm_e[:, :, :], sm_inv[:, :].rearrange("p (g a) -> p g a", a=1).broadcast_to([P, GROUPS, TOPK]), ALU.mult))
                for t in range(TILES):
                    s = Slot(f"c_y{t}", n)
                    dve.wait_ge(ps_full, s.full)
                    x = xall[:, n, t, :]
                    V.tensor_tensor(x, s.bank[:, 0:D], x, ALU.add).then_inc(s.taken, 1)
                    dve.wait_ge(s.taken, s.after)
                chain.close()

            def de(dve, n):
                chain = Chain(dve, dve_de, n, DVE_DE)
                norm(dve, "d", n, h, chain)
                yield
                copy("d_k", n, flat(d_kT[:, :, :]))
                yield
                s = Slot("d_s", n)
                dve.wait_ge(ps_full, s.full)
                V.tensor_reduce(d_top[:, 0:1], s.bank[:, 0:P], AX, ALU.max)
                chain.link(V.tensor_reduce(d_top[:, 1:2], s.bank[:, P:3 * P], AX, ALU.max))
                V.tensor_scalar(d_neg[:, :], d_top[:, :], -1.0 / 16.0, None, ALU.mult).then_inc(d_topped, 1)
                dve.wait_ge(d_exped, n + 1)
                chain.link(V.reciprocal(d_inv[:, :], d_sum[:, :]))
                yield
                s = Slot("d_o", n)
                dve.wait_ge(ps_full, s.full)
                for t in range(TILES):
                    x = xall[:, n, t, :]
                    last = V.scalar_tensor_tensor(x, s.bank[:, t * D:(t + 1) * D], d_inv[:, t:t + 1], x, ALU.mult, ALU.add)
                last.then_inc(s.taken, 1)
                dve.wait_ge(s.taken, s.after)
                yield
                norm(dve, "e", n, h, chain)
                s = Slot("e_hT", n)
                dve.wait_ge(ps_full, s.full)
                V.tensor_reduce(flat(pooled[:, :, :]), s.bank[:, :].rearrange("p (kb j) -> p kb j", j=BLK), AX, ALU.add).then_inc(e_pooled, 1)
                dve.wait_ge(e_pooled, n + 1)
                dve.sem_inc(s.taken, 1)
                yield
                dve.wait_ge(mask_loaded, 16 * (n + 1))
                chain.link(V.tensor_scalar(keep[:, :], mask_i[:, :], 0.0, None, ALU.not_equal))
                chain.link(V.tensor_scalar(shut[:, :], keep[:, :], 1.0, 1.0e9, ALU.subtract, ALU.mult))
                chain.link(V.tensor_scalar(keep[:, :], keep[:, :], SCALE / BLK, None, ALU.mult))

                def each(x, k):
                    return x[:, :].rearrange("p (a n) -> p a n", a=1).broadcast_to([4 * NB, k, SEQ])

                yield
                for i in range(2):
                    s = Slot(f"e_s{i}", n)
                    dve.wait_ge(ps_full, s.full)
                    V.tensor_tensor(e_s[:, 2 * i:2 * i + 2, :], s.bank[0:4 * NB, :].rearrange("p (g n) -> p g n", g=2), each(keep, 2), ALU.mult).then_inc(s.taken, 1)
                    dve.wait_ge(s.taken, s.after)
                chain.link(V.tensor_tensor(e_s[:, :, :], e_s[:, :, :], each(shut, H4), ALU.add))
                chain.link(V.tensor_reduce(e_top[:, :], e_s[:, :, :], AX, ALU.max))
                V.tensor_scalar(e_neg[:, :], e_top[:, :], -1.0, None, ALU.mult).then_inc(e_topped, 1)
                dve.wait_ge(e_exped, n + 1)
                chain.link(V.reciprocal(e_inv[:, :], e_sum[:, :]))
                V.tensor_tensor(e_p[:, :, :], e_p[:, :, :], e_inv[:, :].rearrange("p (g a) -> p g a", a=1).broadcast_to([4 * NB, H4, SEQ]), ALU.mult).then_inc(e_normed, 1)
                yield
                yield
                s = Slot("e_u", n)
                dve.wait_ge(ps_full, s.full)
                x = xall[:, n, :, :]
                V.tensor_tensor(x, s.bank[:, :].rearrange("p (t d) -> p t d", t=TILES), x, ALU.add).then_inc(e_added, 1)
                dve.wait_ge(e_added, n + 1)
                dve.sem_inc(s.taken, 1)
                chain.close()

            def start(dve):
                dve.wait_ge(consts_set, 1)
                dve.wait_ge(loaded["b"], 16 * LOADS["b"])
                V.tensor_scalar(out_gain[:, :], out_gain[:, :], 1.0, None, ALU.add).then_inc(gain_set, 1)
                dve.wait_ge(gain_set, 1)

            def tail(dve, n):
                for w in POINTS:
                    point(w, n)

            DVE_AB, DVE_C, DVE_DE = 28, 22, 12
            SUM_STEPS = GROUPS * (4 + TOPK)
            program(ab, route, de, start, tail)(dve)


def local_layers(nc, xall, ident, ident_bf, passed, dram, layers, out_dram):
    H, DH = 16, 64
    INNER = H * DH
    HP = H // 2
    FF = dram["L1_ffn_W2"].shape[1]
    FC = (FF + P - 1) // P
    FR = FF - (FC - 1) * P
    STEPS = layers * BATCH
    KW = 192

    PHASE = {"scores": "attn", "turn": "attn", "values": "attn", "group": "attn", "o_turn": "attn", "wo": "attn", "res_a": "attn",
             "xs": "x", "rope": "front", "project": "front", "rotate": "front", "qk_turn": "front",
             "ln_stats": "ffn", "ln_apply": "ffn", "xn": "ffn", "w1": "ffn", "halves": "ffn", "gelu": "ffn", "gates": "ffn",
             "w2": "out", "res_f": "out"}
    AHEAD = {"x": 2, "attn": 0, "front": 1, "ffn": -1, "out": -2}
    PROJ = [(t, w, c) for t in range(TILES) for w in range(3) for c in range(2)]
    QK = [x for x in PROJ if x[1] < 2]
    PROJ_AT = [0, 1, 2, 4, 5, 6, 7, 8, 11, 12, 13, 14]
    TURN_AT = [3, 5, 6, 7, 10, 11, 13, 15]
    LN_AT, XN_AT = (3, 4), 6
    W1_AT = [7, 8, 10, 12, 14, 15]
    W2_AT = [1, 2]
    STEP = []
    for i in range(H + 3):
        if i < H and i % 2 == 0:
            STEP += [("scores", i), ("scores", i + 1)]
        if i == 0:
            STEP.append(("rope", 0))
        if i in PROJ_AT:
            STEP.append(("project", PROJ_AT.index(i)))
        if i >= 8 and i % 4 == 0:
            STEP.append(("o_turn", i // 4 - 2))
        if 2 <= i < H + 2:
            STEP.append(("turn", i - 2))
        if i in PROJ_AT and PROJ[PROJ_AT.index(i)] in QK:
            STEP.append(("rotate", QK.index(PROJ[PROJ_AT.index(i)])))
        if i in W2_AT:
            STEP.append(("w2", W2_AT.index(i)))
        if i == LN_AT[0]:
            STEP.append(("ln_stats", 0))
        if i == W2_AT[1] + 1:
            STEP.append(("res_f", 0))
        if i == LN_AT[1]:
            STEP.append(("ln_apply", 0))
        if i == XN_AT:
            STEP.append(("xn", 0))
        if i in TURN_AT:
            STEP.append(("qk_turn", TURN_AT.index(i)))
        if i in W1_AT:
            STEP.append(("w1", W1_AT.index(i)))
        if i >= 3:
            STEP.append(("values", i - 3))
        if i in W1_AT:
            STEP.append(("halves", W1_AT.index(i)))
        if i == H + 1:
            STEP.append(("gelu", 0))
        if i >= 6 and i % 4 == 2:
            STEP.append(("group", i // 4 - 1))
    STEP += [("wo", 0), ("xs", 0), ("o_turn", 3), ("wo", 1), ("res_a", 0), ("gates", 0)]
    TP_EVENTS = [x for x in STEP if x[0] in ("xs", "qk_turn", "turn", "o_turn", "xn")]
    PJ_EVENTS = [x for x in STEP if x[0] in ("project", "w1")]
    TP, PJ = len(TP_EVENTS), len(PJ_EVENTS)
    assert TP % 2 == 0 and PJ % 2 == 0 and STEPS % 2 == 0

    ctx = ExitStack()
    with ctx:
        def sb(name, shape, dt=F32):
            return ctx.enter_context(nc.sbuf_tensor("l_" + name, shape, dt))

        def sem(name):
            return ctx.enter_context(nc.semaphore("l_" + name))

        w_qkv = sb("w_qkv", [P, KC, 3 * INNER])
        w_o = sb("w_o", [P, INNER // P, D])
        w_1 = sb("w_1", [P, KC, 2 * FF])
        w_2 = sb("w_2", [P, FC, D])
        ff_cols = sb("ff_cols", [P, 2 * FC + 2 * KC])
        b1 = ff_cols[:, 0:2 * FC].rearrange("p (s c) -> p s c", s=2)
        ln_g, ln_b = ff_cols[:, 2 * FC:2 * FC + KC], ff_cols[:, 2 * FC + KC:]
        b2 = sb("b_2", [1, D])
        qk_gain = sb("qk_gain", [P, 2, 2, DH])
        rope_base = sb("rope_0", [P, 2, 2, TILES, DH])
        rope = sb("rope", [P, 2, 2, TILES, DH])
        band = sb("band", [P, 2 * KW], BF16)
        ones = sb("ones_row", [1, P])
        stream = sb("stream", [P, BATCH, TILES, D])
        ALLT = BATCH * TILES
        all_bn = sb("all_bn", [P, ALLT, 6])
        all_mv = sb("all_mv", [P, ALLT, 2])
        all_var = sb("all_var", [P, ALLT])
        all_half = sb("all_half", [P, ALLT])
        all_rstd = sb("all_rstd", [P, ALLT])
        xs = sb("xs", [P, TILES, D])
        xT = sb("xT", [P, KC, SEQ])
        qk_raw = sb("qk_raw", [P, 2, 512])
        qk_sq = sb("qk_sq", [P, 2, 512])
        qk_cos = sb("qk_cos", [P, 2, 512])
        qk_sin = sb("qk_sin", [P, 2, 512])
        qk_rot = sb("qk_rot", [P, 2, 512])
        ss = sb("ss", [P, 2, 8])
        ssm = sb("ssm", [P, 2, 8])
        r_q = sb("r_q", [P, 2, TILES, H])
        r_k = sb("r_k", [P, 2, 8])
        minus_half = sb("minus_half", [P, 8])
        qT = sb("qT", [P, 2, HP, SEQ])
        kT = sb("kT", [P, 2, HP, SEQ])
        v = sb("v", [P, 2, TILES, INNER])
        top = sb("top", [P, 2, TILES])
        neg_top = sb("neg_top", [P, 2, TILES])
        p_sum = sb("p_sum", [P, H, TILES])
        p_inv = sb("p_inv", [P, 4, TILES])
        probs = sb("probs", [P, 4, 3 * P])
        pT = sb("pT", [P, 2, 3, P])
        o_tok = sb("o_tok", [P, TILES, INNER])
        oT = sb("oT", [P, INNER // P, SEQ])
        xf = sb("xf", [P, TILES, D])
        xn = sb("xn", [P, TILES, D])
        xnT = sb("xnT", [P, KC, SEQ])
        bn = sb("bn", [P, TILES, 6])
        mv = sb("mv", [P, TILES, 2])
        var_eps = sb("var_eps", [P, TILES])
        rstd = sb("rstd", [P, TILES])
        gate = sb("gate", [P, FC, SEQ])
        hT = sb("hT", [P, FC, SEQ])

        tp = [ctx.enter_context(nc.psum_tensor(f"tp{i}", [P, 512], F32)) for i in range(2)]
        pj = [ctx.enter_context(nc.psum_tensor(f"pj{i}", [P, 512], F32)) for i in range(2)]
        sc = [ctx.enter_context(nc.psum_tensor(f"sc{i}", [P, 512], F32)) for i in range(2)]
        o_ps = ctx.enter_context(nc.psum_tensor("o_ps", [P, 512], F32))
        y_ps = ctx.enter_context(nc.psum_tensor("y_ps", [P, TILES, D], F32))

        const_loaded, consts_set = sem("const_loaded"), sem("consts_set")
        wqk_loaded, wv_loaded, wo_loaded = sem("wqk_loaded"), sem("wv_loaded"), sem("wo_loaded")
        w1_loaded, w2_loaded = sem("w1_loaded"), sem("w2_loaded")
        xs_staged, xf_staged = sem("xs_staged"), sem("xf_staged")
        rope_ready = sem("rope_ready")
        tp_full, tp_taken = sem("tp_full"), [sem("tp_taken0"), sem("tp_taken1")]
        pj_full, pj_taken = sem("pj_full"), [sem("pj_taken0"), sem("pj_taken1")]
        qk_read = sem("qk_read")
        rotated = sem("rotated")
        sc_full, top_ready, exped = sem("sc_full"), sem("top_ready"), sem("exped")
        pT_used = sem("pT_used")
        o_taken = sem("o_taken")
        wo_done, w2_done = sem("wo_done"), sem("w2_done")
        res_a, res_f = sem("res_a"), sem("res_f")
        stats_ready, rstd_ready, xn_ready = sem("stats_ready"), sem("rstd_ready"), sem("xn_ready")
        gated, gelus, h_ready = sem("gated"), sem("gelus"), sem("h_ready")
        dve_attn, dve_ln, pool_front, pool_init = sem("dve_attn"), sem("dve_ln"), sem("pool_front"), sem("pool_init")
        entry_stats, entry_rstd, entry_done, dve_entry = sem("entry_stats"), sem("entry_rstd"), sem("entry_done"), sem("dve_entry")
        summed = sem("summed")
        stored = sem("stored")

        def slot(events, n, what, k):
            c, at = events.index((what, k)), n - AHEAD[PHASE[what]] + 2
            return c % 2, at * (len(events) // 2) + c // 2, at * len(events) + c + 1

        def tp_slot(n, what, k=0):
            return slot(TP_EVENTS, n, what, k)

        def pj_slot(n, what, k):
            return slot(PJ_EVENTS, n, what, k)

        BY_ACT = lambda i: i % 2 == 1
        OUT_BY_ACT = lambda g: g < 2

        block = ctx.enter_context(nc.Block())

        @block.sync
        def _(sp):
            def load_qk(l):
                for k in range(KC):
                    sp.dma_start(w_qkv[:, k, 0:2 * INNER], dram["L1_ffn_Wqkv"][l, k * P:(k + 1) * P, 0:2 * INNER]).then_inc(wqk_loaded, 16)
                sp.dma_start(qk_gain[:, :, :, :].rearrange("p a b d -> p (a b d)"),
                             dram["gains"][l, :].rearrange("(a n) -> a n", a=1).broadcast_to([P, 4 * DH])).then_inc(wqk_loaded, 16)

            def load_v(l):
                for k in range(KC):
                    sp.dma_start(w_qkv[:, k, 2 * INNER:3 * INNER], dram["L1_ffn_Wqkv"][l, k * P:(k + 1) * P, 2 * INNER:3 * INNER]).then_inc(wv_loaded, 16)

            def load_o(l):
                sp.dma_start(w_o[:, :, :], dram["L1_ffn_Wo"][l].rearrange("(c p) n -> p c n", p=P)).then_inc(wo_loaded, 16)

            def load_1(l):
                sp.dma_start(w_1[:, :, :], dram["L1_ffn_W1"][l].rearrange("(c p) n -> p c n", p=P)).then_inc(w1_loaded, 16)
                sp.dma_start(ff_cols[:, :], dram["ff_cols"][l]).then_inc(w1_loaded, 16)

            def load_2(l):
                sp.dma_start(w_2[:, 0:FC - 1, :], dram["L1_ffn_W2"][l, 0:(FC - 1) * P, :].rearrange("(c p) n -> p c n", p=P)).then_inc(w2_loaded, 16)
                sp.dma_start(w_2[0:FR, FC - 1, :], dram["L1_ffn_W2"][l, (FC - 1) * P:FF, :]).then_inc(w2_loaded, 16)
                sp.dma_start(b2[:, :], dram["L1_ffn_b2"][l, :].rearrange("(a n) -> a n", a=1)).then_inc(w2_loaded, 16)

            def stage(dst, row, staged):
                half = D // 2
                sp.dma_start(dst[:, :, 0:half], stream[:, row, :, 0:half]).then_inc(staged, 16)
                sp.dma_start(dst[1:P, :, half:D], stream[0:P - 1, row, :, half:D]).then_inc(staged, 16)
                sp.dma_start(dst[0:1, 1, half:D], stream[P - 1:P, row, 0, half:D]).then_inc(staged, 16)

            def stage_attn(n, row, first):
                if not first:
                    sp.wait_ge(res_f, n - BATCH + 1)
                wait(sp, tp_full, tp_slot(n - 1, "xs")[2])
                stage(xs, row, xs_staged)

            def stage_ffn(n, row):
                sp.wait_ge(res_a, n + 1)
                apart(sp, passed)
                wait(sp, xn_ready, n)
                stage(xf, row, xf_staged)

            def layer(l, first=False, last=False):
                def step(r):
                    stage_attn(l * BATCH + r + 2, r + 2, first)
                    stage_ffn(l * BATCH + r, r)

                n = l * BATCH
                stage_attn(n + 2, 2, first)
                if not first:
                    sp.wait_ge(gelus, n)
                    load_1(l)
                stage_ffn(n, 0)
                stage_attn(n + 3, 3, first)
                if not first:
                    sp.wait_ge(w2_done, n)
                    load_2(l)
                stage_ffn(n + 1, 1)
                with sp.Fori(2, BATCH - 2) as r:
                    step(r)
                n = l * BATCH + BATCH - 2
                if not last:
                    stage_attn(n + 2, 0, False)
                    sp.wait_ge(pj_full, pj_slot(n + 1, "project", PROJ.index(QK[-1]))[2])
                    apart(sp, passed)
                    sp.wait_ge(rope_ready, n + 2)
                    load_qk(l + 1)
                    sp.wait_ge(pj_full, pj_slot(n + 1, "project", len(PROJ) - 1)[2])
                    load_v(l + 1)
                stage_ffn(n, BATCH - 2)
                if not last:
                    stage_attn(n + 3, 1, False)
                stage_ffn(n + 1, BATCH - 1)
                if not last:
                    sp.wait_ge(wo_done, n + 2)
                    load_o(l + 1)

            def store(row):
                sp.dma_start(out_dram[row].rearrange("(t p) d -> p t d", p=P), xall[:, row, :, :]).then_inc(stored, 16)

            sp.dma_start(rope_base[:, :, :, :, :].rearrange("p a b t d -> p (a b t d)"), dram["rope_base"]).then_inc(const_loaded, 16)
            load_qk(0)
            load_v(0)
            sp.wait_ge(consts_set, 2)
            sp.wait_ge(entry_done, 1)
            stage_attn(0, 0, True)
            load_o(0)
            load_1(0)
            load_2(0)
            stage_attn(1, 1, True)
            layer(0, first=True, last=(layers == 1))
            if layers > 2:
                with sp.Fori(1, layers - 1) as l:
                    layer(l)
            if layers > 1:
                layer(layers - 1, last=True)
            for r in range(BATCH):
                sp.wait_ge(summed, r + 1)
                store(r)
            sp.wait_ge(stored, 16 * BATCH)

        def program(eng, do, skip=None):
            def step(n, parity, phases):
                for what, k in STEP:
                    m, par = n + AHEAD[PHASE[what]], (parity + AHEAD[PHASE[what]]) % 2
                    if PHASE[what] in phases:
                        if what in do:
                            do[what](m, par, k)
                    elif skip:
                        skip(m, what, k)

            full = ("x", "attn", "front", "ffn", "out")
            step(-2, 0, ("x",))
            step(-1, 1, ("x", "front"))
            step(0, 0, ("x", "attn", "front"))
            step(1, 1, ("x", "attn", "front", "ffn"))
            with eng.Fori(1, STEPS // 2 - 1) as pair:
                step(2 * pair, 0, full)
                step(2 * pair + 1, 1, full)
            step(STEPS - 2, 0, ("attn", "front", "ffn", "out"))
            step(STEPS - 1, 1, ("attn", "ffn", "out"))
            step(STEPS, 0, ("ffn", "out"))
            step(STEPS + 1, 1, ("out",))

        @block.gpsimd
        def _(pool):
            def start(pool):
                pool.memset(xs[:, :, :], 0.0).then_inc(consts_set, 1)
                pool.memset(xf[:, :, :], 0.0).then_inc(consts_set, 1)
                pool.memset(minus_half[:, :], -0.5).then_inc(consts_set, 1)
                pool.memset(probs[:, :, :], 0.0).then_inc(consts_set, 1)
                pool.memset(ones[:, :], 1.0).then_inc(consts_set, 1)
                pool.memset(all_half[:, :], -0.5).then_inc(pool_init, 1)
                pool.memset(band[:, :], 0.0).then_inc(pool_init, 1)
                pool.wait_ge(pool_init, 1)
                pool.wait_ge(entry_stats, 1)
                pool.tensor_tensor(all_rstd[:, :], all_var[:, :], all_half[:, :], ALU.pow).then_inc(entry_rstd, 1)
                tiles = band[:, :].rearrange("p (t k) -> p t k", t=2)
                for i, (steps, base, per_query) in enumerate((([[0, 2], [-1, KW]], 64, 1), ([[0, 2], [1, KW]], 0, -1),
                                                              ([[1000, 2], [1, KW]], -64, 0))):
                    pool.wait_ge(pool_init, i + 2)
                    pool.affine_select(out=tiles, in_=tiles, pattern=steps, base=base, channel_multiplier=per_query,
                                       compare_op=ALU.is_ge, fill=-BIG).then_inc(pool_init, 1)
                pool.wait_ge(pool_init, 5)
                pool.wait_ge(const_loaded, 16)
                pool.wait_ge(consts_set, 5)

            def ln_rstd(n, par, _):
                pool.wait_ge(stats_ready, n + 1)
                pool.tensor_tensor(rstd[:, :], var_eps[:, :], minus_half[:, 0:TILES], ALU.pow).then_inc(rstd_ready, 1)

            def rope_tables(n, par, _):
                pool.wait_ge(wqk_loaded, 48 * (n // BATCH + 1))
                wait(pool, qk_read, 8 * n)
                for s in range(2):
                    last = pool.tensor_tensor(rope[:, s, :, :, :], rope_base[:, s, :, :, :],
                                              qk_gain[:, s, :, :].rearrange("p b (a d) -> p b a d", a=1).broadcast_to([P, 2, TILES, DH]), ALU.mult)
                last.then_inc(rope_ready, 1)

            def rotate(n, par, i):
                t, s, c = QK[i]
                b = i % 2
                made = n * 20 + sum(2 + QK[x][1] for x in range(i))
                pool.wait_ge(qk_read, 8 * n + i + 1)
                apart(pool, passed)
                wait(pool, tp_full, tp_slot(n, "qk_turn", i - 2)[2] if i >= 2 else tp_slot(n - 1, "qk_turn", i + 6)[2])
                pool.tensor_tensor(qk_rot[:, b, :], qk_cos[:, b, :], qk_sin[:, b, :], ALU.add).then_inc(rotated if s == 0 else pool_front, 1)
                made += s
                pool.tensor_scalar(ssm[:, b, :], ss[:, b, :], 1e-24, None, ALU.max).then_inc(pool_front, 1)
                pool.wait_ge(pool_front, made + 1)
                inv_norm = r_q[:, par, t, 8 * c:8 * c + 8] if s == 0 else r_k[:, b, :]
                pool.tensor_tensor(inv_norm, ssm[:, b, :], minus_half[:, :], ALU.pow).then_inc(pool_front, 1)
                if s == 0:
                    return
                pool.wait_ge(pool_front, made + 2)
                heads = qk_rot[:, b, :].rearrange("p (h d) -> p h d", h=8)
                pool.tensor_tensor(heads, heads, r_k[:, b, :].rearrange("p (h a) -> p h a", a=1).broadcast_to([P, 8, DH]),
                                   ALU.mult).then_inc(rotated, 1)

            start(pool)
            program(pool, {"ln_stats": ln_rstd, "rope": rope_tables, "rotate": rotate})

        @block.tensor
        def _(pe):
            def turn_in(event):
                wait(pe, tp_taken[event[0]], event[1])
                return tp[event[0]]

            def copied(taken, *events):
                last = {b: before for b, before, _ in events}
                for b in last:
                    pe.wait_ge(taken[b], last[b] + 1)

            def blocks(src, event):
                bank = turn_in(event)
                for k in range(KC):
                    for t in range(TILES):
                        last = pe.transpose(bank[:, (k * TILES + t) * P:(k * TILES + t + 1) * P], src[:, t, k * P:(k + 1) * P], ident[:, :])
                last.then_inc(tp_full, 1)

            def x_turn(n, par, _):
                pe.wait_ge(xs_staged, 48 * (n + 1))
                blocks(xs, tp_slot(n, "xs"))

            def project(n, par, j):
                t, s, c = PROJ[j]
                b, before, _ = pj_slot(n, "project", j)
                if j == 0:
                    pe.wait_ge(wqk_loaded, 48 * (n // BATCH + 1))
                    copied(tp_taken, tp_slot(n, "xs"))
                if (t, s, c) == (0, 2, 0):
                    pe.wait_ge(wv_loaded, 32 * (n // BATCH + 1))
                wait(pe, pj_taken[b], before)
                for k in range(KC):
                    last = pe.matmul(pj[b][:, :], xT[:, k, t * P:(t + 1) * P], w_qkv[:, k, s * INNER + c * 512:s * INNER + (c + 1) * 512],
                                     start=(k == 0), stop=(k == KC - 1))
                last.then_inc(pj_full, 1)

            def qk_turn(n, par, i):
                pe.wait_ge(rotated, 8 * n + i + 1)
                bank = turn_in(tp_slot(n, "qk_turn", i))
                for m in range(4):
                    last = pe.transpose(bank[:, m * P:(m + 1) * P], qk_rot[:, i % 2, m * P:(m + 1) * P], ident[:, :])
                last.then_inc(tp_full, 1)

            def scores(n, par, h):
                if h % 2:
                    return
                if h == 0:
                    copied(tp_taken, *(tp_slot(n, "qk_turn", i) for i in range(len(QK))))
                wait(pe, exped, 16 * n + h)
                for bank in sc:
                    pe.matmul(bank[:, 0:2 * KW], ident_bf[:, :], band[:, :], start=True, stop=False)
                pair = [(bank, qT[rows, par, h // 2, :], kT[rows, par, h // 2, :]) for bank, rows in zip(sc, (slice(0, DH), slice(DH, P)))]
                for bank, q, k in pair:
                    pe.matmul(bank[:, 64:KW], q[:, 0:P], k[:, 0:P], start=False, stop=False)
                for bank, q, k in pair:
                    pe.matmul(bank[:, KW:2 * KW], q[:, P:2 * P], k[:, 64:2 * P], start=False, stop=True).then_inc(sc_full, 1)

            def turn(n, par, h):
                pe.wait_ge(exped, 16 * n + h + 1)
                bank = turn_in(tp_slot(n, "turn", h))
                for m in range(3):
                    last = pe.transpose(bank[:, m * P:(m + 1) * P], probs[:, h % 4, m * P:(m + 1) * P], ident[:, :])
                last.then_inc(tp_full, 1)

            def values(n, par, h):
                copied(tp_taken, tp_slot(n, "turn", h))
                if h == 0:
                    copied(pj_taken, *(pj_slot(n, "project", j) for j in range(len(PROJ))))
                if h % 4 == 0:
                    wait(pe, o_taken, 4 * n + h // 4)
                at = (h % 4) * 2 * DH
                hd = slice(h * DH, (h + 1) * DH)
                pe.matmul(o_ps[:, at:at + DH], pT[:, h % 2, 0, :], v[:, par, 0, hd], start=True, stop=True)
                pe.matmul(o_ps[:, at + DH:at + 2 * DH], pT[:, h % 2, 1, :], v[:, par, 0, hd], start=True, stop=False)
                pe.matmul(o_ps[:, at + DH:at + 2 * DH], pT[:, h % 2, 2, :], v[:, par, 1, hd], start=False, stop=True).then_inc(pT_used, 1)

            def o_turn(n, par, g):
                pe.wait_ge(o_taken, 4 * n + g + 1)
                bank = turn_in(tp_slot(n, "o_turn", g))
                for k in range(2):
                    for t in range(TILES):
                        last = pe.transpose(bank[:, (k * TILES + t) * P:(k * TILES + t + 1) * P], o_tok[:, t, (2 * g + k) * P:(2 * g + k + 1) * P], ident[:, :])
                last.then_inc(tp_full, 1)

            def wo(n, par, part):
                if part == 0:
                    copied(tp_taken, *(tp_slot(n, "o_turn", g) for g in range(3)))
                    pe.wait_ge(wo_loaded, 16 * (n // BATCH + 1))
                    wait(pe, res_f, n - 1)
                else:
                    copied(tp_taken, tp_slot(n, "o_turn", 3))
                chunks = range(0, 6) if part == 0 else range(6, INNER // P)
                for t in range(TILES):
                    for k in chunks:
                        last = pe.matmul(y_ps[:, t, :], oT[:, k, t * P:(t + 1) * P], w_o[:, k, :], start=(t == 0 and k == 0),
                                         stop=(t == TILES - 1 and k == INNER // P - 1))
                if part == 1:
                    last.then_inc(wo_done, 1)

            def xn_turn(n, par, _):
                pe.wait_ge(xn_ready, n + 1)
                blocks(xn, tp_slot(n, "xn"))

            def w1(n, par, f):
                if f == 0:
                    pe.wait_ge(w1_loaded, 32 * (n // BATCH + 1))
                    copied(tp_taken, tp_slot(n, "xn"))
                m = P if f < FC - 1 else FR
                b, before, _ = pj_slot(n, "w1", f)
                wait(pe, pj_taken[b], before)
                for s in range(2):
                    for k in range(KC):
                        last = pe.matmul(pj[b][0:m, s * SEQ:(s + 1) * SEQ], w_1[:, k, s * FF + f * P:s * FF + f * P + m], xnT[:, k, :],
                                         start=(k == 0), stop=(k == KC - 1))
                last.then_inc(pj_full, 1)

            def w2(n, par, t):
                if t == 0:
                    pe.wait_ge(w2_loaded, 48 * (n // BATCH + 1))
                    if not isinstance(n, int) or n < STEPS - 1:
                        pe.wait_ge(res_a, n + 2)
                    pe.wait_ge(h_ready, n + 1)
                for f in range(FC):
                    m = P if f < FC - 1 else FR
                    pe.matmul(y_ps[:, t, :], hT[0:m, f, t * P:(t + 1) * P], w_2[0:m, f, :], start=(f == 0), stop=False)
                last = pe.matmul(y_ps[:, t, :], ones[0:1, :], b2[0:1, :], start=False, stop=True)
                if t == TILES - 1:
                    last.then_inc(w2_done, 1)

            def skip(n, what, k):
                for events, full, taken in ((TP_EVENTS, tp_full, tp_taken), (PJ_EVENTS, pj_full, pj_taken)):
                    if (what, k) in events:
                        b, before, count = slot(events, n, what, k)
                        wait(pe, taken[b], before)
                        wait(pe, full, count - 1)
                        pe.sem_inc(taken[b], 1)
                        pe.sem_inc(full, 1)

            pe.wait_ge(consts_set, 5)
            program(pe, {"xs": x_turn, "project": project, "qk_turn": qk_turn, "scores": scores, "turn": turn, "values": values,
                         "o_turn": o_turn, "wo": wo, "xn": xn_turn, "w1": w1, "w2": w2}, skip)

        def copy_turned(eng, copy, n, par, i):
            t, s, c = QK[i]
            b, _, full = tp_slot(n, "qk_turn", i)
            eng.wait_ge(tp_full, full)
            copy((kT if s else qT)[:, par, 4 * c:4 * c + 4, t * P:(t + 1) * P], tp[b][:, :].rearrange("p (m q) -> p m q", m=4)).then_inc(tp_taken[b], 1)

        def copy_probs(eng, copy, n, h):
            b, _, full = tp_slot(n, "turn", h)
            eng.wait_ge(tp_full, full)
            wait(eng, pT_used, 16 * n + h - 1)
            copy(pT[:, h % 2, :, :].rearrange("p m q -> p (m q)"), tp[b][:, 0:3 * P]).then_inc(tp_taken[b], 1)

        def copy_out(eng, copy, n, g):
            b, _, full = tp_slot(n, "o_turn", g)
            eng.wait_ge(tp_full, full)
            copy(oT[:, 2 * g:2 * g + 2, :].rearrange("p k q -> p (k q)"), tp[b][:, :]).then_inc(tp_taken[b], 1)

        @block.scalar
        def _(act):
            def copy(dst, src):
                return nc.scalar.activation(dst, src, ACT.Copy)

            def x_turn(n, par, _):
                b, _, full = tp_slot(n, "xs")
                act.wait_ge(tp_full, full)
                copy(xT[:, :, :].rearrange("p k q -> p (k q)"), tp[b][:, :]).then_inc(tp_taken[b], 1)

            def project(n, par, j):
                t, s, c = PROJ[j]
                b, _, full = pj_slot(n, "project", j)
                act.wait_ge(pj_full, full)
                if s == 2:
                    copy(v[:, par, t, c * 512:(c + 1) * 512], pj[b][:, :]).then_inc(pj_taken[b], 1)
                    return
                i = QK.index(PROJ[j])
                wait(act, qk_read, 8 * n + i - 1)
                copy(qk_raw[:, i % 2, :], pj[b][:, :])
                nc.scalar.activation(qk_sq[:, i % 2, :], pj[b][:, :], ACT.Square).then_inc(pj_taken[b], 1)

            def qk_turn(n, par, i):
                if BY_ACT(i):
                    copy_turned(act, copy, n, par, i)

            def exps(n, par, h):
                act.wait_ge(top_ready, 16 * n + h + 1)
                wait(act, tp_full, tp_slot(n, "turn", h - 4)[2] if h >= 4 else tp_slot(n - 1, "turn", H + h - 4)[2])
                for t in range(TILES):
                    src = sc[h % 2][:, 64:KW] if t == 0 else sc[h % 2][:, KW:2 * KW]
                    dst = probs[:, h % 4, 0:P] if t == 0 else probs[:, h % 4, P + 64:3 * P]
                    last = nc.scalar.activation(dst, src, ACT.Exp, bias=neg_top[:, h % 2, t:t + 1], scale=r_q[:, par, t, h:h + 1],
                                                accum_out=p_sum[:, h, t:t + 1])
                last.then_inc(exped, 1)

            def turn(n, par, h):
                if BY_ACT(h):
                    copy_probs(act, copy, n, h)

            def o_turn(n, par, g):
                if OUT_BY_ACT(g):
                    copy_out(act, copy, n, g)

            def xn_turn(n, par, _):
                b, _, full = tp_slot(n, "xn")
                act.wait_ge(tp_full, full)
                act.wait_ge(w1_loaded, 32 * (n // BATCH + 1))
                for k in range(KC):
                    last = nc.scalar.activation(xnT[:, k, :], tp[b][:, k * SEQ:(k + 1) * SEQ], ACT.Identity, bias=ln_b[:, k:k + 1], scale=ln_g[:, k:k + 1])
                last.then_inc(tp_taken[b], 1)

            def w1(n, par, f):
                m = P if f < FC - 1 else FR
                b, _, full = pj_slot(n, "w1", f)
                act.wait_ge(pj_full, full)
                if f == 0:
                    wait(act, h_ready, n)
                nc.scalar.activation(gate[0:m, f, :], pj[b][0:m, SEQ:2 * SEQ], ACT.Identity, bias=b1[0:m, 1, f:f + 1]).then_inc(gated, 1)

            def gelu(n, par, _):
                act.wait_ge(gated, FC * (n + 1))
                for rows, chunks in ((P, slice(0, FC - 1)), (FR, slice(FC - 1, FC))):
                    last = nc.scalar.activation(gate[0:rows, chunks, :], gate[0:rows, chunks, :], ACT.Gelu)
                last.then_inc(gelus, 1)

            act.wait_ge(consts_set, 5)
            program(act, {"xs": x_turn, "project": project, "qk_turn": qk_turn, "scores": exps, "turn": turn, "o_turn": o_turn,
                          "xn": xn_turn, "w1": w1, "gelu": gelu})

        @block.vector
        def _(dve):
            def copy(dst, src):
                return nc.vector.tensor_copy(dst, src)

            def start(dve):
                tiles_in = xall[:, :, :, :].rearrange("p b t d -> p (b t) d")
                tiles_out = stream[:, :, :, :].rearrange("p b t d -> p (b t) d")
                for i in range(ALLT):
                    last = nc.vector.bn_stats(all_bn[:, i, :], tiles_in[:, i, :])
                last.then_inc(dve_entry, 1)
                dve.wait_ge(dve_entry, 1)
                for i in range(ALLT):
                    last = nc.vector.bn_aggr(all_mv[:, i, :], all_bn[:, i, :])
                last.then_inc(dve_entry, 1)
                dve.wait_ge(dve_entry, 2)
                nc.vector.tensor_scalar(all_var[:, :], all_mv[:, :, 1], 1e-5, None, ALU.add).then_inc(entry_stats, 1)
                dve.wait_ge(entry_rstd, 1)
                for i in range(ALLT):
                    last = nc.vector.tensor_scalar(tiles_out[:, i, :], tiles_in[:, i, :], all_mv[:, i, 0:1], all_rstd[:, i:i + 1],
                                                   ALU.subtract, ALU.mult)
                last.then_inc(entry_done, 1)
                dve.wait_ge(entry_done, 1)
                dve.wait_ge(consts_set, 5)

            def ln_stats(n, par, _):
                dve.wait_ge(xf_staged, 48 * (n + 1))
                apart(dve, passed)
                for t in range(TILES):
                    last = nc.vector.bn_stats(bn[:, t, :], xf[:, t, :])
                last.then_inc(dve_ln, 1)
                dve.wait_ge(dve_ln, 2 * n + 1)
                apart(dve, passed)
                for t in range(TILES):
                    last = nc.vector.bn_aggr(mv[:, t, :], bn[:, t, :])
                last.then_inc(dve_ln, 1)
                dve.wait_ge(dve_ln, 2 * n + 2)
                nc.vector.tensor_scalar(var_eps[:, :], mv[:, :, 1], 1e-5, None, ALU.add).then_inc(stats_ready, 1)

            def ln_apply(n, par, _):
                dve.wait_ge(rstd_ready, n + 1)
                wait(dve, tp_full, tp_slot(n - 1, "xn")[2])
                for t in range(TILES):
                    last = nc.vector.tensor_scalar(xn[:, t, :], xf[:, t, :], mv[:, t, 0:1], rstd[:, t:t + 1], ALU.subtract, ALU.mult)
                last.then_inc(xn_ready, 1)

            def rotate(n, par, i):
                t, s, c = QK[i]
                if i == 0:
                    dve.wait_ge(rope_ready, n + 1)
                b, before, _ = pj_slot(n, "project", PROJ.index(QK[i]))
                dve.wait_ge(pj_taken[b], before + 1)
                wait(dve, rotated, 8 * n + i - 1)
                wait(dve, pool_front, n * 20 + sum(2 + QK[x][1] for x in range(i - 1)))
                raw, cos, sin = (x[:, i % 2, :].rearrange("p (h d) -> p h d", h=8) for x in (qk_raw, qk_cos, qk_sin))
                nc.vector.tensor_reduce(ss[:, i % 2, :], qk_sq[:, i % 2, :].rearrange("p (h d) -> p h d", h=8), AX, ALU.add)

                def table(r, lo, hi):
                    return rope[:, s, r, t, lo:hi].rearrange("p (a d) -> p a d", a=1).broadcast_to([P, 8, hi - lo])

                nc.vector.tensor_tensor(cos, raw, table(0, 0, DH), ALU.mult)
                hd = DH // 2
                nc.vector.tensor_tensor(sin[:, :, 0:hd], raw[:, :, hd:DH], table(1, 0, hd), ALU.mult)
                nc.vector.tensor_tensor(sin[:, :, hd:DH], raw[:, :, 0:hd], table(1, hd, DH), ALU.mult).then_inc(qk_read, 1)

            def qk_turn(n, par, i):
                if not BY_ACT(i):
                    copy_turned(dve, copy, n, par, i)

            counted = [x for x in STEP if x[0] in ("scores", "group")]
            DEPENDENT = len(counted)

            def tops(n, par, h):
                dve.wait_ge(sc_full, 16 * n + h + 1)
                if h == 0:
                    dve.wait_ge(rotated, 8 * n + 8)
                nc.vector.tensor_reduce(top[:, h % 2, :], sc[h % 2][:, 0:2 * KW].rearrange("p (t k) -> p t k", t=2), AX, ALU.max).then_inc(dve_attn, 1)
                dve.wait_ge(dve_attn, DEPENDENT * n + counted.index(("scores", h)) + 1)
                nc.vector.scalar_tensor_tensor(neg_top[:, h % 2, :], top[:, h % 2, :], -1.0, r_q[:, par, :, h], ALU.mult, ALU.mult).then_inc(top_ready, 1)

            def group(n, par, g):
                dve.wait_ge(pT_used, 16 * n + 4 * g + 4)
                nc.vector.reciprocal(p_inv[:, :, :], p_sum[:, 4 * g:4 * g + 4, :]).then_inc(dve_attn, 1)
                dve.wait_ge(dve_attn, DEPENDENT * n + counted.index(("group", g)) + 1)
                for t in range(TILES):
                    last = nc.vector.tensor_tensor(
                        o_tok[:, t, g * 4 * DH:(g + 1) * 4 * DH].rearrange("p (h d) -> p h d", h=4),
                        o_ps[:, :].rearrange("p (h t d) -> p h t d", h=4, t=TILES)[:, :, t, :],
                        p_inv[:, :, t:t + 1].broadcast_to([P, 4, DH]), ALU.mult)
                last.then_inc(o_taken, 1)

            def turn(n, par, h):
                if not BY_ACT(h):
                    copy_probs(dve, copy, n, h)

            def o_turn(n, par, g):
                if not OUT_BY_ACT(g):
                    copy_out(dve, copy, n, g)

            def add_attn(n, par, _):
                dve.wait_ge(wo_done, n + 1)
                row = n % BATCH
                nc.vector.tensor_tensor(stream[:, row, :, :], y_ps[:, :, :], stream[:, row, :, :], ALU.add).then_inc(res_a, 1)

            def halves(n, par, f):
                m = P if f < FC - 1 else FR
                b, _, _ = pj_slot(n, "w1", f)
                dve.wait_ge(gated, FC * n + f + 1)
                nc.vector.tensor_scalar(hT[0:m, f, :], pj[b][0:m, 0:SEQ], b1[0:m, 0, f:f + 1], None, ALU.add).then_inc(pj_taken[b], 1)

            def gates(n, par, _):
                b, before, _ = pj_slot(n, "w1", FC - 1)
                dve.wait_ge(pj_taken[b], before + 1)
                dve.wait_ge(gelus, n + 1)
                for rows, chunks in ((P, slice(0, FC - 1)), (FR, slice(FC - 1, FC))):
                    last = nc.vector.tensor_tensor(hT[0:rows, chunks, :], hT[0:rows, chunks, :], gate[0:rows, chunks, :], ALU.mult)
                last.then_inc(h_ready, 1)

            def add_ffn(n, par, _):
                dve.wait_ge(w2_done, n + 1)
                row = n % BATCH
                nc.vector.tensor_tensor(stream[:, row, :, :], y_ps[:, :, :], stream[:, row, :, :], ALU.add).then_inc(res_f, 1)

            start(dve)
            program(dve, {"ln_stats": ln_stats, "ln_apply": ln_apply, "rotate": rotate, "qk_turn": qk_turn, "scores": tops, "group": group,
                          "turn": turn, "o_turn": o_turn, "res_a": add_attn, "halves": halves, "gates": gates, "res_f": add_ffn})
            for row in range(BATCH):
                dve.wait_ge(res_f, (layers - 1) * BATCH + row + 1)
                nc.vector.tensor_tensor(xall[:, row, :, :], xall[:, row, :, :], stream[:, row, :, :], ALU.add).then_inc(summed, 1)


def build(nc, dram, out_dram):
    with ExitStack() as ctx:
        xall = ctx.enter_context(nc.sbuf_tensor("x_all", [P, BATCH, TILES, D], F32))
        ident = ctx.enter_context(nc.sbuf_tensor("identity", [P, P], F32))
        ident_bf = ctx.enter_context(nc.sbuf_tensor("identity_bf", [P, P], BF16))
        x_loaded = ctx.enter_context(nc.semaphore("x_loaded"))
        passed = ctx.enter_context(nc.semaphore("passed"))
        identity_step = ctx.enter_context(nc.semaphore("identity_step"))
        with nc.Block() as block:
            @block.sync
            def _(sp):
                sp.dma_start(xall[:, :, :, :].rearrange("p b t d -> p (b t) d"), dram["x"].rearrange("b (t p) d -> p (b t) d", p=P)).then_inc(x_loaded, 16)
                sp.wait_ge(x_loaded, 16)

            @block.gpsimd
            def _(pool):
                pool.memset(ident[:, :], 0.0).then_inc(identity_step, 1)
                pool.wait_ge(identity_step, 1)
                pool.affine_select(out=ident[:, :], in_=ident[:, :], compare_op=ALU.not_equal, fill=1.0, base=0,
                                   pattern=[[-1, P]], channel_multiplier=1).then_inc(identity_step, 1)
                pool.wait_ge(identity_step, 2)
                pool.tensor_copy(ident_bf[:, :], ident[:, :]).then_inc(identity_step, 1)
                pool.wait_ge(identity_step, 3)
        first_layers(nc, xall, ident, ident_bf, passed, dram)
        local_layers(nc, xall, ident, ident_bf, passed, dram, DEPTH, out_dram)


def rotary_base():
    dim, window, qk_scale = 64, 64, 8.0
    half = np.arange(0, dim, 2, dtype=np.float32)
    inv_freq = (1.0 / 10000.0 ** (half / dim)).astype(np.float32)
    t = np.arange(SEQ, dtype=np.float32)
    freqs = np.concatenate([t[:, None] * inv_freq[None, :]] * 2, -1)
    base = (half + 0.4 * dim) / (1.4 * dim)
    power = (t - SEQ // 2) / (window // 2)
    scale = np.concatenate([(base[None, :] ** power[:, None]).astype(np.float32)] * 2, -1)
    sign = np.where(np.arange(dim) < dim // 2, -1.0, 1.0)
    q = np.stack([np.cos(freqs) * scale, np.sin(freqs) * scale * sign])
    k = np.stack([np.cos(freqs) / scale * qk_scale, np.sin(freqs) / scale * qk_scale * sign])
    both = np.stack([q, k]).reshape(2, 2, TILES, P, dim)
    return np.ascontiguousarray(both.transpose(3, 0, 1, 2, 4).reshape(P, -1), dtype=np.float32)


def lay_out(inp):
    a = {k: np.asarray(v) for k, v in inp.items()}
    c = lambda x: np.ascontiguousarray(x)
    o = {"x": c(a["x"]), "ctx": c(a["ctx_1024"]), "mask": c(a["mask_BxS2_ik0"])}
    o["a_w"] = c(np.stack([a[f"L0_attn_W{w}"].T for w in "qkvo"]))
    o["gate_w"] = c(np.concatenate([a["L0_xattn_igate_w"], a["L0_xattn_fgate_w"]]).T)
    o["gate_b"] = c(np.stack([a["L0_xattn_igate_b"], a["L0_xattn_fgate_b"]], 1))
    o["out_w"] = c(a["L0_xattn_out_w"])
    o["c_wq"] = c(a["L0_ffn_Wq"].T)
    keys = a["L0_ffn_keys"]
    nk, dh = keys.shape[1], keys.shape[3]
    o["c_keys"] = c(keys.reshape(2, 2, nk, 2, dh).transpose(1, 4, 3, 0, 2).reshape(2 * dh, 4 * nk))
    o["c_wg"], o["c_wu"], o["c_wd"] = c(a["L0_ffn_Wg"].T), c(a["L0_ffn_Wu"].T), c(a["L0_ffn_Wd"].T)
    o["emb"] = c(np.concatenate([a["L0_ffn_down_embed"], a["L0_ffn_up_embed"]], 1))
    o["d_w"] = c(np.stack([a[f"L1_attn_W{w}"] for w in "qkv"]))
    o["e_wq"] = c(a["L1_xattn_Wq"].reshape(D, 2, 2, 4, 64).transpose(0, 1, 3, 2, 4).reshape(D, -1))
    o["e_wk"], o["e_wv"] = c(a["L1_xattn_Wk"]), c(a["L1_xattn_Wv"])
    o["e_wo"] = c(a["L1_xattn_Wo"].reshape(2, 2, 4, 64, D).transpose(0, 2, 1, 3, 4).reshape(-1, D))
    f = "L1_ffn_"
    for w in ("Wqkv", "Wo", "W1", "W2", "b2"):
        o[f + w] = c(a[f + w])
    rolled = lambda g: np.concatenate([g, g[:, 32:], g[:, :32]], 1)
    o["gains"] = c(np.concatenate([rolled(a[f + "q_scale"]), rolled(a[f + "k_scale"])], 1))
    depth, two_ff = a[f + "b1"].shape
    ff = two_ff // 2
    chunks = (ff + P - 1) // P
    b1 = np.pad(a[f + "b1"].reshape(depth, 2, ff), ((0, 0), (0, 0), (0, chunks * P - ff)))
    cols = [b1.reshape(depth, 2, chunks, P).transpose(0, 3, 1, 2).reshape(depth, P, -1)]
    cols += [a[f + g].reshape(depth, KC, P).transpose(0, 2, 1) for g in ("ln_g", "ln_b")]
    o["ff_cols"] = c(np.concatenate(cols, 2))
    o["rope_base"] = rotary_base()
    return o


def kernel(**inputs):
    import concourse.bacc as bacc
    from concourse.bass_utils import run_bass_kernel_spmd

    nc = bacc.Bacc("TRN2", target_bir_lowering=False, num_devices=1)
    arrays = lay_out(inputs)
    dram = {k: nc.dram_tensor(f"in_{k}", v.shape, mybir.dt.from_np(v.dtype), kind="ExternalInput").ap() for k, v in arrays.items()}
    out = nc.dram_tensor("out", (BATCH, SEQ, D), F32, kind="ExternalOutput").ap()
    build(nc, dram, out)
    r = run_bass_kernel_spmd(nc, [{f"in_{k}": v for k, v in arrays.items()}], core_ids=[0])
    return r.results[0]["out"]
```
